# Optimizing a Trainium2 kernel written in Bass

```python
import numpy as np
import jax
import jax.numpy as jnp

def _softmax(x, axis=-1):
    return jax.nn.softmax(x, axis=axis)

def _gelu(x):
    return jax.nn.gelu(x, approximate=True)

def _silu(x):
    return jax.nn.silu(x)

def _sigmoid(x):
    return jax.nn.sigmoid(x)

def _layernorm(x, axis=-1, eps=1e-05):
    m = jnp.mean(x, axis=axis, keepdims=True)
    v = jnp.var(x, axis=axis, keepdims=True)
    return (x - m) / jnp.sqrt(v + eps)

def _scatter_add(tgt, idx, src, axis=0):
    return tgt.at[idx].add(src)

def _segment_sum(src, seg, n):
    return jax.ops.segment_sum(src, seg, n)
kernel_name = 'mk_adj_ffn_d2_adj_r2_fcef49'

def setup_inputs(seed: int=0):
    np.random.seed(seed)
    _w = jnp.asarray

    def _rec_inputs():
        import jax
        import jax.numpy as jnp
        _gk = jax.random.key(seed)
        x = -8.776e-05 + 1 * jax.random.normal(jax.random.fold_in(_gk, 1), (10000, 128), jnp.float32)
        _w = (1.0 + jnp.arange(10000, dtype=jnp.float32)) ** (-0.5)
        _w = _w / _w.mean()
        _pij = jnp.clip(0.0002 * _w[:, None] * _w[None, :], 0.0, 1.0)
        _a = jax.random.uniform(jax.random.fold_in(_gk, 2), (10000, 10000)) < _pij
        _a = jnp.logical_or(_a, jnp.eye(10000, dtype=bool))
        _af = _a.astype(jnp.float32)
        _af = _af * jax.random.uniform(jax.random.fold_in(_gk, 3), (10000, 10000), jnp.float32, 0.05, 1)
        adj = _af
        return (x, adj)
    x, adj = _rec_inputs()

    def _L0_gnn_setup():
        import jax, jax.numpy as jnp
        import numpy as np
        N_USER = 10000
        N_ITEM = 10000
        HID = 128
        key = jax.random.key(seed)
        k1, k2, k3, k4, k5, k6, k7 = jax.random.split(key, 7)
        scale = 1.0 / np.sqrt(HID)
        return {'user_feat': jax.random.normal(k1, (N_USER, HID), dtype=jnp.float32), 'item_feat': jax.random.normal(k2, (N_ITEM, HID), dtype=jnp.float32), 'adj': jax.random.uniform(k3, (N_USER, N_ITEM), dtype=jnp.float32), 'W_item': jax.random.uniform(k4, (HID, HID), dtype=jnp.float32, minval=-scale, maxval=scale), 'b_item': jax.random.uniform(k5, (HID,), dtype=jnp.float32, minval=-scale, maxval=scale), 'W_user': jax.random.uniform(k6, (HID, HID), dtype=jnp.float32, minval=-scale, maxval=scale), 'b_user': jax.random.uniform(k7, (HID,), dtype=jnp.float32, minval=-scale, maxval=scale)}
    _L0_gnn_all = _L0_gnn_setup()
    _L0_gnn_in = {k: v for k, v in _L0_gnn_all.items() if k in ('item_feat', 'W_item', 'b_item', 'W_user', 'b_user')}
    del _L0_gnn_all

    def _L0_ffn_setup():
        import jax, jax.numpy as jnp
        import numpy as np
        B, N, D = (16, 2048, 128)
        NUM_EXPERTS, TOP_K, HEADS = (4, 2, 4)
        N_EDGES = 524288
        LN_EPS = 1e-05

        def _layernorm(x, g, b):
            mu = x.mean(-1, keepdims=True)
            var = ((x - mu) ** 2).mean(-1, keepdims=True)
            return (x - mu) * jax.lax.rsqrt(var + LN_EPS) * g + b

        def _forward(x, edge_index, W_gat, att_src, att_dst, b_gat, ln_gamma, ln_beta, W1, b1, W2, b2):
            Bc, Nc, Dc = x.shape
            M = Bc * Nc
            x_flat = x.reshape(M, Dc)
            h = (x_flat @ W_gat).reshape(M, HEADS, NUM_EXPERTS)
            loops = jnp.arange(M, dtype=edge_index.dtype)
            src = jnp.concatenate([edge_index[0], loops])
            dst = jnp.concatenate([edge_index[1], loops])
            a_src = (h * att_src).sum(-1)
            a_dst = (h * att_dst).sum(-1)
            e = jax.nn.leaky_relu(a_src[src] + a_dst[dst], negative_slope=0.2)
            e_max = jax.ops.segment_max(e, dst, num_segments=M)
            ee = jnp.exp(e - e_max[dst])
            denom = jax.ops.segment_sum(ee, dst, num_segments=M)
            alpha = ee / (denom[dst] + 1e-16)
            msg = h[src] * alpha[:, :, None]
            agg = jax.ops.segment_sum(msg, dst, num_segments=M).reshape(M, HEADS * NUM_EXPERTS) + b_gat
            scores = _layernorm(agg, ln_gamma, ln_beta).reshape(M, HEADS, NUM_EXPERTS).mean(1)
            scores = scores.reshape(Bc, Nc, NUM_EXPERTS)
            topk_s, topk_i = jax.lax.top_k(scores, TOP_K)
            w = jax.nn.softmax(topk_s, axis=-1)
            out = jnp.zeros_like(x)
            for ei in range(NUM_EXPERTS):
                g = jnp.where(topk_i == ei, w, 0.0).sum(-1)
                hh = jax.nn.gelu(x @ W1[ei] + b1[ei], approximate=False)
                out = out + g[..., None] * (hh @ W2[ei] + b2[ei])
            return out
        key = jax.random.key(seed)
        ks = jax.random.split(key, 8)
        s = 0.05
        return {'x': jax.random.normal(ks[0], (B, N, D), jnp.float32), 'W_gat': jax.random.normal(ks[1], (D, HEADS * NUM_EXPERTS), jnp.float32) * s, 'att_src': jax.random.normal(ks[2], (HEADS, NUM_EXPERTS), jnp.float32) * s, 'att_dst': jax.random.normal(ks[3], (HEADS, NUM_EXPERTS), jnp.float32) * s, 'b_gat': jnp.zeros((HEADS * NUM_EXPERTS,), jnp.float32), 'ln_gamma': jnp.ones((HEADS * NUM_EXPERTS,), jnp.float32), 'ln_beta': jnp.zeros((HEADS * NUM_EXPERTS,), jnp.float32), 'W1': jax.random.normal(ks[4], (NUM_EXPERTS, D, 2 * D), jnp.float32) * s, 'b1': jnp.zeros((NUM_EXPERTS, 2 * D), jnp.float32), 'W2': jax.random.normal(ks[5], (NUM_EXPERTS, 2 * D, D), jnp.float32) * s, 'b2': jnp.zeros((NUM_EXPERTS, D), jnp.float32), 'edge_index': jax.random.randint(ks[6], (2, N_EDGES), 0, B * N, jnp.int32)}
    _L0_ffn_all = _L0_ffn_setup()
    _L0_ffn_in = {k: v for k, v in _L0_ffn_all.items() if k in ('W_gat', 'att_src', 'att_dst', 'b_gat', 'ln_gamma', 'ln_beta', 'W1', 'b1', 'W2', 'b2', 'edge_index')}
    del _L0_ffn_all

    def _L1_gnn_setup():
        import jax, jax.numpy as jnp
        import numpy as np
        N = 4096
        D = 128
        CUTOFF = 1.0
        MU = 1.0
        SIGMA = 0.5

        def sensitivity(r, mu, sigma):
            return jnp.exp(-(1.0 / r - 1.0 / mu) ** 2 / (2.0 * sigma * sigma))
        key = jax.random.key(seed)
        k_z, k_d, k_w = jax.random.split(key, 3)
        z = jax.random.normal(k_z, (N, D), dtype=jnp.float32)
        dist_matrix = jax.random.uniform(k_d, (N, N), dtype=jnp.float32) * 2.0 + 0.05
        W = jax.random.normal(k_w, (D, D), dtype=jnp.float32)
        B = jnp.zeros((D,), dtype=jnp.float32)
        return {'z': z, 'dist_matrix': dist_matrix, 'W': W, 'B': B}
    _L1_gnn_all = _L1_gnn_setup()
    _L1_gnn_in = {k: v for k, v in _L1_gnn_all.items() if k in ('W', 'B')}
    del _L1_gnn_all

    def _L1_ffn_setup():
        import jax, jax.numpy as jnp
        import numpy as np
        E = 8
        K = 2
        D = 128
        H = 256
        DOUT = 128
        EPS = 1e-05
        key = jax.random.key(seed)
        ks = jax.random.split(key, 9)
        s = 0.02
        return {'x': jax.random.normal(ks[0], (4, 4096, D), jnp.float32), 'gamma': 1.0 + 0.05 * jax.random.normal(ks[1], (D,), jnp.float32), 'beta': 0.05 * jax.random.normal(ks[2], (D,), jnp.float32), 'Wr': 0.01 * jax.random.normal(ks[3], (D, E), jnp.float32), 'br': jnp.zeros((E,), jnp.float32), 'W1': s * jax.random.normal(ks[4], (E, D, H), jnp.float32), 'b1': s * jax.random.normal(ks[5], (E, H), jnp.float32), 'W2': s * jax.random.normal(ks[6], (E, H, DOUT), jnp.float32), 'b2': s * jax.random.normal(ks[7], (E, DOUT), jnp.float32)}
    _L1_ffn_all = _L1_ffn_setup()
    _L1_ffn_in = {k: v for k, v in _L1_ffn_all.items() if k in ('gamma', 'beta', 'Wr', 'br', 'W1', 'b1', 'W2', 'b2')}
    del _L1_ffn_all
    return {'x': x, 'adj': adj, 'L0_gnn_item_feat': _L0_gnn_in['item_feat'], 'L0_gnn_W_item': _L0_gnn_in['W_item'], 'L0_gnn_b_item': _L0_gnn_in['b_item'], 'L0_gnn_W_user': _L0_gnn_in['W_user'], 'L0_gnn_b_user': _L0_gnn_in['b_user'], 'L0_ffn_W_gat': _L0_ffn_in['W_gat'], 'L0_ffn_att_src': _L0_ffn_in['att_src'], 'L0_ffn_att_dst': _L0_ffn_in['att_dst'], 'L0_ffn_b_gat': _L0_ffn_in['b_gat'], 'L0_ffn_ln_gamma': _L0_ffn_in['ln_gamma'], 'L0_ffn_ln_beta': _L0_ffn_in['ln_beta'], 'L0_ffn_W1': _L0_ffn_in['W1'], 'L0_ffn_b1': _L0_ffn_in['b1'], 'L0_ffn_W2': _L0_ffn_in['W2'], 'L0_ffn_b2': _L0_ffn_in['b2'], 'L0_ffn_edge_index': _L0_ffn_in['edge_index'], 'L1_gnn_W': _L1_gnn_in['W'], 'L1_gnn_B': _L1_gnn_in['B'], 'L1_ffn_gamma': _L1_ffn_in['gamma'], 'L1_ffn_beta': _L1_ffn_in['beta'], 'L1_ffn_Wr': _L1_ffn_in['Wr'], 'L1_ffn_br': _L1_ffn_in['br'], 'L1_ffn_W1': _L1_ffn_in['W1'], 'L1_ffn_b1': _L1_ffn_in['b1'], 'L1_ffn_W2': _L1_ffn_in['W2'], 'L1_ffn_b2': _L1_ffn_in['b2']}

def reference(x, adj, L0_gnn_item_feat, L0_gnn_W_item, L0_gnn_b_item, L0_gnn_W_user, L0_gnn_b_user, L0_ffn_W_gat, L0_ffn_att_src, L0_ffn_att_dst, L0_ffn_b_gat, L0_ffn_ln_gamma, L0_ffn_ln_beta, L0_ffn_W1, L0_ffn_b1, L0_ffn_W2, L0_ffn_b2, L0_ffn_edge_index, L1_gnn_W, L1_gnn_B, L1_ffn_gamma, L1_ffn_beta, L1_ffn_Wr, L1_ffn_br, L1_ffn_W1, L1_ffn_b1, L1_ffn_W2, L1_ffn_b2):
    import jax
    import jax.numpy as jnp

    def _L0_gnn_ref(user_feat, item_feat, adj, W_item, b_item, W_user, b_user):
        import jax, jax.numpy as jnp
        import numpy as np
        N_USER = 10000
        N_ITEM = 10000
        HID = 128
        h = item_feat @ W_item.T + b_item
        b = user_feat @ W_user.T + b_user
        return jax.nn.relu(adj @ h + b)

    def _L0_ffn_ref(x, W_gat, att_src, att_dst, b_gat, ln_gamma, ln_beta, W1, b1, W2, b2, edge_index):
        import jax, jax.numpy as jnp
        import numpy as np
        B, N, D = (16, 2048, 128)
        NUM_EXPERTS, TOP_K, HEADS = (4, 2, 4)
        N_EDGES = 524288
        LN_EPS = 1e-05

        def _layernorm(x, g, b):
            mu = x.mean(-1, keepdims=True)
            var = ((x - mu) ** 2).mean(-1, keepdims=True)
            return (x - mu) * jax.lax.rsqrt(var + LN_EPS) * g + b

        def _forward(x, edge_index, W_gat, att_src, att_dst, b_gat, ln_gamma, ln_beta, W1, b1, W2, b2):
            Bc, Nc, Dc = x.shape
            M = Bc * Nc
            x_flat = x.reshape(M, Dc)
            h = (x_flat @ W_gat).reshape(M, HEADS, NUM_EXPERTS)
            loops = jnp.arange(M, dtype=edge_index.dtype)
            src = jnp.concatenate([edge_index[0], loops])
            dst = jnp.concatenate([edge_index[1], loops])
            a_src = (h * att_src).sum(-1)
            a_dst = (h * att_dst).sum(-1)
            e = jax.nn.leaky_relu(a_src[src] + a_dst[dst], negative_slope=0.2)
            e_max = jax.ops.segment_max(e, dst, num_segments=M)
            ee = jnp.exp(e - e_max[dst])
            denom = jax.ops.segment_sum(ee, dst, num_segments=M)
            alpha = ee / (denom[dst] + 1e-16)
            msg = h[src] * alpha[:, :, None]
            agg = jax.ops.segment_sum(msg, dst, num_segments=M).reshape(M, HEADS * NUM_EXPERTS) + b_gat
            scores = _layernorm(agg, ln_gamma, ln_beta).reshape(M, HEADS, NUM_EXPERTS).mean(1)
            scores = scores.reshape(Bc, Nc, NUM_EXPERTS)
            topk_s, topk_i = jax.lax.top_k(scores, TOP_K)
            w = jax.nn.softmax(topk_s, axis=-1)
            out = jnp.zeros_like(x)
            for ei in range(NUM_EXPERTS):
                g = jnp.where(topk_i == ei, w, 0.0).sum(-1)
                hh = jax.nn.gelu(x @ W1[ei] + b1[ei], approximate=False)
                out = out + g[..., None] * (hh @ W2[ei] + b2[ei])
            return out
        return _forward(x, edge_index, W_gat, att_src, att_dst, b_gat, ln_gamma, ln_beta, W1, b1, W2, b2)

    def _L1_gnn_ref(z, dist_matrix, W, B):
        import jax, jax.numpy as jnp
        import numpy as np
        N = 4096
        D = 128
        CUTOFF = 1.0
        MU = 1.0
        SIGMA = 0.5

        def sensitivity(r, mu, sigma):
            return jnp.exp(-(1.0 / r - 1.0 / mu) ** 2 / (2.0 * sigma * sigma))
        msg = z @ W + B
        sens = sensitivity(dist_matrix, MU, SIGMA)
        weights = jnp.where(dist_matrix < CUTOFF, sens, 0.0)
        return weights @ msg

    def _L1_ffn_ref(x, gamma, beta, Wr, br, W1, b1, W2, b2):
        import jax, jax.numpy as jnp
        import numpy as np
        E = 8
        K = 2
        D = 128
        H = 256
        DOUT = 128
        EPS = 1e-05
        mu = jnp.mean(x, axis=-1, keepdims=True)
        var = jnp.mean(jnp.square(x - mu), axis=-1, keepdims=True)
        xn = (x - mu) * jax.lax.rsqrt(var + EPS) * gamma + beta
        logits = jnp.einsum('bsd,de->bse', xn, Wr) + br
        top_vals, top_idx = jax.lax.top_k(logits, K)
        w = jax.nn.softmax(top_vals, axis=-1)
        w_full = jnp.einsum('bsk,bske->bse', w, jax.nn.one_hot(top_idx, E, dtype=w.dtype))
        y = jnp.zeros(x.shape[:-1] + (DOUT,), x.dtype)
        for e in range(E):
            h = jax.nn.gelu(jnp.einsum('bsd,dh->bsh', xn, W1[e]) + b1[e], approximate=False)
            y_e = jnp.einsum('bsh,hd->bsd', h, W2[e]) + b2[e]
            y = y + y_e * w_full[..., e, None]
        return y
    x = x + _L0_gnn_ref(_layernorm(x, axis=-1), L0_gnn_item_feat, adj, L0_gnn_W_item, L0_gnn_b_item, L0_gnn_W_user, L0_gnn_b_user)
    x = x + _L0_ffn_ref(_layernorm(x, axis=-1)[None], L0_ffn_W_gat, L0_ffn_att_src, L0_ffn_att_dst, L0_ffn_b_gat, L0_ffn_ln_gamma, L0_ffn_ln_beta, L0_ffn_W1, L0_ffn_b1, L0_ffn_W2, L0_ffn_b2, L0_ffn_edge_index)[0]
    x = x + _L1_gnn_ref(_layernorm(x, axis=-1), adj, L1_gnn_W, L1_gnn_B)
    x = x + _L1_ffn_ref(_layernorm(x, axis=-1)[None], L1_ffn_gamma, L1_ffn_beta, L1_ffn_Wr, L1_ffn_br, L1_ffn_W1, L1_ffn_b1, L1_ffn_W2, L1_ffn_b2)[0]
    return x

_drawn_inputs = setup_inputs


def setup_inputs(seed=0):
    import zlib

    import numpy as np

    out = dict(_drawn_inputs(seed))
    spreads = {'L0_ffn_b_gat': (0.0, 0.1),
     'L0_ffn_ln_gamma': (1.0, 0.2),
     'L0_ffn_ln_beta': (0.0, 0.1),
     'L0_ffn_b1': (0.0, 0.1),
     'L0_ffn_b2': (0.0, 0.1),
     'L1_gnn_B': (0.0, 0.509),
     'L1_ffn_br': (0.0, 0.8)}
    factors = {'L0_ffn_att_dst': 4.041,
     'L1_ffn_gamma': 8.0,
     'L1_ffn_beta': 8.0,
     'L1_ffn_Wr': 8.0,
     'L1_ffn_W1': 8.0,
     'L1_ffn_b1': 42.905,
     'L1_ffn_W2': 8.0,
     'L1_ffn_b2': 64.0}
    for name, (base, spread) in spreads.items():
        noise = np.random.default_rng([zlib.crc32(name.encode()), seed]).standard_normal(out[name].shape)
        drawn = base * np.exp(spread * noise) if base else spread * noise
        out[name] = jnp.asarray(drawn.astype(out[name].dtype))
    for name, factor in factors.items():
        out[name] = (out[name] * factor).astype(out[name].dtype)
    return out
```

```python
import concourse.bass as bass
from concourse import mybir
from contextlib import ExitStack

F32 = mybir.dt.float32
I32 = mybir.dt.int32
ALU = mybir.AluOpType
ACT = mybir.ActivationFunctionType
AX = mybir.AxisListType

P = 128
N = 10000
D = 128
EPS = 1e-5

UB = 500
NUB = N // UB
NT = -(-N // P)
NPAD = NT * P
CT = 8
NCH = -(-NT // CT)
NBUF = 5

E = 524288
ROW = E // P
LOGP, LOGR = 7, 12
DST_SHIFT = 14
FIELD = (1 << DST_SHIFT) - 1
KEY_BASE = 0x30000000
CH = 128
HF = CH // 2
CHMAX = (E + N) // (P * CH) + 1
RMAX = CHMAX * CH
BIG = 1 << 20
NEG = -1e30

H0, C0 = 4, 4
HC = C0 + 1
NF = H0 * HC
TABW = NF + 2 * H0
STW = NF + H0
HID = 256
BLANK = RMAX * STW // 48


def keep(shared, sem):
    shared["used_sems"].append(sem)
    return sem


def pool_sem(nc, shared, name):
    return shared["stack"].enter_context(nc.semaphore(name))


def clear_semaphores(nc, shared):
    with nc.Block() as block:
        @block.gpsimd
        def _(pool):
            for sem in shared["used_sems"]:
                pool.sem_clear(sem)
    shared["used_sems"] = []


def hold(eng, sem, value, passed):
    eng.wait_ge(sem, value)
    eng.sem_inc(passed, 1)


def stage_views(buf, b, k, width):
    if k is None:
        v = buf.rearrange("p (a two d) -> p a two d", two=2, d=1 << b)
        yield v[:, :, 0, :], v[:, :, 1, :], True
    elif k > b:
        v = buf.rearrange("p (a dir c two d) -> p a dir c two d", dir=2, c=1 << (k - 1 - b), two=2, d=1 << b)
        for way in range(2):
            yield v[:, :, way, :, 0, :], v[:, :, way, :, 1, :], way == 0
    else:
        v = buf.rearrange("p (a two c dir d) -> p a two c dir d", two=2, c=1 << (b - 1 - k), dir=2, d=1 << k)
        for way in range(2):
            yield v[:, :, 0, :, way, :], v[:, :, 1, :, way, :], way == 0


def prepare(nc, shared, x_t, item_t, edges, w_item_t, b_item, y0_dram):
    with ExitStack() as ctx:
        sb = lambda name, shape, dt=F32: ctx.enter_context(nc.sbuf_tensor(name, shape, dt))
        pb = lambda name, shape: ctx.enter_context(nc.psum_tensor(name, shape, F32))
        sem = lambda name: keep(shared, ctx.enter_context(nc.semaphore(name)))
        s = shared
        xc = sb("p_xc", [P, N])
        sq = sb("p_sq", [P, N])
        item = sb("p_item", [P, 2, CT * P])
        w_item = sb("p_w_item", [P, D])
        b_row = sb("p_b_item", [1, D])
        flag = sb("p_flag", [P, 512])
        count = sb("p_count", [P, 16])
        total_i = sb("p_total_i", [P, 1], I32)
        part_i = sb("p_part_i", [P, 1], I32)
        bits = sb("p_bits", [P, LOGP], I32)
        zero_ids = sb("p_zero_ids", [1, NPAD - N], I32)
        mean_ps = [pb(f"p_mean{u}", [P, 512]) for u in range(2)]
        var_ps = [pb(f"p_var{u}", [P, 512]) for u in range(2)]
        h_ps = [pb(f"p_h{u}", [P, 512]) for u in range(2)]
        tot_ps = pb("p_tot", [P, 512])

        weights_in = sem("p_weights_in")
        x_in = sem("p_x_in")
        item_in = [sem(f"p_item_in{u}") for u in range(2)]
        item_used = sem("p_item_used")
        src_in = sem("p_src_in")
        dst_in = sem("p_dst_in")
        consts = sem("p_consts")
        ident_zero = sem("p_ident_zero")
        loops_made = sem("p_loops_made")
        mean_free, mean_ready = sem("p_mean_free"), sem("p_mean_ready")
        centred, squared = sem("p_centred"), sem("p_squared")
        var_free, var_ready = sem("p_var_free"), sem("p_var_ready")
        logged, rstd_ready = sem("p_logged"), sem("p_rstd_ready")
        normed, y_stored = sem("p_normed"), sem("p_y_stored")
        h_free, h_ready = sem("p_h_free"), sem("p_h_ready")
        key_step = sem("p_key_step")
        counted, total_ready = sem("p_counted"), sem("p_total_ready")
        held = sem("p_held")
        zeroed, ids_stored = sem("p_zeroed"), sem("p_ids_stored")
        block = ctx.enter_context(nc.Block())

        @block.sync
        def _(sp):
            sp.dma_start(w_item[:], w_item_t).then_inc(weights_in, 16)
            sp.dma_start(b_row[:], b_item).then_inc(weights_in, 16)
            sp.dma_start(xc[:], x_t).then_inc(x_in, 16)
            sp.dma_start(s["keys"][:, 1, :], edges[0].rearrange("(p j) -> p j", p=P)).then_inc(src_in, 16)
            sp.dma_start(s["keys"][:, 0, :], edges[1].rearrange("(p j) -> p j", p=P)).then_inc(dst_in, 16)
            for c in range(NCH):
                if c >= 2:
                    sp.wait_ge(item_used, c - 1)
                w = min(CT * P, NPAD - c * CT * P)
                sp.dma_start(item[:, c % 2, 0:w], item_t[:, c * CT * P:c * CT * P + w]).then_inc(item_in[c % 2], 16)
            with sp.Fori(0, NUB // 4) as i:
                sp.wait_ge(normed, 4 * i + 4)
                sp.dma_start(y0_dram[:, bass.ds(i * (4 * UB), 4 * UB)],
                             xc[:, bass.ds(i * (4 * UB), 4 * UB)]).then_inc(y_stored, 16)
            sp.wait_ge(zeroed, 1)
            sp.dma_start(s["end_id"][N:NPAD, :].rearrange("n o -> o n"), zero_ids[:]).then_inc(ids_stored, 16)
            sp.wait_ge(ids_stored, 16)
            sp.wait_ge(y_stored, 16 * (NUB // 4))

        @block.gpsimd
        def _(pool):
            nc.gpsimd.iota(s["keys"][:, 3, :], [[-1, ROW]], base=P * ROW - 1, channel_multiplier=-ROW).then_inc(loops_made, 1)
            nc.gpsimd.memset(s["mean_w"][:], 1.0 / D)
            nc.gpsimd.memset(s["ones"][:], 1.0)
            nc.gpsimd.memset(s["eps"][:], EPS)
            nc.gpsimd.memset(s["zero"][:], 0.0)
            nc.gpsimd.memset(s["tiny"][:], 1e-18)
            nc.gpsimd.memset(s["minus2"][:], -2.0)
            nc.gpsimd.memset(zero_ids[:], 0).then_inc(zeroed, 1)
            nc.gpsimd.iota(part_i[:], [[0, 1]], base=0, channel_multiplier=1)
            nc.gpsimd.memset(s["ident"][:], 0.0).then_inc(ident_zero, 1)
            pool.wait_ge(ident_zero, 1)
            nc.gpsimd.affine_select(out=s["ident"][:], in_=s["ident"][:], compare_op=ALU.not_equal, fill=1.0,
                                    base=0, pattern=[[-1, P]], channel_multiplier=1).then_inc(consts, 1)

        @block.tensor
        def _(pe):
            pe.wait_ge(consts, 1)
            pe.wait_ge(x_in, 16)
            pe.sem_inc(mean_free, 2)
            pe.sem_inc(var_free, 2)
            pe.sem_inc(h_free, 2)
            with pe.Fori(0, NUB // 2) as i:
                for u in range(2):
                    pe.wait_ge(mean_free, 2 * i + u + 1)
                    nc.tensor.matmul(mean_ps[u][:, 0:UB], s["mean_w"][:], xc[:, bass.ds((2 * i + u) * UB, UB)],
                                     start=True, stop=True).then_inc(mean_ready, 1)
            with pe.Fori(0, NUB // 2) as i:
                for u in range(2):
                    pe.wait_ge(var_free, 2 * i + u + 1)
                    pe.wait_ge(squared, 2 * i + u + 1)
                    nc.tensor.matmul(var_ps[u][:, 0:UB], s["mean_w"][:], sq[:, bass.ds((2 * i + u) * UB, UB)],
                                     start=True, stop=True).then_inc(var_ready, 1)
            pe.wait_ge(counted, 1)
            nc.tensor.matmul(tot_ps[:, 0:1], s["ones"][:], count[:, 8:9], start=True, stop=True).then_inc(total_ready, 1)
            pe.wait_ge(weights_in, 32)
            for t in range(NT):
                c, k = divmod(t, CT)
                if k == 0:
                    pe.wait_ge(item_in[c % 2], 16 * (c // 2 + 1))
                g, q = divmod(t, 4)
                if q == 0:
                    pe.wait_ge(h_free, g + 1)
                nc.tensor.matmul(h_ps[g % 2][:, q * D:(q + 1) * D], item[:, c % 2, k * P:(k + 1) * P], w_item[:],
                                 start=True, stop=False)
                last = nc.tensor.matmul(h_ps[g % 2][:, q * D:(q + 1) * D], s["ones"][0:1, :], b_row[:],
                                        start=False, stop=True)
                if k == CT - 1 or t == NT - 1:
                    last.then_inc(item_used, 1)
                elif q == 3:
                    last.then_inc(h_ready, 1)
                if (q == 3 or t == NT - 1) and (k == CT - 1 or t == NT - 1):
                    pe.wait_ge(item_used, c + 1)
                    pe.sem_inc(h_ready, 1)

        @block.scalar
        def _(act):
            with act.Fori(0, NUB) as b:
                hold(act, centred, b + 1, held)
                nc.scalar.activation(sq[:, bass.ds(b * UB, UB)], xc[:, bass.ds(b * UB, UB)], ACT.Square).then_inc(squared, 1)
            with act.Fori(0, NUB // 2) as i:
                nc.scalar.preload_act_table_set("natural_log_exp_and_others")
                for u in range(2):
                    hold(act, var_ready, 2 * i + u + 1, held)
                    nc.scalar.activation(sq[:, bass.ds((2 * i + u) * UB, UB)], var_ps[u][:, 0:UB], ACT.Ln,
                                         bias=s["eps"][:, 0:1]).then_inc(var_free, 1)
                    hold(act, var_free, 2 * i + u + 3, held)
                    nc.scalar.activation(sq[:, bass.ds((2 * i + u) * UB, UB)], sq[:, bass.ds((2 * i + u) * UB, UB)],
                                         ACT.Exp, scale=-0.5).then_inc(rstd_ready, 1)
            for g in range(-(-NT // 4)):
                act.wait_ge(h_ready, g + 1)
                w = min(4, NT - 4 * g)
                nc.scalar.copy(s["h"][:, 4 * g:4 * g + w, :].rearrange("p t d -> p (t d)"),
                               h_ps[g % 2][:, 0:w * D]).then_inc(h_free, 1)

        @block.vector
        def _(dve):
            with dve.Fori(0, NUB // 2) as i:
                for u in range(2):
                    dve.wait_ge(mean_ready, 2 * i + u + 1)
                    nc.vector.tensor_tensor(xc[:, bass.ds((2 * i + u) * UB, UB)], xc[:, bass.ds((2 * i + u) * UB, UB)],
                                            mean_ps[u][:, 0:UB], ALU.subtract).then_inc(centred, 1)
                    dve.wait_ge(centred, 2 * i + u + 1)
                    dve.sem_inc(mean_free, 1)
            with dve.Fori(0, NUB) as b:
                dve.wait_ge(rstd_ready, b + 1)
                nc.vector.tensor_tensor(xc[:, bass.ds(b * UB, UB)], xc[:, bass.ds(b * UB, UB)],
                                        sq[:, bass.ds(b * UB, UB)], ALU.mult).then_inc(normed, 1)

            steps = [0]

            def step(ins):
                steps[0] += 1
                ins.then_inc(key_step, 1)
                dve.wait_ge(key_step, steps[0])

            src, dst, flags, loops = (s["keys"][:, n, :] for n in range(4))
            src, dst = s["keys"][:, 1, :], s["keys"][:, 0, :]
            flags = s["keys"][:, 2, :].bitcast(F32)
            dve.wait_ge(dst_in, 16)
            step(nc.vector.tensor_scalar(flags, dst, float(N), None, ALU.is_lt))
            step(nc.vector.tensor_reduce(count[:, 8:9], flags, AX.X, ALU.add))
            dve.sem_inc(counted, 1)
            step(nc.vector.tensor_scalar(dst, dst, FIELD, None, ALU.min))
            step(nc.vector.tensor_scalar(dst, dst, DST_SHIFT, KEY_BASE, ALU.logical_shift_left, ALU.bitwise_or))
            dve.wait_ge(src_in, 16)
            step(nc.vector.tensor_scalar(src, src, N - 1, 1, ALU.min, ALU.add))
            step(nc.vector.tensor_tensor(dst, dst, src, ALU.bitwise_or))
            dve.wait_ge(loops_made, 1)
            step(nc.vector.tensor_scalar(loops, loops, FIELD, None, ALU.min))
            step(nc.vector.tensor_scalar(loops, loops, DST_SHIFT, KEY_BASE, ALU.logical_shift_left, ALU.bitwise_or))
            dve.wait_ge(total_ready, 1)
            step(nc.vector.tensor_scalar(total_i[:], tot_ps[:, 0:1], float(N), None, ALU.add))
            step(nc.vector.tensor_scalar(total_i[:], total_i[:], 14, None, ALU.logical_shift_right))
            step(nc.vector.tensor_scalar(s["chunks"][:], total_i[:], 1, None, ALU.add))
            dve.wait_ge(consts, 1)
            step(nc.vector.tensor_tensor(s["row_first"][:], part_i[:], s["chunks"][:], ALU.mult))
            for r in range(LOGP):
                step(nc.vector.tensor_scalar(bits[:, r:r + 1], part_i[:], r, 1, ALU.logical_shift_right, ALU.bitwise_and))
            step(nc.vector.tensor_scalar(s["sign"][:], bits[:], -2.0, 1.0, ALU.mult, ALU.add))


def first_pass(nc, shared, adj_t, w_user_t, b_user, y0_dram, r_dram, keys_dram, rows_dram, sums_dram):
    with ExitStack() as ctx:
        sb = lambda name, shape, dt=F32: ctx.enter_context(nc.sbuf_tensor(name, shape, dt))
        pb = lambda name, shape: ctx.enter_context(nc.psum_tensor(name, shape, F32))
        sem = lambda name: keep(shared, ctx.enter_context(nc.semaphore(name)))
        s = shared
        adj = sb("f_adj", [P, NBUF, CT * UB])
        y = sb("f_y", [P, UB])
        r = sb("f_r", [P, UB])
        w_user = sb("f_w_user", [P, D])
        b_u = sb("f_b_user", [P, 1])
        cur = sb("f_cur", [P, CH], I32)
        nxt = sb("f_nxt", [P, CH], I32)
        dst = sb("f_dst", [P, CH + 1], I32)
        same = sb("f_same", [P, CH], I32)
        target = sb("f_target", [P, CH], I32)
        place = sb("f_place", [P, CH], I32)
        row_cur = sb("f_row_cur", [P, 1], I32)
        row_nxt = sb("f_row_nxt", [P, 1], I32)
        blank = sb("f_blank", [P, BLANK])
        acc = pb("f_acc", [P, 512])
        tp = [pb(f"f_tp{n}", [P, 512]) for n in range(4)]

        adj_in = [sem(f"f_adj_in{n}") for n in range(NBUF)]
        adj_used = sem("f_adj_used")
        small_in = sem("f_small_in")
        y_in = sem("f_y_in")
        acc_free, acc_ready = sem("f_acc_free"), sem("f_acc_ready")
        r_stored = sem("f_r_stored")
        blank_made, blanks_stored = sem("f_blank_made"), pool_sem(nc, s, "f_blanks_stored")
        sorted_step = sem("f_sorted_step")
        unflipped = sem("f_unflipped")
        turned, turn_free = sem("f_turned"), sem("f_turn_free")
        place_made = sem("f_place_made")
        keys_stored = pool_sem(nc, s, "f_keys_stored")
        row_ready = sem("f_row_ready")
        chunk_in = pool_sem(nc, s, "f_chunk_in")
        ends_ready = sem("f_ends_ready")
        index_step = sem("f_index_step")
        rows_stored = pool_sem(nc, s, "f_rows_stored")
        ends_stored = pool_sem(nc, s, "f_ends_stored")
        held = sem("f_held")
        block = ctx.enter_context(nc.Block())

        K = [s["keys"][:, n, :].bitcast(F32) for n in range(4)]
        KI = [s["keys"][:, n, :] for n in range(4)]

        done_rows, done_cols = {}, {}
        n = 0
        for k in range(1, LOGR):
            n += k
        n += 1 + LOGR
        done_rows[12] = n
        for k in range(13, 20):
            n += k - LOGP
            done_cols[k] = n
            n += LOGP
            done_rows[k] = n
        n += 1
        merge_first = n
        n += 12
        done_cols[20] = n
        n += LOGP
        done_rows[20] = n

        @block.sync
        def _(sp):
            def load(ub, c):
                w = min(CT, NT - c * CT) * UB
                sp.dma_start(adj[:, c % NBUF, 0:w], adj_t[ub, :, c * CT * UB:c * CT * UB + w]
                             if isinstance(ub, int) else
                             adj_t[bass.ds(ub, 1), :, c * CT * UB:c * CT * UB + w].rearrange("o p n -> (o p) n")
                             ).then_inc(adj_in[c % NBUF], 16)
            for c in range(NCH):
                if c >= NBUF:
                    sp.wait_ge(adj_used, c - NBUF + 1)
                load(0, c)
            with sp.Fori(1, NUB) as ub:
                for c in range(NCH):
                    sp.wait_ge(adj_used, NCH * ub + (c - NBUF + 1))
                    load(ub, c)

        @block.tensor
        def _(pe):
            pe.sem_inc(acc_free, 1)
            pe.sem_inc(turn_free, 4)

            def products(ub, first, last):
                for c in range(first, last):
                    pe.wait_ge(adj_in[c % NBUF], 32 * ub + 16 * (c // NBUF + 1))
                    if c == 0:
                        pe.wait_ge(acc_free, ub + 1)
                    w = min(CT, NT - c * CT)
                    for k in range(w):
                        ins = nc.tensor.matmul(acc[:, 0:UB], s["h"][:, c * CT + k, :], adj[:, c % NBUF, k * UB:(k + 1) * UB],
                                               start=(c == 0 and k == 0), stop=False)
                    ins.then_inc(adj_used, 1)
                if last == NCH:
                    pe.wait_ge(y_in, 16 * ub + 16)
                    nc.tensor.matmul(acc[:, 0:UB], w_user[:], y[:], start=False, stop=True).then_inc(acc_ready, 1)

            def turn(src, group):
                for q in range(8):
                    pe.wait_ge(turn_free, group + (q + 1))
                    for m in range(4):
                        b = 4 * q + m
                        ins = nc.tensor.transpose(tp[q % 4][:, m * P:(m + 1) * P], src[:, b * P:(b + 1) * P], s["ident"][:])
                    ins.then_inc(turned, 1)

            pe.wait_ge(small_in, 32)
            with pe.Fori(0, 5) as ub:
                products(ub, 0, NCH)
            for pair in range(3):
                for v in range(2):
                    k = 13 + 2 * pair + v
                    ub = 5 + 2 * pair + v
                    pe.wait_ge(unflipped, k - 12)
                    turn(K[0], 16 * (k - 13))
                    products(ub, 0, 6)
                    pe.wait_ge(sorted_step, done_cols[k])
                    turn(K[1], 16 * (k - 13) + 8)
                    products(ub, 6, NCH)
            pe.wait_ge(unflipped, 7)
            turn(K[0], 96)
            products(11, 0, 6)
            pe.wait_ge(sorted_step, done_cols[19])
            turn(K[1], 104)
            products(11, 6, NCH)
            pe.wait_ge(sorted_step, merge_first)
            turn(K[1], 112)
            turn(K[2], 120)
            with pe.Fori(12, 14) as ub:
                products(ub, 0, NCH)
            pe.wait_ge(sorted_step, done_cols[20])
            turn(K[0], 128)
            turn(K[3], 136)
            with pe.Fori(14, NUB) as ub:
                products(ub, 0, NCH)

        @block.scalar
        def _(act):
            act.dma_start(w_user[:], w_user_t).then_inc(small_in, 16)
            act.dma_start(b_u[:], b_user).then_inc(small_in, 16)
            act.dma_start(y[:], y0_dram[:, 0:UB]).then_inc(y_in, 16)
            act.wait_ge(small_in, 32)
            act.sem_inc(r_stored, 16)

            def finish(ub, more):
                act.wait_ge(acc_ready, ub + 1)
                act.wait_ge(r_stored, 16 * ub + 16)
                if more:
                    act.dma_start(y[:], y0_dram[:, bass.ds((ub + 1) * UB, UB)]).then_inc(y_in, 16)
                nc.scalar.activation(r[:], acc[:, 0:UB], ACT.Relu, bias=b_u[:, 0:1]).then_inc(acc_free, 1)
                act.wait_ge(acc_free, ub + 2)
                act.dma_start(r_dram[:, bass.ds(ub * UB, UB)], r[:]).then_inc(r_stored, 16)

            def unturn(dst, group, sign=None):
                for q in range(8):
                    act.wait_ge(turned, group + (q + 1))
                    if sign is None:
                        nc.scalar.copy(dst[:, q * 512:(q + 1) * 512], tp[q % 4][:]).then_inc(turn_free, 1)
                    else:
                        nc.scalar.mul(dst[:, q * 512:(q + 1) * 512], tp[q % 4][:], sign).then_inc(turn_free, 1)

            with act.Fori(0, 5) as ub:
                finish(ub, True)
            for k in range(13, 20):
                act.wait_ge(sorted_step, done_rows[k - 1])
                nc.scalar.mul(K[0], K[0], s["sign"][:, k - 13:k - 12]).then_inc(unflipped, 1)
                unturn(K[1] if (k - LOGP) % 2 == 0 else K[2], 16 * (k - 13))
                unturn(K[2], 16 * (k - 13) + 8, s["sign"][:, k - 12:k - 11] if k < 19 else None)
                finish(k - 8, True)
            unturn(K[0], 112)
            unturn(K[3], 120)
            with act.Fori(12, 14) as ub:
                finish(ub, True)
            unturn(K[1], 128)
            unturn(K[2], 136)
            with act.Fori(14, NUB - 1) as ub:
                finish(ub, True)
            finish(NUB - 1, False)
            act.wait_ge(r_stored, 16 * NUB + 16)

        @block.vector
        def _(dve):
            steps = [0]

            def exchange(pairs):
                for lo_in, hi_in, lo_out, hi_out, up in pairs:
                    nc.vector.tensor_tensor(lo_out, lo_in, hi_in, ALU.min if up else ALU.max)
                    ins = nc.vector.tensor_tensor(hi_out, lo_in, hi_in, ALU.max if up else ALU.min)
                steps[0] += 1
                ins.then_inc(sorted_step, 1)
                dve.wait_ge(sorted_step, steps[0])

            def stage(bufs_in, bufs_out, b, k):
                pairs = []
                for i, o in zip(bufs_in, bufs_out):
                    for (li, hi, up), (lo, ho, _) in zip(stage_views(i, b, k, LOGR), stage_views(o, b, k, LOGR)):
                        pairs.append((li, hi, lo, ho, up))
                exchange(pairs)

            at = 0
            for k in range(1, LOGR):
                for b in reversed(range(k)):
                    stage([K[at]], [K[1 - at]], b, k)
                    at = 1 - at
            assert at == 0
            nc.vector.tensor_scalar(K[0], K[0], s["sign"][:, 0:1], None, ALU.mult).then_inc(sorted_step, 1)
            steps[0] += 1
            dve.wait_ge(sorted_step, steps[0])
            for b in reversed(range(LOGR)):
                stage([K[at]], [K[1 - at]], b, None)
                at = 1 - at
            assert at == 0 and steps[0] == done_rows[12]
            for k in range(13, 20):
                dve.wait_ge(turn_free, 4 + 16 * (k - 13) + 8)
                at = 1 if (k - LOGP) % 2 == 0 else 2
                for b in reversed(range(LOGP, k)):
                    place_bit = b - LOGR if b >= LOGR else b
                    stage([K[at]], [K[3 - at]], place_bit, k - LOGR if k < 19 else None)
                    at = 3 - at
                assert at == 1 and steps[0] == done_cols[k]
                dve.wait_ge(turn_free, 4 + 16 * (k - 13) + 16)
                at = 2
                for b in reversed(range(LOGP)):
                    stage([K[at]], [K[2 - at]], b, None)
                    at = 2 - at
                assert at == 0 and steps[0] == done_rows[k]
            exchange([(K[0], K[3], K[1], K[2], True)])
            dve.wait_ge(turn_free, 4 + 128)
            a, o = [K[0], K[3]], [K[1], K[2]]
            for b in reversed(range(LOGP, 19)):
                stage(a, o, b - LOGR if b >= LOGR else b, None)
                a, o = o, a
            dve.wait_ge(turn_free, 4 + 144)
            a, o = [K[1], K[2]], [K[0], K[3]]
            for b in reversed(range(LOGP)):
                stage(a, o, b, None)
                a, o = o, a
            assert steps[0] == done_rows[20]

            count = dve.value_load(s["chunks"][0:1, 0:1], min_val=1, max_val=CHMAX)
            nc.vector.tensor_copy(row_cur[:], s["row_first"][:])
            nc.vector.tensor_scalar(row_nxt[:], s["row_first"][:], 1, None, ALU.add).then_inc(row_ready, 1)
            dve.wait_ge(place_made, 1)
            with dve.Fori(0, count) as i:
                dve.wait_ge(chunk_in, 32 * i + 32)
                nc.vector.tensor_scalar(row_cur[:], row_cur[:], 1, None, ALU.add)
                nc.vector.tensor_scalar(row_nxt[:], row_nxt[:], 1, None, ALU.add)
                nc.vector.tensor_scalar(dst[:, 0:CH], cur[:], DST_SHIFT, FIELD, ALU.logical_shift_right, ALU.bitwise_and)
                nc.vector.tensor_scalar(dst[:, CH:CH + 1], nxt[:, 0:1], DST_SHIFT, FIELD, ALU.logical_shift_right,
                                        ALU.bitwise_and).then_inc(index_step, 1)
                dve.wait_ge(index_step, 3 * i + 1)
                nc.vector.tensor_tensor(same[:], dst[:, 0:CH], dst[:, 1:CH + 1], ALU.is_equal).then_inc(index_step, 1)
                dve.wait_ge(index_step, 3 * i + 2)
                nc.vector.scalar_tensor_tensor(out=target[:], in0=same[:], scalar=float(BIG), in1=dst[:, 0:CH],
                                               op0=ALU.mult, op1=ALU.add)
                nc.vector.tensor_scalar(place[:], place[:], CH, None, ALU.add).then_inc(index_step, 1)
                dve.wait_ge(index_step, 3 * i + 3)
                dve.sem_inc(ends_ready, 1)
                dve.wait_ge(ends_stored, i * (16 * CH) + 16 * CH)
                dve.sem_inc(row_ready, 1)

        @block.gpsimd
        def _(pool):
            nc.gpsimd.iota(place[:], [[1, CH]], base=-CH, channel_multiplier=RMAX).then_inc(place_made, 1)
            nc.gpsimd.memset(blank[:], 0.0).then_inc(blank_made, 1)
            pool.wait_ge(blank_made, 1)
            sums_flat = sums_dram.rearrange("(p c) f -> p (c f)", p=P)
            with pool.Fori(0, RMAX * STW // BLANK) as i:
                pool.dma_start(sums_flat[:, bass.ds(i * BLANK, BLANK)], blank[:]).then_inc(blanks_stored, 16)
            pool.wait_ge(blanks_stored, RMAX * STW // BLANK * 16)
            pool.wait_ge(sorted_step, done_rows[20])
            for half, n in ((0, 0), (1, 3)):
                pool.dma_start(keys_dram[half * E:(half + 1) * E].rearrange("(p j) -> p j", p=P), KI[n]).then_inc(keys_stored, 16)
            pool.wait_ge(keys_stored, 32)
            count = pool.value_load(s["chunks"][0:1, 0:1], min_val=1, max_val=CHMAX)
            by_chunk = keys_dram.rearrange("(n j) -> n j", j=CH)
            with pool.Fori(0, count) as i:
                hold(pool, row_ready, i + 1, held)
                pool.indirect_dma_start(cur[:], None, by_chunk, bass.IndirectOffsetOnAxis(ap=row_cur[:, 0:1], axis=0)).then_inc(chunk_in, 16)
                pool.indirect_dma_start(nxt[:], None, by_chunk, bass.IndirectOffsetOnAxis(ap=row_nxt[:, 0:1], axis=0)).then_inc(chunk_in, 16)
                pool.wait_ge(chunk_in, 32 * i + 32)
                pool.dma_start(rows_dram[:, bass.ds(i * CH, CH)], cur[:]).then_inc(rows_stored, 16)
                hold(pool, ends_ready, i + 1, held)
                for j in range(CH):
                    pool.indirect_dma_start(s["end_id"], bass.IndirectOffsetOnAxis(ap=target[:, j:j + 1], axis=0),
                                            place[:, j:j + 1], None, bounds_check=N - 1, oob_is_err=False).then_inc(ends_stored, 16)
                hold(pool, rows_stored, 16 * i + 16, held)
            pool.dma_start(rows_dram[:, bass.ds(count * CH, CH)], cur[:]).then_inc(rows_stored, 16)
            hold(pool, rows_stored, 16 * count + 16, held)
            hold(pool, ends_stored, count * (16 * CH), held)


def layernorm(nc, shared, name, add=None, gamma=None, beta=None):
    with ExitStack() as ctx:
        sb = lambda what, shape, dt=F32: ctx.enter_context(nc.sbuf_tensor(f"{name}_{what}", shape, dt))
        pb = lambda what, shape: ctx.enter_context(nc.psum_tensor(f"{name}_{what}", shape, F32))
        sem = lambda what: keep(shared, ctx.enter_context(nc.semaphore(f"{name}_{what}")))
        s = shared
        x, y = s["x"], s["y"]
        sq = sb("sq", [P, N])
        gain = sb("gain", [P, 2])
        mean_ps = [pb(f"mean{u}", [P, 512]) for u in range(2)]
        var_ps = [pb(f"var{u}", [P, 512]) for u in range(2)]
        held, add_in, gain_in, added = sem("held"), sem("add_in"), sem("gain_in"), sem("added")
        centred, squared, scaled, normed = sem("centred"), sem("squared"), sem("scaled"), sem("normed")
        mean_free, mean_ready, var_free, var_ready = sem("mean_free"), sem("mean_ready"), sem("var_free"), sem("var_ready")
        rstd_ready = sem("rstd_ready")
        block = ctx.enter_context(nc.Block())
        at = lambda t, b: t[:, bass.ds(b * UB, UB)]

        @block.sync
        def _(sp):
            if add is not None:
                sp.dma_start(x[:], s["x_in"]).then_inc(add_in, 16)
                sp.dma_start(y[:, 0:N], add).then_inc(add_in, 16)
                sp.wait_ge(add_in, 32)
            if gamma is not None:
                sp.dma_start(gain[:, 0:1], gamma).then_inc(gain_in, 16)
                sp.dma_start(gain[:, 1:2], beta).then_inc(gain_in, 16)
                sp.wait_ge(gain_in, 32)

        @block.tensor
        def _(pe):
            pe.sem_inc(mean_free, 2)
            pe.sem_inc(var_free, 2)
            with pe.Fori(0, NUB // 2) as i:
                for u in range(2):
                    b = 2 * i + u
                    pe.wait_ge(mean_free, b + 1)
                    if add is not None:
                        pe.wait_ge(added, b + 1)
                    nc.tensor.matmul(mean_ps[u][:, 0:UB], s["mean_w"][:], at(x, b), start=True, stop=True).then_inc(mean_ready, 1)
            with pe.Fori(0, NUB // 2) as i:
                for u in range(2):
                    b = 2 * i + u
                    pe.wait_ge(var_free, b + 1)
                    pe.wait_ge(squared, b + 1)
                    nc.tensor.matmul(var_ps[u][:, 0:UB], s["mean_w"][:], at(sq, b), start=True, stop=True).then_inc(var_ready, 1)

        @block.scalar
        def _(act):
            with act.Fori(0, NUB) as b:
                hold(act, centred, b + 1, held)
                nc.scalar.activation(at(sq, b), at(y, b), ACT.Square).then_inc(squared, 1)
            with act.Fori(0, NUB // 2) as i:
                nc.scalar.preload_act_table_set("natural_log_exp_and_others")
                for u in range(2):
                    b = 2 * i + u
                    hold(act, var_ready, b + 1, held)
                    nc.scalar.activation(at(sq, b), var_ps[u][:, 0:UB], ACT.Ln, bias=s["eps"][:, 0:1]).then_inc(var_free, 1)
                    hold(act, var_free, b + 3, held)
                    nc.scalar.activation(at(sq, b), at(sq, b), ACT.Exp, scale=-0.5).then_inc(rstd_ready, 1)

        @block.vector
        def _(dve):
            if add is not None:
                nc.vector.memset(y[:, N:NPAD], 0.0)
                dve.wait_ge(add_in, 32)
            with dve.Fori(0, NUB // 2) as i:
                if add is not None:
                    for u in range(2):
                        b = 2 * i + u
                        nc.vector.tensor_tensor(at(x, b), at(x, b), at(y, b), ALU.add).then_inc(added, 1)
                for u in range(2):
                    b = 2 * i + u
                    dve.wait_ge(mean_ready, b + 1)
                    nc.vector.tensor_tensor(at(y, b), at(x, b), mean_ps[u][:, 0:UB], ALU.subtract).then_inc(centred, 1)
                    dve.wait_ge(centred, b + 1)
                    dve.sem_inc(mean_free, 1)
            if gamma is not None:
                dve.wait_ge(gain_in, 32)
            with dve.Fori(0, NUB) as b:
                dve.wait_ge(rstd_ready, b + 1)
                if gamma is None:
                    nc.vector.tensor_tensor(at(y, b), at(y, b), at(sq, b), ALU.mult).then_inc(normed, 1)
                else:
                    nc.vector.scalar_tensor_tensor(out=at(y, b), in0=at(y, b), scalar=gain[:, 0:1], in1=at(sq, b),
                                                   op0=ALU.mult, op1=ALU.mult).then_inc(scaled, 1)
                    dve.wait_ge(scaled, b + 1)
                    nc.vector.tensor_scalar(at(y, b), at(y, b), gain[:, 1:2], None, ALU.add).then_inc(normed, 1)


def node_table(nc, shared, w_gat, att_src, att_dst):
    with ExitStack() as ctx:
        sb = lambda name, shape, dt=F32: ctx.enter_context(nc.sbuf_tensor(name, shape, dt))
        pb = lambda name, shape: ctx.enter_context(nc.psum_tensor(name, shape, F32))
        sem = lambda name: keep(shared, ctx.enter_context(nc.semaphore(name)))
        s = shared
        w = sb("n_w", [P, H0 * C0])
        att = sb("n_att", [P, 2, H0 * C0])
        table = sb("n_table", [P, NT, TABW])
        prod = sb("n_prod", [P, NT, H0 * C0])
        h_ps = pb("n_h", [P, 3, 512])
        small_in, h_ready, padded = sem("n_small_in"), sem("n_h_ready"), sem("n_padded")
        step_done, table_ready, table_stored = sem("n_step"), sem("n_table_ready"), sem("n_table_stored")
        block = ctx.enter_context(nc.Block())

        @block.sync
        def _(sp):
            sp.dma_start(w[:], w_gat).then_inc(small_in, 16)
            for n, v in enumerate((att_src, att_dst)):
                sp.dma_start(att[:, n, :], v.to_broadcast([P, H0 * C0])).then_inc(small_in, 16)
            sp.wait_ge(table_ready, 1)
            sp.dma_start(s["table"].rearrange("(p t) f -> p (t f)", p=P), table[:].rearrange("p t f -> p (t f)")).then_inc(table_stored, 16)
            sp.wait_ge(table_stored, 16)

        @block.gpsimd
        def _(pool):
            for k in range(H0):
                ins = nc.gpsimd.memset(table[:, :, k * HC + C0:k * HC + HC], 1.0)
            ins.then_inc(padded, 1)

        @block.tensor
        def _(pe):
            pe.wait_ge(small_in, 48)
            by_tile = s["y"][:].rearrange("p (n t) -> p t n", t=NT)
            for t in range(NT):
                at = t % 32 * 16
                ins = nc.tensor.matmul(h_ps[:, t // 32, at:at + 16], by_tile[:, t, :], w[:], start=True, stop=True)
            ins.then_inc(h_ready, 1)

        @block.vector
        def _(dve):
            steps = [0]

            def step(ins):
                steps[0] += 1
                ins.then_inc(step_done, 1)
                dve.wait_ge(step_done, steps[0])

            dve.wait_ge(h_ready, 1)
            dve.wait_ge(padded, 1)
            dve.wait_ge(small_in, 48)
            for g in range(3):
                n = min(32, NT - 32 * g)
                ins = nc.vector.tensor_copy(
                    table[:, 32 * g:32 * g + n, 0:NF].rearrange("p t (k c) -> p t k c", c=HC)[:, :, :, 0:C0],
                    h_ps[:, g, 0:16 * n].rearrange("p (t k c) -> p t k c", k=H0, c=C0))
            step(ins)
            heads = table[:, :, 0:NF].rearrange("p t (k c) -> p t k c", c=HC)[:, :, :, 0:C0]
            for n in range(2):
                for k in range(H0):
                    ins = nc.vector.tensor_tensor(
                        prod[:, :, k * C0:(k + 1) * C0], heads[:, :, k, :],
                        att[:, n:n + 1, k * C0:(k + 1) * C0].to_broadcast([P, NT, C0]), ALU.mult)
                step(ins)
                step(nc.vector.tensor_reduce(table[:, :, NF + n * H0:NF + n * H0 + H0],
                                             prod[:].rearrange("p t (k c) -> p t k c", c=C0), AX.X, ALU.add))
            dve.sem_inc(table_ready, 1)


def attend(nc, shared, rows_dram, sums_dram):
    with ExitStack() as ctx:
        sb = lambda name, shape, dt=F32: ctx.enter_context(nc.sbuf_tensor(name, shape, dt))
        pb = lambda name, shape: ctx.enter_context(nc.psum_tensor(name, shape, F32))
        sem = lambda name: keep(shared, ctx.enter_context(nc.semaphore(name)))
        s = shared
        keys = [sb(f"a_keys{u}", [P, HF], I32) for u in range(2)]
        field = sb("a_field", [P, HF], I32)
        dst = sb("a_dst", [P, HF], I32)
        is_loop = sb("a_is_loop", [P, HF], I32)
        index = [sb(f"a_index{u}", [P, HF], I32) for u in range(2)]
        first = [sb(f"a_first{u}", [P, HF]) for u in range(2)]
        rest_ = [sb(f"a_rest{u}", [P, HF]) for u in range(2)]
        wall = [sb(f"a_wall{u}", [P, HF]) for u in range(2)]
        got = [sb(f"a_got{u}", [P, HF, TABW]) for u in range(2)]
        start = sb("a_start", [P, H0, HF])
        a_dst = [sb(f"a_a_dst{u}", [P, H0, HF]) for u in range(2)]
        score = sb("a_score", [P, H0, HF])
        top = [sb(f"a_top{u}", [P, H0, HF + 1]) for u in range(2)]
        weight = sb("a_weight", [P, 2, H0, HF])
        value = sb("a_value", [P, NF, HF])
        sums = [sb(f"a_sums{u}", [P, HF, STW]) for u in range(2)]
        row_key = sb("a_row_key", [P, 1], I32)
        row_dst = sb("a_row_dst", [P, 1], I32)
        row_index = sb("a_row_index", [P, 1], I32)
        row_got = sb("a_row_got", [P, TABW])
        tail = sb("a_tail", [P, 4, NF])
        rows = sb("a_rows", [NF, 4, P])
        join = sb("a_join", [NF, 8, P])
        run_top = sb("a_run_top", [NF, P + 1])
        run_sum = sb("a_run_sum", [NF, P + 1])
        carry = sb("a_carry", [P, 3, NF])
        last_key = sb("a_last_key", [P, 1], I32)
        last_dst = sb("a_last_dst", [P, 1], I32)
        end_f = sb("a_end_f", [P, 2])
        place_f = sb("a_place_f", [P, 1])
        target_f = sb("a_target_f", [P, 1])
        place = sb("a_place", [P, 1], I32)
        target = sb("a_target", [P, 1], I32)
        ended = sb("a_ended", [P, STW])
        mix = sb("a_mix", [P, 6, NF])
        tr_ps = pb("a_tr", [P, 4, P])
        back_ps = pb("a_back", [P, 4, P])

        held = sem("a_held")
        keys_in = [sem(f"a_keys_in{u}") for u in range(2)]
        keys_used = sem("a_keys_used")
        row_in, row_ready, row_got_in, row_set = sem("a_row_in"), sem("a_row_ready"), pool_sem(nc, s, "a_row_got_in"), sem("a_row_set")
        index_ready, got_in, got_used = sem("a_index_ready"), [pool_sem(nc, s, f"a_got_in{u}") for u in range(2)], sem("a_got_used")
        prep_step, main_step = sem("a_prep_step"), sem("a_main_step")
        gaps_ready, weights_ready = sem("a_gaps_ready"), sem("a_weights_ready")
        sums_ready, sums_stored = sem("a_sums_ready"), [sem(f"a_sums_stored{u}") for u in range(2)]
        end_step, tails_ready, turned = sem("a_end_step"), sem("a_tails_ready"), sem("a_turned")
        gap_ready, gap_exp, carry_ready, carry_turned = sem("a_gap_ready"), sem("a_gap_exp"), sem("a_carry_ready"), sem("a_carry_turned")
        place_in, ended_in, mix_ready, mix_exp = pool_sem(nc, s, "a_place_in"), pool_sem(nc, s, "a_ended_in"), sem("a_mix_ready"), sem("a_mix_exp")
        last_in = sem("a_last_in")
        fixed, fixed_stored, edges_done = sem("a_fixed"), pool_sem(nc, s, "a_fixed_stored"), sem("a_edges_done")
        block = ctx.enter_context(nc.Block())
        sums_flat = sums_dram.rearrange("(p c) f -> p (c f)", p=P)

        @block.sync
        def _(sp):
            count = sp.value_load(s["chunks"][0:1, 0:1], min_val=1, max_val=CHMAX)
            sp.dma_start(row_key[:], rows_dram[:, 0:1], allow_slow_non_contiguous=True).then_inc(row_in, 16)
            for u in range(2):
                sp.dma_start(keys[u][:], rows_dram[:, u * HF:(u + 1) * HF]).then_inc(keys_in[u], 16)
                sp.sem_inc(sums_stored[u], 16)
            with sp.Fori(0, count) as i:
                for u in range(2):
                    sp.wait_ge(keys_used, 2 * i + u + 1)
                    sp.dma_start(keys[u][:], rows_dram[:, bass.ds((i + 1) * CH + u * HF, HF)]).then_inc(keys_in[u], 16)
                    sp.wait_ge(sums_ready, 2 * i + u + 1)
                    sp.dma_start(sums_flat[:, bass.ds((i * CH + u * HF) * STW, HF * STW)],
                                 sums[u][:].rearrange("p c f -> p (c f)")).then_inc(sums_stored[u], 16)
            sp.dma_start(last_key[:], rows_dram[:, bass.ds(count * CH - 1, 1)], allow_slow_non_contiguous=True).then_inc(last_in, 16)
            for u in range(2):
                hold(sp, sums_stored[u], 16 * count + 16, held)
                hold(sp, keys_in[u], 16 * count + 16, held)
            sp.sem_inc(edges_done, 1)

        @block.gpsimd
        def _(pool):
            count = pool.value_load(s["chunks"][0:1, 0:1], min_val=1, max_val=CHMAX)
            pool.wait_ge(row_ready, 1)
            pool.indirect_dma_start(row_got[:], None, s["table"], bass.IndirectOffsetOnAxis(ap=row_index[:, 0:1], axis=0)).then_inc(row_got_in, 16)
            pool.sem_inc(got_used, 2)
            with pool.Fori(0, count) as i:
                for u in range(2):
                    hold(pool, index_ready, 2 * i + u + 1, held)
                    hold(pool, got_used, 2 * i + u + 1, held)
                    for j in range(HF):
                        pool.indirect_dma_start(got[u][:, j, :], None, s["table"],
                                                bass.IndirectOffsetOnAxis(ap=index[u][:, j:j + 1], axis=0)).then_inc(got_in[u], 16)
            pool.wait_ge(edges_done, 1)
            pool.indirect_dma_start(place[:], None, s["end_id"], bass.IndirectOffsetOnAxis(ap=row_index[:, 0:1], axis=0)).then_inc(place_in, 16)
            pool.wait_ge(place_in, 16)
            pool.indirect_dma_start(ended[:], None, sums_dram, bass.IndirectOffsetOnAxis(ap=place[:, 0:1], axis=0)).then_inc(ended_in, 16)
            pool.wait_ge(fixed, 1)
            pool.indirect_dma_start(sums_dram, bass.IndirectOffsetOnAxis(ap=target[:, 0:1], axis=0), ended[:], None,
                                    bounds_check=P * RMAX - 1, oob_is_err=False).then_inc(fixed_stored, 16)
            pool.wait_ge(fixed_stored, 16)

        @block.scalar
        def _(act):
            count = act.value_load(s["chunks"][0:1, 0:1], min_val=1, max_val=CHMAX)
            with act.Fori(0, count) as i:
                for u in range(2):
                    act.wait_ge(gaps_ready, 2 * i + u + 1)
                    nc.scalar.activation(weight[:], weight[:], ACT.Exp).then_inc(weights_ready, 1)
            act.wait_ge(gap_ready, 1)
            nc.scalar.activation(join[:, 5:7, :], join[:, 5:7, :], ACT.Exp).then_inc(gap_exp, 1)
            act.wait_ge(mix_ready, 1)
            nc.scalar.activation(mix[:, 1:3, :], mix[:, 1:3, :], ACT.Exp).then_inc(mix_exp, 1)

        @block.vector
        def _(dve):
            count = dve.value_load(s["chunks"][0:1, 0:1], min_val=1, max_val=CHMAX)
            steps = [0]

            def step(ins, sem):
                steps[0] += 1
                ins.then_inc(sem, 1)
                dve.wait_ge(sem, steps[0])

            dve.wait_ge(row_in, 16)
            step(nc.vector.tensor_scalar(row_dst[:], row_key[:], DST_SHIFT, FIELD, ALU.logical_shift_right, ALU.bitwise_and), row_set)
            step(nc.vector.tensor_scalar(row_index[:], row_dst[:], N - 1, None, ALU.min), row_set)
            dve.sem_inc(row_ready, 1)
            nc.vector.memset(top[1][:, :, HF:HF + 1], NEG)
            step(nc.vector.memset(sums[1][:, HF - 1, :], 0.0), row_set)
            dve.wait_ge(row_got_in, 16)
            step(nc.vector.tensor_copy(a_dst[1][:, :, HF - 1], row_got[:, NF + H0:TABW]), row_set)

            PREP, MAIN = 4, 9

            def prep(u, n):
                at = PREP * n

                def done(ins, k):
                    ins.then_inc(prep_step, 1)
                    dve.wait_ge(prep_step, at + k)
                dve.wait_ge(keys_in[u], 8 * n + (16 - 8 * u))
                nc.vector.tensor_scalar(field[:], keys[u][:], FIELD, None, ALU.bitwise_and)
                done(nc.vector.tensor_scalar(dst[:], keys[u][:], DST_SHIFT, FIELD, ALU.logical_shift_right, ALU.bitwise_and), 1)
                nc.vector.tensor_scalar(first[u][:], field[:], 0, None, ALU.is_equal)
                done(nc.vector.tensor_scalar(is_loop[:], field[:], 0, None, ALU.is_equal), 2)
                nc.vector.tensor_scalar(rest_[u][:], first[u][:], -1.0, 1.0, ALU.mult, ALU.add)
                nc.vector.tensor_scalar(wall[u][:], first[u][:], NEG, None, ALU.mult)
                nc.vector.tensor_scalar(field[:], field[:], 1, None, ALU.subtract)
                done(nc.vector.scalar_tensor_tensor(out=dst[:], in0=dst[:], scalar=1, in1=is_loop[:], op0=ALU.add, op1=ALU.mult), 3)
                dve.sem_inc(held, 1)
                done(nc.vector.tensor_tensor(dst[:], dst[:], field[:], ALU.add), 4)
                nc.vector.tensor_scalar(index[u][:], dst[:], N - 1, None, ALU.min).then_inc(index_ready, 1)
                dve.wait_ge(index_ready, n + 1)
                dve.sem_inc(keys_used, 1)

            def halves(u, i):
                n = 2 * i + u
                at = MAIN * n
                g, t, before = got[u], top[u], 1 - u
                each = lambda v: v[:].rearrange("p (o j) -> p o j", o=1).to_broadcast([P, H0, HF])

                def done(ins, k):
                    ins.then_inc(main_step, 1)
                    dve.wait_ge(main_step, at + k)

                dve.wait_ge(got_in[u], i * (16 * HF) + 16 * HF)
                nc.vector.tensor_copy(t[:, :, 0:1], top[before][:, :, HF:HF + 1])
                done(nc.vector.tensor_tensor(start[:], g[:, :, NF + H0:TABW].rearrange("p j k -> p k j"), each(first[u]), ALU.mult), 1)
                for k in range(H0):
                    ins = nc.vector.tensor_tensor_scan(a_dst[u][:, k, :], rest_[u][:], start[:, k, :],
                                                       a_dst[before][:, k, HF - 1:HF], ALU.mult, ALU.add)
                done(ins, 2)
                done(nc.vector.tensor_tensor(start[:], g[:, :, NF:NF + H0].rearrange("p j k -> p k j"), a_dst[u][:], ALU.add), 3)
                done(nc.vector.scalar_tensor_tensor(out=score[:], in0=start[:], scalar=0.2, in1=start[:], op0=ALU.mult, op1=ALU.max), 4)
                for k in range(H0):
                    ins = nc.vector.tensor_tensor_scan(t[:, k, 1:HF + 1], wall[u][:], score[:, k, :], t[:, k, 0:1], ALU.add, ALU.max)
                done(ins, 5)
                nc.vector.tensor_tensor(weight[:, 1], score[:], t[:, :, 1:HF + 1], ALU.subtract)
                done(nc.vector.tensor_tensor(weight[:, 0], t[:, :, 0:HF], t[:, :, 1:HF + 1], ALU.subtract), 6)
                done(nc.vector.tensor_tensor(weight[:, 0], weight[:, 0], each(wall[u]), ALU.add), 7)
                dve.sem_inc(gaps_ready, 1)
                dve.wait_ge(weights_ready, n + 1)
                for k in range(H0):
                    ins = nc.vector.tensor_tensor(value[:, k * HC:(k + 1) * HC, :],
                                                  g[:, :, k * HC:(k + 1) * HC].rearrange("p j c -> p c j"),
                                                  weight[:, 1, k:k + 1, :].to_broadcast([P, HC, HF]), ALU.mult)
                done(ins, 8)
                dve.sem_inc(got_used, 1)
                dve.wait_ge(sums_stored[u], 16 * i + 16)
                for f in range(NF):
                    nc.vector.tensor_tensor_scan(sums[u][:, :, f], weight[:, 0, f // HC, :], value[:, f, :],
                                                 sums[before][:, HF - 1, f:f + 1], ALU.mult, ALU.add)
                done(nc.vector.tensor_copy(sums[u][:, :, NF:STW], t[:, :, 1:HF + 1].rearrange("p k j -> p j k")), 9)
                dve.sem_inc(sums_ready, 1)

            prep(0, 0)
            with dve.Fori(0, count) as i:
                prep(1, 2 * i + 1)
                halves(0, i)
                prep(0, 2 * i + 2)
                halves(1, i)

            steps[0] = 0
            step = lambda ins: (steps.__setitem__(0, steps[0] + 1), ins.then_inc(end_step, 1), dve.wait_ge(end_step, steps[0]))
            dve.wait_ge(last_in, 16)
            nc.vector.tensor_copy(tail[:, 0, :], sums[1][:, HF - 1, 0:NF])
            for k in range(H0):
                nc.vector.tensor_scalar(tail[:, 1, k * HC:(k + 1) * HC], s["ones"][:, 0:HC], top[1][:, k, HF:HF + 1], None, ALU.mult)
            nc.vector.tensor_copy(end_f[:, 1:2], row_dst[:])
            step(nc.vector.tensor_scalar(last_dst[:], last_key[:], DST_SHIFT, FIELD, ALU.logical_shift_right, ALU.bitwise_and))
            step(nc.vector.tensor_copy(end_f[:, 0:1], last_dst[:]))
            nc.vector.tensor_scalar(tail[:, 2, :], s["ones"][:, 0:NF], end_f[:, 0:1], None, ALU.mult)
            step(nc.vector.tensor_scalar(tail[:, 3, :], s["ones"][:, 0:NF], end_f[:, 1:2], None, ALU.mult))
            dve.sem_inc(tails_ready, 1)
            dve.wait_ge(turned, 1)
            nc.vector.memset(run_top[:, 0:1], NEG)
            nc.vector.memset(run_sum[:, 0:1], 0.0)
            nc.vector.memset(join[:, 0, 0:1], 0.0)
            nc.vector.memset(join[:, 4, P - 1:P], 0.0)
            step(nc.vector.tensor_copy(rows[:], tr_ps[0:NF, :, :]))
            S, M, T, F = (rows[:, n, :] for n in range(4))
            CONT, WHOLE, THROUGH, WALL, ON, RATIO, SHARE, PART = (join[:, n, :] for n in range(8))
            nc.vector.tensor_tensor(CONT[:, 1:P], F[:, 1:P], T[:, 0:P - 1], ALU.is_equal)
            nc.vector.tensor_tensor(ON[:, 0:P - 1], F[:, 1:P], T[:, 0:P - 1], ALU.is_equal)
            step(nc.vector.tensor_tensor(WHOLE, F, T, ALU.is_equal))
            step(nc.vector.tensor_tensor(THROUGH, CONT, WHOLE, ALU.mult))
            step(nc.vector.tensor_scalar(WALL, THROUGH, -NEG, NEG, ALU.mult, ALU.add))
            step(nc.vector.tensor_tensor_scan(run_top[:, 1:P + 1], WALL, M, NEG, ALU.add, ALU.max))
            nc.vector.tensor_tensor(SHARE, M, run_top[:, 1:P + 1], ALU.subtract)
            step(nc.vector.tensor_tensor(RATIO, run_top[:, 0:P], run_top[:, 1:P + 1], ALU.subtract))
            step(nc.vector.tensor_tensor(RATIO, RATIO, WALL, ALU.add))
            dve.sem_inc(gap_ready, 1)
            dve.wait_ge(gap_exp, 1)
            step(nc.vector.tensor_tensor(PART, S, SHARE, ALU.mult))
            nc.vector.tensor_tensor_scan(run_sum[:, 1:P + 1], RATIO, PART, 0.0, ALU.mult, ALU.add)
            step(nc.vector.tensor_tensor(THROUGH, WHOLE, ON, ALU.mult))
            step(nc.vector.tensor_scalar(THROUGH, THROUGH, -1.0, 1.0, ALU.mult, ALU.add))
            step(nc.vector.tensor_tensor(THROUGH, THROUGH, CONT, ALU.mult))
            step(nc.vector.scalar_tensor_tensor(out=THROUGH, in0=F, scalar=float(N), in1=THROUGH, op0=ALU.is_lt, op1=ALU.mult))
            dve.sem_inc(carry_ready, 1)
            dve.wait_ge(carry_turned, 1)
            step(nc.vector.tensor_copy(carry[:], back_ps[:, 0:3, 0:NF]))
            dve.wait_ge(place_in, 16)
            dve.wait_ge(ended_in, 16)
            for k in range(H0):
                nc.vector.tensor_scalar(mix[:, 0, k * HC:(k + 1) * HC], s["ones"][:, 0:HC], ended[:, NF + k:NF + k + 1], None, ALU.mult)
            nc.vector.tensor_copy(place_f[:], place[:])
            step(nc.vector.tensor_scalar(target_f[:], carry[:, 2, 0:1], -float(BIG), float(BIG), ALU.mult, ALU.add))
            nc.vector.tensor_tensor(target[:], target_f[:], place_f[:], ALU.add)
            step(nc.vector.tensor_tensor(mix[:, 3, :], mix[:, 0, :], carry[:, 0, :], ALU.max))
            nc.vector.tensor_tensor(mix[:, 1, :], mix[:, 0, :], mix[:, 3, :], ALU.subtract)
            step(nc.vector.tensor_tensor(mix[:, 2, :], carry[:, 0, :], mix[:, 3, :], ALU.subtract))
            dve.sem_inc(mix_ready, 1)
            dve.wait_ge(mix_exp, 1)
            nc.vector.tensor_tensor(mix[:, 4, :], ended[:, 0:NF], mix[:, 1, :], ALU.mult)
            step(nc.vector.tensor_tensor(mix[:, 5, :], carry[:, 1, :], mix[:, 2, :], ALU.mult))
            nc.vector.tensor_tensor(ended[:, 0:NF], mix[:, 4, :], mix[:, 5, :], ALU.add)
            step(nc.vector.tensor_copy(ended[:, NF:STW], mix[:, 3, :].rearrange("p (k c) -> p k c", c=HC)[:, :, 0]))
            dve.sem_inc(fixed, 1)

        @block.tensor
        def _(pe):
            pe.wait_ge(tails_ready, 1)
            for n in range(4):
                ins = nc.tensor.transpose(tr_ps[0:NF, n, :], tail[:, n, :], s["ident"][:])
            ins.then_inc(turned, 1)
            pe.wait_ge(carry_ready, 1)
            for n, v in enumerate((run_top[:, 0:P], run_sum[:, 0:P], join[:, 2, :])):
                ins = nc.tensor.transpose(back_ps[:, n, 0:NF], v, s["ident"][0:NF, 0:NF])
            ins.then_inc(carry_turned, 1)


def gate_steps(nc, dve, step, s, E_, score, better, count, gate, best, total):
    step(nc.vector.memset(count[:], 0.0))
    for j in range(E_):
        one = score[:, :, j:j + 1]
        if j:
            ins = nc.vector.tensor_tensor(better[:, :, 0:j], score[:, :, 0:j], one.to_broadcast([P, NT, j]), ALU.is_lt)
        if j < E_ - 1:
            ins = nc.vector.tensor_tensor(better[:, :, j + 1:E_], score[:, :, j + 1:E_],
                                          one.to_broadcast([P, NT, E_ - 1 - j]), ALU.is_le)
        step(ins)
        if j:
            ins = nc.vector.tensor_tensor(count[:, :, 0:j], count[:, :, 0:j], better[:, :, 0:j], ALU.add)
        if j < E_ - 1:
            ins = nc.vector.tensor_tensor(count[:, :, j + 1:E_], count[:, :, j + 1:E_], better[:, :, j + 1:E_], ALU.add)
        step(ins)
    step(nc.vector.tensor_reduce(best[:], score[:], AX.X, ALU.max))
    step(nc.vector.tensor_tensor(gate[:], score[:], best[:].rearrange("p (t o) -> p t o", o=1).to_broadcast([P, NT, E_]),
                                 ALU.subtract))


def gate_ends(nc, step, E_, count, gate, total):
    step(nc.vector.scalar_tensor_tensor(out=gate[:], in0=count[:], scalar=2.0, in1=gate[:], op0=ALU.is_lt, op1=ALU.mult))
    step(nc.vector.tensor_reduce(total[:], gate[:], AX.X, ALU.add))
    step(nc.vector.reciprocal(total[:], total[:]))
    step(nc.vector.tensor_tensor(gate[:], gate[:], total[:].rearrange("p (t o) -> p t o", o=1).to_broadcast([P, NT, E_]), ALU.mult))


def turn_gates_pe(nc, pe, s, gate, E_, gate_ps, gates_ready, bank_free, bank_ready):
    pe.sem_inc(bank_free, 2)
    pe.wait_ge(gates_ready, 1)
    for g in range(-(-NT // 4)):
        pe.wait_ge(bank_free, g + 1)
        for q in range(min(4, NT - 4 * g)):
            ins = nc.tensor.transpose(gate_ps[g % 2][0:E_, q * P:(q + 1) * P], gate[:, 4 * g + q, :], s["ident"][:])
        ins.then_inc(bank_ready, 1)


def turn_gates_act(nc, act, s, E_, gate_ps, bank_free, bank_ready):
    by_tile = s["gates"][0:E_, :].rearrange("e (p t) -> e t p", t=NT)
    for g in range(-(-NT // 4)):
        n = min(4, NT - 4 * g)
        act.wait_ge(bank_ready, g + 1)
        nc.scalar.copy(by_tile[:, 4 * g:4 * g + n, :],
                       gate_ps[g % 2][0:E_, 0:n * P].rearrange("e (t p) -> e t p", p=P)).then_inc(bank_free, 1)


def graph_gates(nc, shared, sums_dram, b_gat, ln_gamma, ln_beta):
    with ExitStack() as ctx:
        sb = lambda name, shape, dt=F32: ctx.enter_context(nc.sbuf_tensor(name, shape, dt))
        pb = lambda name, shape: ctx.enter_context(nc.psum_tensor(name, shape, F32))
        sem = lambda name: keep(shared, ctx.enter_context(nc.semaphore(name)))
        s = shared
        Q = H0 * C0
        ends = sb("g_ends", [P, NT], I32)
        got = sb("g_got", [P, NT, STW])
        rows = sb("g_rows", [P, 3, Q])
        agg = sb("g_agg", [P, NT, Q])
        sq = sb("g_sq", [P, NT, Q])
        den = sb("g_den", [P, NT, H0])
        mean = sb("g_mean", [P, NT])
        var = sb("g_var", [P, NT])
        score = sb("g_score", [P, NT, C0])
        better = sb("g_better", [P, NT, C0])
        count = sb("g_count", [P, NT, C0])
        gate = sb("g_gate", [P, NT, C0])
        gate_ps = [pb(f"g_ps{u}", [P, 512]) for u in range(2)]
        ends_in, got_in, rows_in = sem("g_ends_in"), pool_sem(nc, s, "g_got_in"), sem("g_rows_in")
        step_done, var_ready, rooted = sem("g_step"), sem("g_var_ready"), sem("g_rooted")
        raised, exp_done, gates_ready = sem("g_raised"), sem("g_exp_done"), sem("g_gates_ready")
        bank_free, bank_ready = sem("g_bank_free"), sem("g_bank_ready")
        block = ctx.enter_context(nc.Block())

        @block.sync
        def _(sp):
            sp.dma_start(ends[:], s["end_id"].rearrange("(p t) o -> p (t o)", p=P)).then_inc(ends_in, 16)
            for n, v in enumerate((b_gat, ln_gamma, ln_beta)):
                sp.dma_start(rows[:, n, :], v.to_broadcast([P, Q])).then_inc(rows_in, 16)

        @block.gpsimd
        def _(pool):
            pool.wait_ge(ends_in, 16)
            for t in range(NT):
                pool.indirect_dma_start(got[:, t, :], None, sums_dram,
                                        bass.IndirectOffsetOnAxis(ap=ends[:, t:t + 1], axis=0)).then_inc(got_in, 16)

        @block.vector
        def _(dve):
            steps = [0]

            def step(ins):
                steps[0] += 1
                ins.then_inc(step_done, 1)
                dve.wait_ge(step_done, steps[0])

            per_tile = lambda v: v.rearrange("p (o q) -> p o q", o=1).to_broadcast([P, NT, Q])
            per_node = lambda v: v[:].rearrange("p (t o) -> p t o", o=1).to_broadcast([P, NT, Q])
            dve.wait_ge(got_in, 16 * NT)
            dve.wait_ge(rows_in, 48)
            heads = got[:, :, 0:NF].rearrange("p t (k c) -> p t k c", c=HC)
            step(nc.vector.tensor_scalar(den[:], heads[:, :, :, C0], 1e-16, None, ALU.add))
            step(nc.vector.reciprocal(den[:], den[:]))
            for k in range(H0):
                ins = nc.vector.tensor_tensor(agg[:, :, k * C0:(k + 1) * C0], heads[:, :, k, 0:C0],
                                              den[:, :, k:k + 1].to_broadcast([P, NT, C0]), ALU.mult)
            step(ins)
            step(nc.vector.tensor_tensor(agg[:], agg[:], per_tile(rows[:, 0, :]), ALU.add))
            step(nc.vector.tensor_reduce(mean[:], agg[:], AX.X, ALU.add))
            step(nc.vector.tensor_scalar(mean[:], mean[:], 1.0 / Q, None, ALU.mult))
            step(nc.vector.tensor_tensor(agg[:], agg[:], per_node(mean), ALU.subtract))
            step(nc.vector.tensor_tensor(sq[:], agg[:], agg[:], ALU.mult))
            step(nc.vector.tensor_reduce(var[:], sq[:], AX.X, ALU.add))
            step(nc.vector.tensor_scalar(var[:], var[:], 1.0 / Q, EPS, ALU.mult, ALU.add))
            dve.sem_inc(var_ready, 1)
            dve.wait_ge(rooted, 1)
            step(nc.vector.reciprocal(var[:], var[:]))
            step(nc.vector.tensor_tensor(agg[:], agg[:], per_node(var), ALU.mult))
            step(nc.vector.tensor_tensor(agg[:], agg[:], per_tile(rows[:, 1, :]), ALU.mult))
            step(nc.vector.tensor_tensor(agg[:], agg[:], per_tile(rows[:, 2, :]), ALU.add))
            step(nc.vector.tensor_reduce(score[:], agg[:].rearrange("p t (k c) -> p t c k", c=C0), AX.X, ALU.add))
            step(nc.vector.tensor_scalar(score[:], score[:], 1.0 / H0, None, ALU.mult))
            gate_steps(nc, dve, step, s, C0, score, better, count, gate, mean, var)
            dve.sem_inc(raised, 1)
            dve.wait_ge(exp_done, 1)
            gate_ends(nc, step, C0, count, gate, var)
            dve.sem_inc(gates_ready, 1)

        @block.scalar
        def _(act):
            act.wait_ge(var_ready, 1)
            nc.scalar.activation(var[:], var[:], ACT.Sqrt).then_inc(rooted, 1)
            act.wait_ge(raised, 1)
            nc.scalar.activation(gate[:], gate[:], ACT.Exp).then_inc(exp_done, 1)
            turn_gates_act(nc, act, s, C0, gate_ps, bank_free, bank_ready)

        @block.tensor
        def _(pe):
            turn_gates_pe(nc, pe, s, gate, C0, gate_ps, gates_ready, bank_free, bank_ready)


def routed_gates(nc, shared, w_r, b_r):
    with ExitStack() as ctx:
        sb = lambda name, shape, dt=F32: ctx.enter_context(nc.sbuf_tensor(name, shape, dt))
        pb = lambda name, shape: ctx.enter_context(nc.psum_tensor(name, shape, F32))
        sem = lambda name: keep(shared, ctx.enter_context(nc.semaphore(name)))
        s = shared
        E_ = 8
        w = sb("r_w", [P, E_])
        bias = sb("r_b", [P, E_])
        score = sb("r_score", [P, NT, E_])
        better = sb("r_better", [P, NT, E_])
        count = sb("r_count", [P, NT, E_])
        gate = sb("r_gate", [P, NT, E_])
        best = sb("r_best", [P, NT])
        total = sb("r_total", [P, NT])
        score_ps = pb("r_score_ps", [P, 2, 512])
        gate_ps = [pb(f"r_ps{u}", [P, 512]) for u in range(2)]
        w_in, score_ready, step_done = sem("r_w_in"), sem("r_score_ready"), sem("r_step")
        raised, exp_done, gates_ready = sem("r_raised"), sem("r_exp_done"), sem("r_gates_ready")
        bank_free, bank_ready = sem("r_bank_free"), sem("r_bank_ready")
        block = ctx.enter_context(nc.Block())

        @block.sync
        def _(sp):
            sp.dma_start(w[:], w_r).then_inc(w_in, 16)
            sp.dma_start(bias[:], b_r.to_broadcast([P, E_])).then_inc(w_in, 16)

        @block.tensor
        def _(pe):
            pe.wait_ge(w_in, 32)
            by_tile = s["y"][:].rearrange("p (n t) -> p t n", t=NT)
            for t in range(NT):
                ins = nc.tensor.matmul(score_ps[:, t // 64, t % 64 * E_:t % 64 * E_ + E_], by_tile[:, t, :], w[:],
                                       start=True, stop=True)
            ins.then_inc(score_ready, 1)
            turn_gates_pe(nc, pe, s, gate, E_, gate_ps, gates_ready, bank_free, bank_ready)

        @block.scalar
        def _(act):
            act.wait_ge(raised, 1)
            nc.scalar.activation(gate[:], gate[:], ACT.Exp).then_inc(exp_done, 1)
            turn_gates_act(nc, act, s, E_, gate_ps, bank_free, bank_ready)

        @block.vector
        def _(dve):
            steps = [0]

            def step(ins):
                steps[0] += 1
                ins.then_inc(step_done, 1)
                dve.wait_ge(step_done, steps[0])

            dve.wait_ge(score_ready, 1)
            dve.wait_ge(w_in, 32)
            for g in range(2):
                n = min(64, NT - 64 * g)
                ins = nc.vector.tensor_tensor(score[:, 64 * g:64 * g + n, :],
                                              score_ps[:, g, 0:n * E_].rearrange("p (t e) -> p t e", e=E_),
                                              bias[:].rearrange("p (o e) -> p o e", o=1).to_broadcast([P, n, E_]), ALU.add)
            step(ins)
            gate_steps(nc, dve, step, s, E_, score, better, count, gate, best, total)
            dve.sem_inc(raised, 1)
            dve.wait_ge(exp_done, 1)
            gate_ends(nc, step, E_, count, gate, total)
            dve.sem_inc(gates_ready, 1)


def experts(nc, shared, name, E_, w1_d, b1_d, w2_d, b2_d, out):
    with ExitStack() as ctx:
        sb = lambda what, shape, dt=F32: ctx.enter_context(nc.sbuf_tensor(f"{name}_{what}", shape, dt))
        pb = lambda what, shape: ctx.enter_context(nc.psum_tensor(f"{name}_{what}", shape, F32))
        sem = lambda what: keep(shared, ctx.enter_context(nc.semaphore(f"{name}_{what}")))
        s = shared
        x, y, gates = s["x"], s["y"], s["gates"]
        w1 = sb("w1", [P, E_, HID])
        b1 = sb("b1", [P, E_, 2])
        w2 = sb("w2", [P, E_, 2, D])
        b2 = sb("b2", [E_, D])
        hid = [sb(f"hid{u}", [P, 2, UB]) for u in range(2)]
        up_ps = [pb(f"up{u}", [P, 2, 512]) for u in range(2)]
        gate_ps = [pb(f"gate{u}", [P, 512]) for u in range(2)]
        acc = [pb(f"acc{u}", [P, 512]) for u in range(2)]
        held = sem("held")
        w_in = sem("w_in")
        up_ready, up_free, gate_free = sem("up_ready"), sem("up_free"), sem("gate_free")
        hid_ready, hid_scaled, hid_free = sem("hid_ready"), sem("hid_scaled"), sem("hid_free")
        acc_ready, acc_free, stored = sem("acc_ready"), sem("acc_free"), sem("stored")
        block = ctx.enter_context(nc.Block())
        at = lambda t, b: t[:, bass.ds(b * UB, UB)]

        @block.sync
        def _(sp):
            sp.dma_start(w1[:].rearrange("p e h -> p (e h)"), w1_d).then_inc(w_in, 16)
            sp.dma_start(b1[:].rearrange("p e h -> p (e h)"), b1_d).then_inc(w_in, 16)
            sp.dma_start(w2[:].rearrange("p e h d -> p (e h d)"), w2_d).then_inc(w_in, 16)
            sp.dma_start(b2[:], b2_d).then_inc(w_in, 16)
            if out is not None:
                with sp.Fori(0, NUB) as b:
                    sp.wait_ge(acc_free, b + 3)
                    sp.dma_start(out[:, bass.ds(b * UB, UB)], at(x, b)).then_inc(stored, 16)
                sp.wait_ge(stored, 16 * NUB)

        @block.tensor
        def _(pe):
            pe.wait_ge(w_in, 64)
            pe.sem_inc(up_free, 2)
            pe.sem_inc(gate_free, 2)
            pe.sem_inc(acc_free, 2)

            def up(b, e, n):
                pe.wait_ge(up_free, n + 1)
                pe.wait_ge(gate_free, n + 1)
                for h in range(2):
                    nc.tensor.matmul(up_ps[e % 2][:, h, 0:UB], w1[:, e, h * P:(h + 1) * P], at(y, b), start=True, stop=True)
                nc.tensor.matmul(gate_ps[e % 2][:, 0:UB], s["ident"][0:E_, e:e + 1].to_broadcast([E_, P]),
                                 at(gates[0:E_, :], b), start=True, stop=True).then_inc(up_ready, 1)

            def down(u, b, e, n):
                pe.wait_ge(hid_scaled, n + 1)
                for h in range(2):
                    ins = nc.tensor.matmul(acc[u][:, 0:UB], w2[:, e, h, :], hid[e % 2][:, h, :],
                                           start=(e == 0 and h == 0), stop=False)
                ins.then_inc(hid_free, 1)

            with pe.Fori(0, NUB // 2) as i:
                for u in range(2):
                    b = 2 * i + u
                    up(b, 0, b * E_)
                    pe.wait_ge(acc_free, b + 1)
                    for e in range(E_):
                        if e < E_ - 1:
                            up(b, e + 1, b * E_ + (e + 1))
                        down(u, b, e, b * E_ + e)
                    nc.tensor.matmul(acc[u][:, 0:UB], b2[:], at(gates[0:E_, :], b), start=False, stop=True).then_inc(acc_ready, 1)

        @block.scalar
        def _(act):
            act.wait_ge(w_in, 64)
            act.sem_inc(hid_free, 2)
            with act.Fori(0, NUB) as b:
                for e in range(E_):
                    n = b * E_ + e
                    act.wait_ge(up_ready, n + 1)
                    act.wait_ge(hid_free, n + 1)
                    for h in range(2):
                        ins = nc.scalar.activation(hid[e % 2][:, h, :], up_ps[e % 2][:, h, 0:UB], ACT.Gelu, bias=b1[:, e, h:h + 1])
                    ins.then_inc(hid_ready, 1)
                    act.wait_ge(hid_ready, n + 1)
                    act.sem_inc(up_free, 1)

        @block.vector
        def _(dve):
            with dve.Fori(0, NUB // 2) as i:
                for u in range(2):
                    b = 2 * i + u
                    for e in range(E_):
                        n = b * E_ + e
                        dve.wait_ge(hid_ready, n + 1)
                        for h in range(2):
                            ins = nc.vector.tensor_tensor(hid[e % 2][:, h, :], hid[e % 2][:, h, :], gate_ps[e % 2][:, 0:UB], ALU.mult)
                        ins.then_inc(hid_scaled, 1)
                        dve.wait_ge(hid_scaled, n + 1)
                        dve.sem_inc(gate_free, 1)
                    dve.wait_ge(acc_ready, b + 1)
                    nc.vector.tensor_tensor(at(x, b), at(x, b), acc[u][:, 0:UB], ALU.add).then_inc(acc_free, 1)


def second_pass(nc, shared, adj_t, w_msg, b_msg):
    with ExitStack() as ctx:
        sb = lambda name, shape, dt=F32: ctx.enter_context(nc.sbuf_tensor(name, shape, dt))
        pb = lambda name, shape: ctx.enter_context(nc.psum_tensor(name, shape, F32))
        sem = lambda name: keep(shared, ctx.enter_context(nc.semaphore(name)))
        s = shared
        x, y = s["x"], s["y"]
        w = sb("m_w", [P, D])
        b_row = sb("m_b", [1, D])
        msg = sb("m_msg", [P, NT, D])
        adj = sb("m_adj", [P, NBUF, CT * UB])
        inv = [y[:, u * CT * UB:(u + 1) * CT * UB] for u in range(2)]
        msg_ps = [pb(f"m_msg_ps{u}", [P, 512]) for u in range(2)]
        acc = pb("m_acc", [P, 512])
        w_in = sem("m_w_in")
        msg_free, msg_ready = sem("m_msg_free"), sem("m_msg_ready")
        adj_in = [sem(f"m_adj_in{n}") for n in range(NBUF)]
        adj_used, acc_free, acc_ready = sem("m_adj_used"), sem("m_acc_free"), sem("m_acc_ready")
        logged, inverted, squared, raised, weighted = (sem("m_logged"), sem("m_inverted"), sem("m_squared"),
                                                       sem("m_raised"), sem("m_weighted"))
        block = ctx.enter_context(nc.Block())
        width = lambda c: min(CT, NT - c * CT) * UB

        @block.sync
        def _(sp):
            sp.dma_start(w[:], w_msg).then_inc(w_in, 16)
            sp.dma_start(b_row[:], b_msg).then_inc(w_in, 16)

            def load(ub, c):
                n = width(c)
                sp.dma_start(adj[:, c % NBUF, 0:n], adj_t[ub, :, c * CT * UB:c * CT * UB + n] if isinstance(ub, int) else
                             adj_t[bass.ds(ub, 1), :, c * CT * UB:c * CT * UB + n].rearrange("o p n -> (o p) n")
                             ).then_inc(adj_in[c % NBUF], 16)
            for c in range(NCH):
                if c >= NBUF:
                    sp.wait_ge(adj_used, c - NBUF + 1)
                load(0, c)
            with sp.Fori(1, NUB) as ub:
                for c in range(NCH):
                    sp.wait_ge(adj_used, NCH * ub + (c - NBUF + 1))
                    load(ub, c)

        @block.tensor
        def _(pe):
            pe.wait_ge(w_in, 32)
            pe.sem_inc(msg_free, 2)
            pe.sem_inc(acc_free, 1)
            for t in range(NT):
                g, q = divmod(t, 4)
                if q == 0:
                    pe.wait_ge(msg_free, g + 1)
                nc.tensor.matmul(msg_ps[g % 2][:, q * D:(q + 1) * D], y[:, t * P:(t + 1) * P], w[:], start=True, stop=False)
                ins = nc.tensor.matmul(msg_ps[g % 2][:, q * D:(q + 1) * D], s["ones"][0:1, :], b_row[:], start=False, stop=True)
                if q == 3 or t == NT - 1:
                    ins.then_inc(msg_ready, 1)
            pe.wait_ge(msg_free, -(-NT // 4) + 2)
            with pe.Fori(0, NUB) as ub:
                pe.wait_ge(acc_free, ub + 1)
                for c in range(NCH):
                    pe.wait_ge(weighted, NCH * ub + (c + 2))
                    for k in range(min(CT, NT - c * CT)):
                        ins = nc.tensor.matmul(acc[:, 0:UB], msg[:, c * CT + k, :], adj[:, c % NBUF, k * UB:(k + 1) * UB],
                                               start=(c == 0 and k == 0), stop=(c * CT + k == NT - 1))
                    ins.then_inc(adj_used, 1)
                pe.wait_ge(adj_used, NCH * ub + NCH)
                pe.sem_inc(acc_ready, 1)

        @block.scalar
        def _(act):
            for g in range(-(-NT // 4)):
                n = min(4, NT - 4 * g)
                act.wait_ge(msg_ready, g + 1)
                nc.scalar.copy(msg[:, 4 * g:4 * g + n, :].rearrange("p t d -> p (t d)"), msg_ps[g % 2][:, 0:n * D]).then_inc(msg_free, 1)
            act.wait_ge(msg_free, -(-NT // 4) + 2)

            def invert(ub, c, at_least):
                n, v = width(c), inv[c % 2]
                act.wait_ge(adj_in[c % NBUF], 32 * ub + 16 * (c // NBUF + 1))
                if at_least is not None:
                    act.wait_ge(weighted, at_least + 1)
                nc.scalar.activation(v[:, 0:n], adj[:, c % NBUF, 0:n], ACT.Ln, bias=s["tiny"][:, 0:1]).then_inc(logged, 1)
                act.wait_ge(logged, NCH * ub + (c + 1))
                nc.scalar.activation(v[:, 0:n], v[:, 0:n], ACT.Exp, scale=-1.0).then_inc(inverted, 1)

            def raise_(ub, c):
                n, v = width(c), inv[c % 2]
                act.wait_ge(squared, NCH * ub + (c + 1))
                nc.scalar.activation(v[:, 0:n], v[:, 0:n], ACT.Exp, bias=s["minus2"][:, 0:1], scale=-2.0).then_inc(raised, 1)

            nc.scalar.preload_act_table_set("natural_log_exp_and_others")
            invert(0, 0, None)
            with act.Fori(0, NUB - 1) as ub:
                nc.scalar.preload_act_table_set("natural_log_exp_and_others")
                for c in range(NCH):
                    if c < NCH - 1:
                        invert(ub, c + 1, NCH * ub + c if c else NCH * ub)
                    else:
                        invert(ub + 1, 0, NCH * ub + c)
                    raise_(ub, c)
            ub = NUB - 1
            for c in range(NCH):
                if c < NCH - 1:
                    invert(ub, c + 1, NCH * ub + c)
                raise_(ub, c)

        @block.vector
        def _(dve):
            def square(ub, c):
                n, v = width(c), inv[c % 2]
                dve.wait_ge(inverted, NCH * ub + (c + 1))
                nc.vector.scalar_tensor_tensor(out=v[:, 0:n], in0=v[:, 0:n], scalar=-2.0, in1=v[:, 0:n],
                                               op0=ALU.add, op1=ALU.mult).then_inc(squared, 1)

            def weigh(ub, c):
                n, v = width(c), inv[c % 2]
                dve.wait_ge(raised, NCH * ub + (c + 1))
                r = adj[:, c % NBUF, 0:n]
                nc.vector.scalar_tensor_tensor(out=r, in0=r, scalar=1.0, in1=v[:, 0:n], op0=ALU.is_lt, op1=ALU.mult).then_inc(weighted, 1)

            def gather(ub):
                dve.wait_ge(acc_ready, ub + 1)
                nc.vector.tensor_tensor(x[:, bass.ds(ub * UB, UB)], x[:, bass.ds(ub * UB, UB)], acc[:, 0:UB], ALU.add).then_inc(acc_free, 1)

            dve.sem_inc(weighted, 1)
            square(0, 0)
            with dve.Fori(0, NUB - 1) as ub:
                for c in range(NCH):
                    if c < NCH - 1:
                        square(ub, c + 1)
                    else:
                        square(ub + 1, 0)
                    weigh(ub, c)
                gather(ub)
            ub = NUB - 1
            for c in range(NCH):
                if c < NCH - 1:
                    square(ub, c + 1)
                weigh(ub, c)
            gather(ub)


def layer_kernel(nc, a, out, stop=99):
    with ExitStack() as ctx:
        dram = lambda name, shape, dt=F32: nc.dram_tensor(name, shape, dt).ap()
        y0_dram = dram("d_y0", [P, N])
        r_dram = dram("d_r", [P, N])
        keys_dram = dram("d_keys", [2 * E], I32)
        rows_dram = dram("d_rows", [P, RMAX + CH], I32)
        sums_dram = dram("d_sums", [P * RMAX, STW])
        sb = lambda name, shape, dt=F32: ctx.enter_context(nc.sbuf_tensor(name, shape, dt))
        shared = {
            "used_sems": [], "stack": ctx,
            "mean_w": sb("mean_w", [P, P]), "ones": sb("ones", [P, P]), "ident": sb("ident", [P, P]),
            "sign": sb("sign", [P, LOGP]), "eps": sb("eps", [P, 1]), "zero": sb("zero", [P, 1]),
            "tiny": sb("tiny", [P, 1]), "minus2": sb("minus2", [P, 1]),
            "chunks": sb("chunks", [P, 1], I32), "row_first": sb("row_first", [P, 1], I32),
            "end_id": dram("d_end_id", [NPAD, 1], I32),
        }
        with ExitStack() as early:
            shared["keys"] = early.enter_context(nc.sbuf_tensor("keys", [P, 4, ROW], I32))
            shared["h"] = early.enter_context(nc.sbuf_tensor("h_items", [P, NT, D], F32))
            prepare(nc, shared, a["x_t"], a["item_t"], a["edges"], a["w_item_t"], a["b_item"], y0_dram)
            if stop >= 1:
                first_pass(nc, shared, a["adj_t"], a["w_user_t"], a["b_user"], y0_dram, r_dram, keys_dram, rows_dram, sums_dram)
        if stop < 2:
            return
        shared["x_in"] = a["x_t"]
        shared["x"] = sb("x", [P, N])
        shared["y"] = sb("y", [P, NPAD])
        shared["table"] = dram("d_table", [NPAD, TABW])
        layernorm(nc, shared, "ln1", add=r_dram)
        node_table(nc, shared, a["w_gat"], a["att_src"], a["att_dst"])
        attend(nc, shared, rows_dram, sums_dram)
        clear_semaphores(nc, shared)
        if stop < 3:
            return
        with ExitStack() as late:
            shared["gates"] = late.enter_context(nc.sbuf_tensor("gates0", [8, NPAD], F32))
            graph_gates(nc, shared, sums_dram, a["b_gat"], a["ln_gamma"], a["ln_beta"])
            experts(nc, shared, "e0", 4, a["w1_0"], a["b1_0"], a["w2_0"], a["b2_0"], None)
        layernorm(nc, shared, "ln2")
        if stop < 4:
            return
        second_pass(nc, shared, a["adj_t"], a["w_msg"], a["b_msg"])
        layernorm(nc, shared, "ln3", gamma=a["gamma"], beta=a["beta"])
        with ExitStack() as late:
            shared["gates"] = late.enter_context(nc.sbuf_tensor("gates1", [8, NPAD], F32))
            routed_gates(nc, shared, a["w_r"], a["b_r"])
            experts(nc, shared, "e1", 8, a["w1_1"], a["b1_1"], a["w2_1"], a["b2_1"], out)


def lay_out(x, adj, L0_gnn_item_feat, L0_gnn_W_item, L0_gnn_b_item, L0_gnn_W_user, L0_gnn_b_user,
            L0_ffn_W_gat, L0_ffn_att_src, L0_ffn_att_dst, L0_ffn_b_gat, L0_ffn_ln_gamma, L0_ffn_ln_beta,
            L0_ffn_W1, L0_ffn_b1, L0_ffn_W2, L0_ffn_b2, L0_ffn_edge_index, L1_gnn_W, L1_gnn_B,
            L1_ffn_gamma, L1_ffn_beta, L1_ffn_Wr, L1_ffn_br, L1_ffn_W1, L1_ffn_b1, L1_ffn_W2, L1_ffn_b2):
    import numpy as np
    c = np.ascontiguousarray
    padded = np.zeros((NUB, UB, NT * P), adj.dtype)
    padded[:, :, :N] = np.asarray(adj).reshape(NUB, UB, N)
    adj_t = c(padded.reshape(NUB, UB, NT, P).transpose(0, 3, 2, 1)).reshape(NUB, P, NT * UB)
    item_t = np.zeros((D, NPAD), np.asarray(x).dtype)
    item_t[:, :N] = np.asarray(L0_gnn_item_feat).T
    col = lambda v: c(np.asarray(v).reshape(-1, 1))
    row = lambda v: c(np.asarray(v).reshape(1, -1))
    w1 = lambda w: c(np.asarray(w).transpose(1, 0, 2)).reshape(D, -1)
    w2 = lambda w: c(np.asarray(w).reshape(w.shape[0], 2, P, D).transpose(2, 0, 1, 3)).reshape(P, -1)
    b1 = lambda b: c(np.asarray(b).reshape(-1, P).T)
    return {
        "x_t": c(np.asarray(x).T), "adj_t": adj_t, "item_t": item_t,
        "w_item_t": c(np.asarray(L0_gnn_W_item).T), "b_item": row(L0_gnn_b_item),
        "w_user_t": c(np.asarray(L0_gnn_W_user).T), "b_user": col(L0_gnn_b_user),
        "edges": c(np.asarray(L0_ffn_edge_index)),
        "w_gat": c(np.asarray(L0_ffn_W_gat)), "att_src": row(L0_ffn_att_src), "att_dst": row(L0_ffn_att_dst),
        "b_gat": row(L0_ffn_b_gat), "ln_gamma": row(L0_ffn_ln_gamma), "ln_beta": row(L0_ffn_ln_beta),
        "w1_0": w1(L0_ffn_W1), "b1_0": b1(L0_ffn_b1), "w2_0": w2(L0_ffn_W2), "b2_0": c(np.asarray(L0_ffn_b2)),
        "w_msg": c(np.asarray(L1_gnn_W)), "b_msg": row(L1_gnn_B),
        "gamma": col(L1_ffn_gamma), "beta": col(L1_ffn_beta), "w_r": c(np.asarray(L1_ffn_Wr)), "b_r": row(L1_ffn_br),
        "w1_1": w1(L1_ffn_W1), "b1_1": b1(L1_ffn_b1), "w2_1": w2(L1_ffn_W2), "b2_1": c(np.asarray(L1_ffn_b2)),
    }


def kernel(**inputs):
    import numpy as np
    import concourse.bacc as bacc
    from concourse.bass_utils import run_bass_kernel_spmd

    arrays = lay_out(**inputs)
    nc = bacc.Bacc("TRN2", target_bir_lowering=False, num_devices=1)
    aps = {k: nc.dram_tensor(k, v.shape, mybir.dt.from_np(v.dtype), kind="ExternalInput").ap() for k, v in arrays.items()}
    out = nc.dram_tensor("out_t", (D, N), F32, kind="ExternalOutput").ap()
    layer_kernel(nc, aps, out)
    result = run_bass_kernel_spmd(nc, [arrays], core_ids=[0])
    return np.ascontiguousarray(result.results[0]["out_t"].T)
```

```python
import concourse.bass as bass
from concourse import mybir
from contextlib import ExitStack

F32 = mybir.dt.float32
I32 = mybir.dt.int32
BF16 = mybir.dt.bfloat16
ALU = mybir.AluOpType
ACT = mybir.ActivationFunctionType
AX = mybir.AxisListType

P = 128
N = 10000
D = 128
EPS = 1e-5

UB = 500
NUB = N // UB
NT = -(-N // P)
NPAD = NT * P
CT = 8
NCH = -(-NT // CT)
BEFORE = 3
NBUF = 5

MT = 5
MCH = -(-NT // MT)
MBUF = 8
NINV = 4
AHEAD = 2

E = 524288
ROW = E // P
LOGP, LOGR = 7, 12
DST_SHIFT = 14
FIELD = (1 << DST_SHIFT) - 1
APART = 1 << DST_SHIFT
DST_FIELD = 2 * APART - 1
KEY_BASE = 0x20000000
LO = 7
CH = 128
HF = CH // 2
CHMAX = (E + N) // (P * CH) + 1
RMAX = CHMAX * CH
BIG = 1 << 20
NEG = -1e30

H0, C0 = 4, 4
HC = C0 + 1
NF = H0 * HC
TABW = NF + 2 * H0
STW = NF + H0
HID = 256
HOT = 16
BLANK = RMAX * STW // 48


def keep(shared, sem):
    shared["used_sems"].append(sem)
    return sem


def pool_sem(nc, shared, name):
    return shared["stack"].enter_context(nc.semaphore(name))


def clear_semaphores(nc, shared):
    with nc.Block() as block:
        @block.gpsimd
        def _(pool):
            for sem in shared["used_sems"]:
                pool.sem_clear(sem)
    shared["used_sems"] = []


def hold(eng, sem, value, passed):
    eng.wait_ge(sem, value)
    eng.sem_inc(passed, 1)


def stage_views(buf, b, k, width):
    if k is None:
        v = buf.rearrange("p (a two d) -> p a two d", two=2, d=1 << b)
        yield v[:, :, 0, :], v[:, :, 1, :], True
    elif k > b:
        v = buf.rearrange("p (a dir c two d) -> p a dir c two d", dir=2, c=1 << (k - 1 - b), two=2, d=1 << b)
        for way in range(2):
            yield v[:, :, way, :, 0, :], v[:, :, way, :, 1, :], way == 0
    else:
        v = buf.rearrange("p (a two c dir d) -> p a two c dir d", two=2, c=1 << (b - 1 - k), dir=2, d=1 << k)
        for way in range(2):
            yield v[:, :, 0, :, way, :], v[:, :, 1, :, way, :], way == 0


def prepare(nc, shared, x_t, item_t, edges, w_item_t, b_item, y0_dram):
    with ExitStack() as ctx:
        sb = lambda name, shape, dt=F32: ctx.enter_context(nc.sbuf_tensor(name, shape, dt))
        pb = lambda name, shape: ctx.enter_context(nc.psum_tensor(name, shape, F32))
        sem = lambda name: keep(shared, ctx.enter_context(nc.semaphore(name)))
        s = shared
        xc = sb("p_xc", [P, N])
        sq = sb("p_sq", [P, N])
        item = sb("p_item", [P, 2, CT * P])
        w_item = sb("p_w_item", [P, D])
        b_row = sb("p_b_item", [1, D])
        flag = sb("p_flag", [P, 512])
        count = sb("p_count", [P, 16])
        total_i = sb("p_total_i", [P, 1], I32)
        part_i = sb("p_part_i", [P, 1], I32)
        totals = sb("p_totals", [P, 4])
        bits = sb("p_bits", [P, LOGP], I32)
        zero_ids = sb("p_zero_ids", [1, NPAD - N], I32)
        mean_ps = [pb(f"p_mean{u}", [P, 512]) for u in range(2)]
        var_ps = [pb(f"p_var{u}", [P, 512]) for u in range(2)]
        h_ps = [pb(f"p_h{u}", [P, 512]) for u in range(2)]
        tot_ps = pb("p_tot", [P, 512])

        weights_in = sem("p_weights_in")
        x_in = sem("p_x_in")
        item_in = [sem(f"p_item_in{u}") for u in range(2)]
        item_used = sem("p_item_used")
        src_in = sem("p_src_in")
        dst_in = sem("p_dst_in")
        consts = sem("p_consts")
        ident_zero = sem("p_ident_zero")
        loops_made = sem("p_loops_made")
        mean_free, mean_ready = sem("p_mean_free"), sem("p_mean_ready")
        centred, squared = sem("p_centred"), sem("p_squared")
        var_free, var_ready = sem("p_var_free"), sem("p_var_ready")
        logged, rstd_ready = sem("p_logged"), sem("p_rstd_ready")
        normed, y_stored = sem("p_normed"), sem("p_y_stored")
        h_free, h_ready = sem("p_h_free"), sem("p_h_ready")
        key_step = sem("p_key_step")
        counted, total_ready = sem("p_counted"), sem("p_total_ready")
        held = sem("p_held")
        zeroed, ids_stored = sem("p_zeroed"), sem("p_ids_stored")
        block = ctx.enter_context(nc.Block())

        @block.sync
        def _(sp):
            sp.dma_start(w_item[:], w_item_t).then_inc(weights_in, 16)
            sp.dma_start(b_row[:], b_item).then_inc(weights_in, 16)
            sp.dma_start(xc[:], x_t).then_inc(x_in, 16)
            sp.dma_start(s["keys"][:, 1, :], edges[0].rearrange("(p j) -> p j", p=P)).then_inc(src_in, 16)
            sp.dma_start(s["keys"][:, 0, :], edges[1].rearrange("(p j) -> p j", p=P)).then_inc(dst_in, 16)
            for c in range(NCH):
                if c >= 2:
                    sp.wait_ge(item_used, c - 1)
                w = min(CT * P, NPAD - c * CT * P)
                sp.dma_start(item[:, c % 2, 0:w], item_t[:, c * CT * P:c * CT * P + w]).then_inc(item_in[c % 2], 16)
            with sp.Fori(0, NUB // 4) as i:
                sp.wait_ge(normed, 4 * i + 4)
                sp.dma_start(y0_dram[:, bass.ds(i * (4 * UB), 4 * UB)],
                             xc[:, bass.ds(i * (4 * UB), 4 * UB)]).then_inc(y_stored, 16)
            sp.wait_ge(zeroed, 1)
            sp.dma_start(s["end_id"][N:NPAD, :].rearrange("n o -> o n"), zero_ids[:]).then_inc(ids_stored, 16)
            sp.wait_ge(ids_stored, 16)
            sp.wait_ge(y_stored, 16 * (NUB // 4))

        @block.gpsimd
        def _(pool):
            nc.gpsimd.iota(s["keys"][:, 3, :], [[-1, ROW]], base=P * ROW - 1, channel_multiplier=-ROW).then_inc(loops_made, 1)
            nc.gpsimd.memset(s["mean_w"][:], 1.0 / D)
            nc.gpsimd.memset(s["ones"][:], 1.0)
            nc.gpsimd.memset(s["eps"][:], EPS)
            nc.gpsimd.memset(s["zero"][:], 0.0)
            nc.gpsimd.memset(s["tiny"][:], 1e-18)
            nc.gpsimd.memset(s["minus2"][:], -2.0)
            nc.gpsimd.memset(zero_ids[:], 0).then_inc(zeroed, 1)
            nc.gpsimd.iota(part_i[:], [[0, 1]], base=0, channel_multiplier=1)
            nc.gpsimd.memset(s["ident"][:], 0.0).then_inc(ident_zero, 1)
            pool.wait_ge(ident_zero, 1)
            nc.gpsimd.affine_select(out=s["ident"][:], in_=s["ident"][:], compare_op=ALU.not_equal, fill=1.0,
                                    base=0, pattern=[[-1, P]], channel_multiplier=1).then_inc(consts, 1)

        @block.tensor
        def _(pe):
            pe.wait_ge(consts, 1)
            pe.wait_ge(x_in, 16)
            pe.sem_inc(mean_free, 2)
            pe.sem_inc(var_free, 2)
            pe.sem_inc(h_free, 2)
            with pe.Fori(0, NUB // 2) as i:
                for u in range(2):
                    pe.wait_ge(mean_free, 2 * i + u + 1)
                    nc.tensor.matmul(mean_ps[u][:, 0:UB], s["mean_w"][:], xc[:, bass.ds((2 * i + u) * UB, UB)],
                                     start=True, stop=True).then_inc(mean_ready, 1)
            with pe.Fori(0, NUB // 2) as i:
                for u in range(2):
                    pe.wait_ge(var_free, 2 * i + u + 1)
                    pe.wait_ge(squared, 2 * i + u + 1)
                    nc.tensor.matmul(var_ps[u][:, 0:UB], s["mean_w"][:], sq[:, bass.ds((2 * i + u) * UB, UB)],
                                     start=True, stop=True).then_inc(var_ready, 1)
            pe.wait_ge(counted, 1)
            nc.tensor.matmul(tot_ps[:, 0:2], s["ones"][:], count[:, 8:10], start=True, stop=True).then_inc(total_ready, 1)
            pe.wait_ge(weights_in, 32)
            for t in range(NT):
                c, k = divmod(t, CT)
                if k == 0:
                    pe.wait_ge(item_in[c % 2], 16 * (c // 2 + 1))
                g, q = divmod(t, 4)
                if q == 0:
                    pe.wait_ge(h_free, g + 1)
                nc.tensor.matmul(h_ps[g % 2][:, q * D:(q + 1) * D], item[:, c % 2, k * P:(k + 1) * P], w_item[:],
                                 start=True, stop=False)
                last = nc.tensor.matmul(h_ps[g % 2][:, q * D:(q + 1) * D], s["ones"][0:1, :], b_row[:],
                                        start=False, stop=True)
                if k == CT - 1 or t == NT - 1:
                    last.then_inc(item_used, 1)
                elif q == 3:
                    last.then_inc(h_ready, 1)
                if (q == 3 or t == NT - 1) and (k == CT - 1 or t == NT - 1):
                    pe.wait_ge(item_used, c + 1)
                    pe.sem_inc(h_ready, 1)

        @block.scalar
        def _(act):
            with act.Fori(0, NUB) as b:
                hold(act, centred, b + 1, held)
                nc.scalar.activation(sq[:, bass.ds(b * UB, UB)], xc[:, bass.ds(b * UB, UB)], ACT.Square).then_inc(squared, 1)
            with act.Fori(0, NUB // 2) as i:
                nc.scalar.preload_act_table_set("natural_log_exp_and_others")
                for u in range(2):
                    hold(act, var_ready, 2 * i + u + 1, held)
                    nc.scalar.activation(sq[:, bass.ds((2 * i + u) * UB, UB)], var_ps[u][:, 0:UB], ACT.Ln,
                                         bias=s["eps"][:, 0:1]).then_inc(var_free, 1)
                    hold(act, var_free, 2 * i + u + 3, held)
                    nc.scalar.activation(sq[:, bass.ds((2 * i + u) * UB, UB)], sq[:, bass.ds((2 * i + u) * UB, UB)],
                                         ACT.Exp, scale=-0.5).then_inc(rstd_ready, 1)
            for g in range(-(-NT // 4)):
                act.wait_ge(h_ready, g + 1)
                w = min(4, NT - 4 * g)
                nc.scalar.copy(s["h"][:, 4 * g:4 * g + w, :].rearrange("p t d -> p (t d)"),
                               h_ps[g % 2][:, 0:w * D]).then_inc(h_free, 1)

        @block.vector
        def _(dve):
            with dve.Fori(0, NUB // 2) as i:
                for u in range(2):
                    dve.wait_ge(mean_ready, 2 * i + u + 1)
                    nc.vector.tensor_tensor(xc[:, bass.ds((2 * i + u) * UB, UB)], xc[:, bass.ds((2 * i + u) * UB, UB)],
                                            mean_ps[u][:, 0:UB], ALU.subtract).then_inc(centred, 1)
                    dve.wait_ge(centred, 2 * i + u + 1)
                    dve.sem_inc(mean_free, 1)
            with dve.Fori(0, NUB) as b:
                dve.wait_ge(rstd_ready, b + 1)
                nc.vector.tensor_tensor(xc[:, bass.ds(b * UB, UB)], xc[:, bass.ds(b * UB, UB)],
                                        sq[:, bass.ds(b * UB, UB)], ALU.mult).then_inc(normed, 1)

            steps = [0]

            def step(ins):
                steps[0] += 1
                ins.then_inc(key_step, 1)
                dve.wait_ge(key_step, steps[0])

            src, dst, flags, loops = (s["keys"][:, n, :] for n in range(4))
            src, dst = s["keys"][:, 1, :], s["keys"][:, 0, :]
            flags = s["keys"][:, 2, :].bitcast(F32)
            dve.wait_ge(dst_in, 16)
            step(nc.vector.tensor_scalar(flags, dst, float(N), None, ALU.is_lt))
            step(nc.vector.tensor_reduce(count[:, 8:9], flags, AX.X, ALU.add))
            dve.wait_ge(src_in, 16)
            step(nc.vector.scalar_tensor_tensor(out=flags, in0=src, scalar=float(N - 1), in1=flags, op0=ALU.is_lt, op1=ALU.mult))
            step(nc.vector.tensor_reduce(count[:, 9:10], flags, AX.X, ALU.add))
            dve.sem_inc(counted, 1)
            apart = s["keys"][:, 2, :]
            step(nc.vector.tensor_scalar(apart, flags, -float(APART), float(APART), ALU.mult, ALU.add))
            step(nc.vector.tensor_scalar(dst, dst, FIELD, None, ALU.min))
            step(nc.vector.tensor_scalar(src, src, N - 1, 1, ALU.min, ALU.add))
            step(nc.vector.tensor_tensor(dst, dst, apart, ALU.bitwise_or))
            step(nc.vector.tensor_scalar(dst, dst, DST_SHIFT, KEY_BASE, ALU.logical_shift_left, ALU.bitwise_or))
            step(nc.vector.tensor_tensor(dst, dst, src, ALU.bitwise_or))
            dve.wait_ge(loops_made, 1)
            step(nc.vector.tensor_scalar(apart, loops, float(N), float(DST_FIELD), ALU.is_ge, ALU.mult))
            step(nc.vector.scalar_tensor_tensor(out=loops, in0=loops, scalar=float(DST_FIELD), in1=apart, op0=ALU.min, op1=ALU.max))
            step(nc.vector.tensor_scalar(loops, loops, DST_SHIFT, KEY_BASE, ALU.logical_shift_left, ALU.bitwise_or))
            dve.wait_ge(total_ready, 1)
            step(nc.vector.tensor_copy(totals[:, 0:2], tot_ps[:, 0:2]))
            step(nc.vector.tensor_scalar(total_i[:], totals[:, 1:2], float(N), None, ALU.add))
            step(nc.vector.tensor_scalar(s["apart_first"][:], total_i[:], 7, None, ALU.logical_shift_right))
            step(nc.vector.tensor_scalar(total_i[:], total_i[:], 14, None, ALU.logical_shift_right))
            step(nc.vector.tensor_scalar(s["chunks"][:], total_i[:], 1, None, ALU.add))
            step(nc.vector.tensor_tensor(totals[:, 0:1], totals[:, 0:1], totals[:, 1:2], ALU.subtract))
            step(nc.vector.tensor_scalar(total_i[:], totals[:, 0:1], float(P), None, ALU.add))
            step(nc.vector.tensor_scalar(total_i[:], total_i[:], 14, None, ALU.logical_shift_right))
            step(nc.vector.tensor_scalar(totals[:, 0:1], total_i[:], 1.0, None, ALU.add))
            step(nc.vector.tensor_copy(totals[:, 1:2], s["chunks"][:]))
            step(nc.vector.reciprocal(totals[:, 2:3], totals[:, 1:2]))
            step(nc.vector.tensor_tensor(total_i[:], totals[:, 0:1], totals[:, 2:3], ALU.mult))
            step(nc.vector.tensor_scalar(s["apart_each"][:], total_i[:], 1, None, ALU.add))
            step(nc.vector.tensor_tensor(s["apart_all"][:], s["apart_each"][:], s["chunks"][:], ALU.mult))
            dve.wait_ge(consts, 1)
            step(nc.vector.tensor_tensor(s["row_first"][:], part_i[:], s["chunks"][:], ALU.mult))
            for r in range(LOGP):
                step(nc.vector.tensor_scalar(bits[:, r:r + 1], part_i[:], r, 1, ALU.logical_shift_right, ALU.bitwise_and))
            step(nc.vector.tensor_scalar(s["sign"][:], bits[:], -2.0, 1.0, ALU.mult, ALU.add))


def first_pass(nc, shared, adj_t, w_user_t, b_user, y0_dram, r_dram, keys_dram, rows_dram, sums_dram):
    with ExitStack() as ctx:
        sb = lambda name, shape, dt=F32: ctx.enter_context(nc.sbuf_tensor(name, shape, dt))
        pb = lambda name, shape: ctx.enter_context(nc.psum_tensor(name, shape, F32))
        sem = lambda name: keep(shared, ctx.enter_context(nc.semaphore(name)))
        s = shared
        adj = sb("f_adj", [P, NBUF, CT * UB])
        y = sb("f_y", [P, UB])
        r = sb("f_r", [P, UB])
        w_user = sb("f_w_user", [P, D])
        b_u = sb("f_b_user", [P, 1])
        cur = sb("f_cur", [P, CH], I32)
        nxt = sb("f_nxt", [P, CH], I32)
        dst = sb("f_dst", [P, CH + 1], I32)
        same = sb("f_same", [P, CH], I32)
        target = sb("f_target", [P, CH], I32)
        place = sb("f_place", [P, CH], I32)
        row_cur = sb("f_row_cur", [P, 1], I32)
        row_nxt = sb("f_row_nxt", [P, 1], I32)
        blank = sb("f_blank", [P, BLANK])
        acc = pb("f_acc", [P, 512])
        tp = [pb(f"f_tp{n}", [P, 512]) for n in range(4)]

        adj_in = [sem(f"f_adj_in{n}") for n in range(NBUF)]
        adj_used = sem("f_adj_used")
        small_in = sem("f_small_in")
        y_in = sem("f_y_in")
        acc_free, acc_ready = sem("f_acc_free"), sem("f_acc_ready")
        r_stored = sem("f_r_stored")
        blank_made, blanks_stored = sem("f_blank_made"), pool_sem(nc, s, "f_blanks_stored")
        sorted_step = sem("f_sorted_step")
        unflipped = sem("f_unflipped")
        turned, turn_free = sem("f_turned"), sem("f_turn_free")
        place_made = sem("f_place_made")
        keys_stored = pool_sem(nc, s, "f_keys_stored")
        row_ready = sem("f_row_ready")
        chunk_in = pool_sem(nc, s, "f_chunk_in")
        ends_ready = sem("f_ends_ready")
        index_step = sem("f_index_step")
        rows_stored = pool_sem(nc, s, "f_rows_stored")
        ends_stored = pool_sem(nc, s, "f_ends_stored")
        held = sem("f_held")
        tail_made = sem("f_tail_made")
        block = ctx.enter_context(nc.Block())

        K = [s["keys"][:, n, :].bitcast(F32) for n in range(4)]
        KI = [s["keys"][:, n, :] for n in range(4)]

        done_rows, done_cols = {}, {}
        n = 0
        for k in range(1, LOGR):
            n += k
        n += 1 + LOGR
        done_rows[12] = n
        for k in range(13, 20):
            n += k - LOGP
            done_cols[k] = n
            n += LOGP
            done_rows[k] = n
        n += 1
        merge_first = n
        n += 12
        done_cols[20] = n
        n += LOGP
        done_rows[20] = n

        @block.sync
        def _(sp):
            def load(ub, c):
                w = min(CT, NT - c * CT) * UB
                sp.dma_start(adj[:, c % NBUF, 0:w], adj_t[ub, :, c * CT * UB:c * CT * UB + w]
                             if isinstance(ub, int) else
                             adj_t[bass.ds(ub, 1), :, c * CT * UB:c * CT * UB + w].rearrange("o p n -> (o p) n")
                             ).then_inc(adj_in[c % NBUF], 16)
            for c in range(NCH):
                if c >= NBUF:
                    sp.wait_ge(adj_used, c - NBUF + 1)
                load(0, c)
            with sp.Fori(1, NUB) as ub:
                for c in range(NCH):
                    sp.wait_ge(adj_used, NCH * ub + (c - NBUF + 1))
                    load(ub, c)

        @block.tensor
        def _(pe):
            pe.sem_inc(acc_free, 1)
            pe.sem_inc(turn_free, 4)

            def products(ub, first, last):
                for c in range(first, last):
                    pe.wait_ge(adj_in[c % NBUF], 32 * ub + 16 * (c // NBUF + 1))
                    if c == 0:
                        pe.wait_ge(acc_free, ub + 1)
                    w = min(CT, NT - c * CT)
                    for k in range(w):
                        ins = nc.tensor.matmul(acc[:, 0:UB], s["h"][:, c * CT + k, :], adj[:, c % NBUF, k * UB:(k + 1) * UB],
                                               start=(c == 0 and k == 0), stop=False)
                    ins.then_inc(adj_used, 1)
                if last == NCH:
                    pe.wait_ge(y_in, 16 * ub + 16)
                    nc.tensor.matmul(acc[:, 0:UB], w_user[:], y[:], start=False, stop=True).then_inc(acc_ready, 1)

            def turn(src, group):
                for q in range(8):
                    pe.wait_ge(turn_free, group + (q + 1))
                    for m in range(4):
                        b = 4 * q + m
                        ins = nc.tensor.transpose(tp[q % 4][:, m * P:(m + 1) * P], src[:, b * P:(b + 1) * P], s["ident"][:])
                    ins.then_inc(turned, 1)

            pe.wait_ge(small_in, 32)
            with pe.Fori(0, BEFORE) as ub:
                products(ub, 0, NCH)
            for pair in range(3):
                for v in range(2):
                    k = 13 + 2 * pair + v
                    ub = BEFORE + 2 * pair + v
                    pe.wait_ge(unflipped, k - 12)
                    turn(K[0], 16 * (k - 13))
                    products(ub, 0, 6)
                    pe.wait_ge(sorted_step, done_cols[k])
                    turn(K[1], 16 * (k - 13) + 8)
                    products(ub, 6, NCH)
            pe.wait_ge(unflipped, 7)
            turn(K[0], 96)
            products(BEFORE + 6, 0, 6)
            pe.wait_ge(sorted_step, done_cols[19])
            turn(K[1], 104)
            products(BEFORE + 6, 6, NCH)
            pe.wait_ge(sorted_step, merge_first)
            turn(K[1], 112)
            turn(K[2], 120)
            with pe.Fori(BEFORE + 7, BEFORE + 9) as ub:
                products(ub, 0, NCH)
            pe.wait_ge(sorted_step, done_cols[20])
            turn(K[0], 128)
            turn(K[3], 136)
            with pe.Fori(BEFORE + 9, NUB) as ub:
                products(ub, 0, NCH)

        @block.scalar
        def _(act):
            act.dma_start(w_user[:], w_user_t).then_inc(small_in, 16)
            act.dma_start(b_u[:], b_user).then_inc(small_in, 16)
            act.dma_start(y[:], y0_dram[:, 0:UB]).then_inc(y_in, 16)
            act.wait_ge(small_in, 32)
            act.sem_inc(r_stored, 16)

            def finish(ub, more):
                act.wait_ge(acc_ready, ub + 1)
                act.wait_ge(r_stored, 16 * ub + 16)
                if more:
                    act.dma_start(y[:], y0_dram[:, bass.ds((ub + 1) * UB, UB)]).then_inc(y_in, 16)
                nc.scalar.activation(r[:], acc[:, 0:UB], ACT.Relu, bias=b_u[:, 0:1]).then_inc(acc_free, 1)
                act.wait_ge(acc_free, ub + 2)
                act.dma_start(r_dram[:, bass.ds(ub * UB, UB)], r[:]).then_inc(r_stored, 16)

            def unturn(dst, group, sign=None):
                for q in range(8):
                    act.wait_ge(turned, group + (q + 1))
                    if sign is None:
                        nc.scalar.copy(dst[:, q * 512:(q + 1) * 512], tp[q % 4][:]).then_inc(turn_free, 1)
                    else:
                        nc.scalar.mul(dst[:, q * 512:(q + 1) * 512], tp[q % 4][:], sign).then_inc(turn_free, 1)

            with act.Fori(0, BEFORE) as ub:
                finish(ub, True)
            for k in range(13, 20):
                act.wait_ge(sorted_step, done_rows[k - 1])
                nc.scalar.mul(K[0], K[0], s["sign"][:, k - 13:k - 12]).then_inc(unflipped, 1)
                unturn(K[1] if (k - LOGP) % 2 == 0 else K[2], 16 * (k - 13))
                unturn(K[2], 16 * (k - 13) + 8, s["sign"][:, k - 12:k - 11] if k < 19 else None)
                finish(k - 13 + BEFORE, True)
            unturn(K[0], 112)
            unturn(K[3], 120)
            with act.Fori(BEFORE + 7, BEFORE + 9) as ub:
                finish(ub, True)
            unturn(K[1], 128)
            unturn(K[2], 136)
            with act.Fori(BEFORE + 9, NUB - 1) as ub:
                finish(ub, True)
            finish(NUB - 1, False)
            act.wait_ge(r_stored, 16 * NUB + 16)

        @block.vector
        def _(dve):
            steps = [0]

            def exchange(pairs):
                for lo_in, hi_in, lo_out, hi_out, up in pairs:
                    nc.vector.tensor_tensor(lo_out, lo_in, hi_in, ALU.min if up else ALU.max)
                    ins = nc.vector.tensor_tensor(hi_out, lo_in, hi_in, ALU.max if up else ALU.min)
                steps[0] += 1
                ins.then_inc(sorted_step, 1)
                dve.wait_ge(sorted_step, steps[0])

            def stage(bufs_in, bufs_out, b, k):
                pairs = []
                for i, o in zip(bufs_in, bufs_out):
                    for (li, hi, up), (lo, ho, _) in zip(stage_views(i, b, k, LOGR), stage_views(o, b, k, LOGR)):
                        pairs.append((li, hi, lo, ho, up))
                exchange(pairs)

            at = 0
            for k in range(1, LOGR):
                for b in reversed(range(k)):
                    stage([K[at]], [K[1 - at]], b, k)
                    at = 1 - at
            assert at == 0
            nc.vector.tensor_scalar(K[0], K[0], s["sign"][:, 0:1], None, ALU.mult).then_inc(sorted_step, 1)
            steps[0] += 1
            dve.wait_ge(sorted_step, steps[0])
            for b in reversed(range(LOGR)):
                stage([K[at]], [K[1 - at]], b, None)
                at = 1 - at
            assert at == 0 and steps[0] == done_rows[12]
            for k in range(13, 20):
                dve.wait_ge(turn_free, 4 + 16 * (k - 13) + 8)
                at = 1 if (k - LOGP) % 2 == 0 else 2
                for b in reversed(range(LOGP, k)):
                    place_bit = b - LOGR if b >= LOGR else b
                    stage([K[at]], [K[3 - at]], place_bit, k - LOGR if k < 19 else None)
                    at = 3 - at
                assert at == 1 and steps[0] == done_cols[k]
                dve.wait_ge(turn_free, 4 + 16 * (k - 13) + 16)
                at = 2
                for b in reversed(range(LOGP)):
                    stage([K[at]], [K[2 - at]], b, None)
                    at = 2 - at
                assert at == 0 and steps[0] == done_rows[k]
            exchange([(K[0], K[3], K[1], K[2], True)])
            dve.wait_ge(turn_free, 4 + 128)
            a, o = [K[0], K[3]], [K[1], K[2]]
            for b in reversed(range(LOGP, 19)):
                stage(a, o, b - LOGR if b >= LOGR else b, None)
                a, o = o, a
            dve.wait_ge(turn_free, 4 + 144)
            a, o = [K[1], K[2]], [K[0], K[3]]
            for b in reversed(range(LOGP)):
                stage(a, o, b, None)
                a, o = o, a
            assert steps[0] == done_rows[20]

            nc.vector.memset(KI[1], KEY_BASE | DST_FIELD << DST_SHIFT).then_inc(tail_made, 1)

            count = dve.value_load(s["chunks"][0:1, 0:1], min_val=1, max_val=CHMAX)
            nc.vector.tensor_copy(row_cur[:], s["row_first"][:])
            nc.vector.tensor_scalar(row_nxt[:], s["row_first"][:], 1, None, ALU.add).then_inc(row_ready, 1)
            dve.wait_ge(place_made, 1)
            with dve.Fori(0, count) as i:
                dve.wait_ge(chunk_in, 32 * i + 32)
                nc.vector.tensor_scalar(row_cur[:], row_cur[:], 1, None, ALU.add)
                nc.vector.tensor_scalar(row_nxt[:], row_nxt[:], 1, None, ALU.add)
                nc.vector.tensor_scalar(dst[:, 0:CH], cur[:], DST_SHIFT, DST_FIELD, ALU.logical_shift_right, ALU.bitwise_and)
                nc.vector.tensor_scalar(dst[:, CH:CH + 1], nxt[:, 0:1], DST_SHIFT, DST_FIELD, ALU.logical_shift_right,
                                        ALU.bitwise_and).then_inc(index_step, 1)
                dve.wait_ge(index_step, 3 * i + 1)
                nc.vector.tensor_tensor(same[:], dst[:, 0:CH], dst[:, 1:CH + 1], ALU.is_equal).then_inc(index_step, 1)
                dve.wait_ge(index_step, 3 * i + 2)
                nc.vector.scalar_tensor_tensor(out=target[:], in0=same[:], scalar=float(BIG), in1=dst[:, 0:CH],
                                               op0=ALU.mult, op1=ALU.add)
                nc.vector.tensor_scalar(place[:], place[:], CH, None, ALU.add).then_inc(index_step, 1)
                dve.wait_ge(index_step, 3 * i + 3)
                dve.sem_inc(ends_ready, 1)
                dve.wait_ge(ends_stored, i * (16 * CH) + 16 * CH)
                dve.sem_inc(row_ready, 1)

        @block.gpsimd
        def _(pool):
            nc.gpsimd.iota(place[:], [[1, CH]], base=-CH, channel_multiplier=RMAX).then_inc(place_made, 1)
            nc.gpsimd.memset(blank[:], 0.0).then_inc(blank_made, 1)
            pool.wait_ge(blank_made, 1)
            sums_flat = sums_dram.rearrange("(p c) f -> p (c f)", p=P)
            with pool.Fori(0, RMAX * STW // BLANK) as i:
                pool.dma_start(sums_flat[:, bass.ds(i * BLANK, BLANK)], blank[:]).then_inc(blanks_stored, 16)
            pool.wait_ge(blanks_stored, RMAX * STW // BLANK * 16)
            pool.wait_ge(sorted_step, done_rows[20])
            for half, n in ((0, 0), (1, 3)):
                pool.dma_start(keys_dram[half * E:(half + 1) * E].rearrange("(p j) -> p j", p=P), KI[n]).then_inc(keys_stored, 16)
            pool.wait_ge(tail_made, 1)
            pool.dma_start(keys_dram[2 * E:3 * E].rearrange("(p j) -> p j", p=P), KI[1]).then_inc(keys_stored, 16)
            pool.wait_ge(keys_stored, 48)
            count = pool.value_load(s["chunks"][0:1, 0:1], min_val=1, max_val=CHMAX)
            by_chunk = keys_dram.rearrange("(n j) -> n j", j=CH)
            with pool.Fori(0, count) as i:
                hold(pool, row_ready, i + 1, held)
                pool.indirect_dma_start(cur[:], None, by_chunk, bass.IndirectOffsetOnAxis(ap=row_cur[:, 0:1], axis=0)).then_inc(chunk_in, 16)
                pool.indirect_dma_start(nxt[:], None, by_chunk, bass.IndirectOffsetOnAxis(ap=row_nxt[:, 0:1], axis=0)).then_inc(chunk_in, 16)
                pool.wait_ge(chunk_in, 32 * i + 32)
                pool.dma_start(rows_dram[:, bass.ds(i * CH, CH)], cur[:]).then_inc(rows_stored, 16)
                hold(pool, ends_ready, i + 1, held)
                for j in range(CH):
                    pool.indirect_dma_start(s["end_id"], bass.IndirectOffsetOnAxis(ap=target[:, j:j + 1], axis=0),
                                            place[:, j:j + 1], None, bounds_check=N - 1, oob_is_err=False).then_inc(ends_stored, 16)
                hold(pool, rows_stored, 16 * i + 16, held)
            pool.dma_start(rows_dram[:, bass.ds(count * CH, CH)], cur[:]).then_inc(rows_stored, 16)
            hold(pool, rows_stored, 16 * count + 16, held)
            hold(pool, ends_stored, count * (16 * CH), held)


def layernorm(nc, shared, name, add=None, gamma=None, beta=None):
    with ExitStack() as ctx:
        sb = lambda what, shape, dt=F32: ctx.enter_context(nc.sbuf_tensor(f"{name}_{what}", shape, dt))
        pb = lambda what, shape: ctx.enter_context(nc.psum_tensor(f"{name}_{what}", shape, F32))
        sem = lambda what: keep(shared, ctx.enter_context(nc.semaphore(f"{name}_{what}")))
        s = shared
        x, y = s["x"], s["y"]
        sq = sb("sq", [P, N])
        gain = sb("gain", [P, 2])
        mean_ps = [pb(f"mean{u}", [P, 512]) for u in range(2)]
        var_ps = [pb(f"var{u}", [P, 512]) for u in range(2)]
        held, add_in, gain_in, added = sem("held"), sem("add_in"), sem("gain_in"), sem("added")
        centred, squared, scaled, normed = sem("centred"), sem("squared"), sem("scaled"), sem("normed")
        mean_free, mean_ready, var_free, var_ready = sem("mean_free"), sem("mean_ready"), sem("var_free"), sem("var_ready")
        rstd_ready = sem("rstd_ready")
        block = ctx.enter_context(nc.Block())
        at = lambda t, b: t[:, bass.ds(b * UB, UB)]

        @block.sync
        def _(sp):
            if add is not None:
                sp.dma_start(x[:], s["x_in"]).then_inc(add_in, 16)
                sp.dma_start(y[:, 0:N], add).then_inc(add_in, 16)
                sp.wait_ge(add_in, 32)
            if gamma is not None:
                sp.dma_start(gain[:, 0:1], gamma).then_inc(gain_in, 16)
                sp.dma_start(gain[:, 1:2], beta).then_inc(gain_in, 16)
                sp.wait_ge(gain_in, 32)

        @block.tensor
        def _(pe):
            pe.sem_inc(mean_free, 2)
            pe.sem_inc(var_free, 2)
            with pe.Fori(0, NUB // 2) as i:
                for u in range(2):
                    b = 2 * i + u
                    pe.wait_ge(mean_free, b + 1)
                    if add is not None:
                        pe.wait_ge(added, b + 1)
                    nc.tensor.matmul(mean_ps[u][:, 0:UB], s["mean_w"][:], at(x, b), start=True, stop=True).then_inc(mean_ready, 1)
            with pe.Fori(0, NUB // 2) as i:
                for u in range(2):
                    b = 2 * i + u
                    pe.wait_ge(var_free, b + 1)
                    pe.wait_ge(squared, b + 1)
                    nc.tensor.matmul(var_ps[u][:, 0:UB], s["mean_w"][:], at(sq, b), start=True, stop=True).then_inc(var_ready, 1)

        @block.scalar
        def _(act):
            with act.Fori(0, NUB) as b:
                hold(act, centred, b + 1, held)
                nc.scalar.activation(at(sq, b), at(y, b), ACT.Square).then_inc(squared, 1)
            with act.Fori(0, NUB // 2) as i:
                nc.scalar.preload_act_table_set("natural_log_exp_and_others")
                for u in range(2):
                    b = 2 * i + u
                    hold(act, var_ready, b + 1, held)
                    nc.scalar.activation(at(sq, b), var_ps[u][:, 0:UB], ACT.Ln, bias=s["eps"][:, 0:1]).then_inc(var_free, 1)
                    hold(act, var_free, b + 3, held)
                    nc.scalar.activation(at(sq, b), at(sq, b), ACT.Exp, scale=-0.5).then_inc(rstd_ready, 1)

        @block.vector
        def _(dve):
            if add is not None:
                nc.vector.memset(y[:, N:NPAD], 0.0)
                dve.wait_ge(add_in, 32)
            with dve.Fori(0, NUB // 2) as i:
                if add is not None:
                    for u in range(2):
                        b = 2 * i + u
                        nc.vector.tensor_tensor(at(x, b), at(x, b), at(y, b), ALU.add).then_inc(added, 1)
                for u in range(2):
                    b = 2 * i + u
                    dve.wait_ge(mean_ready, b + 1)
                    nc.vector.tensor_tensor(at(y, b), at(x, b), mean_ps[u][:, 0:UB], ALU.subtract).then_inc(centred, 1)
                    dve.wait_ge(centred, b + 1)
                    dve.sem_inc(mean_free, 1)
            if gamma is not None:
                dve.wait_ge(gain_in, 32)
            with dve.Fori(0, NUB) as b:
                dve.wait_ge(rstd_ready, b + 1)
                if gamma is None:
                    nc.vector.tensor_tensor(at(y, b), at(y, b), at(sq, b), ALU.mult).then_inc(normed, 1)
                else:
                    nc.vector.scalar_tensor_tensor(out=at(y, b), in0=at(y, b), scalar=gain[:, 0:1], in1=at(sq, b),
                                                   op0=ALU.mult, op1=ALU.mult).then_inc(scaled, 1)
                    dve.wait_ge(scaled, b + 1)
                    nc.vector.tensor_scalar(at(y, b), at(y, b), gain[:, 1:2], None, ALU.add).then_inc(normed, 1)


def node_table(nc, shared, w_gat, att_src, att_dst):
    with ExitStack() as ctx:
        sb = lambda name, shape, dt=F32: ctx.enter_context(nc.sbuf_tensor(name, shape, dt))
        pb = lambda name, shape: ctx.enter_context(nc.psum_tensor(name, shape, F32))
        sem = lambda name: keep(shared, ctx.enter_context(nc.semaphore(name)))
        s = shared
        w = sb("n_w", [P, H0 * C0])
        att = sb("n_att", [P, 2, H0 * C0])
        table = sb("n_table", [P, NT, TABW])
        prod = sb("n_prod", [P, NT, H0 * C0])
        h_ps = pb("n_h", [P, 3, 512])
        small_in, h_ready, padded = sem("n_small_in"), sem("n_h_ready"), sem("n_padded")
        step_done, table_ready, table_stored = sem("n_step"), sem("n_table_ready"), sem("n_table_stored")
        block = ctx.enter_context(nc.Block())

        @block.sync
        def _(sp):
            sp.dma_start(w[:], w_gat).then_inc(small_in, 16)
            for n, v in enumerate((att_src, att_dst)):
                sp.dma_start(att[:, n, :], v.to_broadcast([P, H0 * C0])).then_inc(small_in, 16)
            sp.wait_ge(table_ready, 1)
            sp.dma_start(s["table"].rearrange("(p t) f -> p (t f)", p=P), table[:].rearrange("p t f -> p (t f)")).then_inc(table_stored, 16)
            sp.wait_ge(table_stored, 16)

        @block.gpsimd
        def _(pool):
            for k in range(H0):
                ins = nc.gpsimd.memset(table[:, :, k * HC + C0:k * HC + HC], 1.0)
            ins.then_inc(padded, 1)

        @block.tensor
        def _(pe):
            pe.wait_ge(small_in, 48)
            by_tile = s["y"][:].rearrange("p (n t) -> p t n", t=NT)
            for t in range(NT):
                at = t % 32 * 16
                ins = nc.tensor.matmul(h_ps[:, t // 32, at:at + 16], by_tile[:, t, :], w[:], start=True, stop=True)
            ins.then_inc(h_ready, 1)

        @block.vector
        def _(dve):
            steps = [0]

            def step(ins):
                steps[0] += 1
                ins.then_inc(step_done, 1)
                dve.wait_ge(step_done, steps[0])

            dve.wait_ge(h_ready, 1)
            dve.wait_ge(padded, 1)
            dve.wait_ge(small_in, 48)
            for g in range(3):
                n = min(32, NT - 32 * g)
                ins = nc.vector.tensor_copy(
                    table[:, 32 * g:32 * g + n, 0:NF].rearrange("p t (k c) -> p t k c", c=HC)[:, :, :, 0:C0],
                    h_ps[:, g, 0:16 * n].rearrange("p (t k c) -> p t k c", k=H0, c=C0))
            step(ins)
            heads = table[:, :, 0:NF].rearrange("p t (k c) -> p t k c", c=HC)[:, :, :, 0:C0]
            for n in range(2):
                for k in range(H0):
                    ins = nc.vector.tensor_tensor(
                        prod[:, :, k * C0:(k + 1) * C0], heads[:, :, k, :],
                        att[:, n:n + 1, k * C0:(k + 1) * C0].to_broadcast([P, NT, C0]), ALU.mult)
                step(ins)
                step(nc.vector.tensor_reduce(table[:, :, NF + n * H0:NF + n * H0 + H0],
                                             prod[:].rearrange("p t (k c) -> p t k c", c=C0), AX.X, ALU.add))
            dve.sem_inc(table_ready, 1)


def attend(nc, shared, keys_dram, rows_dram, sums_dram, counts_dram):
    with ExitStack() as ctx:
        sb = lambda name, shape, dt=F32: ctx.enter_context(nc.sbuf_tensor(name, shape, dt))
        pb = lambda name, shape: ctx.enter_context(nc.psum_tensor(name, shape, F32))
        sem = lambda name: keep(shared, ctx.enter_context(nc.semaphore(name)))
        s = shared
        keys = [sb(f"a_keys{u}", [P, HF], I32) for u in range(2)]
        field = sb("a_field", [P, HF], I32)
        dst = sb("a_dst", [P, HF], I32)
        is_loop = sb("a_is_loop", [P, HF], I32)
        index = [sb(f"a_index{u}", [P, HF], I32) for u in range(2)]
        first = [sb(f"a_first{u}", [P, HF]) for u in range(2)]
        rest_ = [sb(f"a_rest{u}", [P, HF]) for u in range(2)]
        wall = [sb(f"a_wall{u}", [P, HF]) for u in range(2)]
        got = [sb(f"a_got{u}", [P, HF, TABW]) for u in range(2)]
        start = sb("a_start", [P, H0, HF])
        a_dst = [sb(f"a_a_dst{u}", [P, H0, HF]) for u in range(2)]
        score = sb("a_score", [P, H0, HF])
        top = [sb(f"a_top{u}", [P, H0, HF + 1]) for u in range(2)]
        weight = sb("a_weight", [P, 2, H0, HF])
        value = sb("a_value", [P, NF, HF])
        sums = [sb(f"a_sums{u}", [P, HF, STW]) for u in range(2)]
        apart = sb("a_apart", [P, CH], I32)
        part = sb("a_part", [P, 2, CH], I32)
        part_b = sb("a_part_b", [P, 2, CH], BF16)
        line = sb("a_line", [P, 2, P], BF16)
        line_i = sb("a_line_i", [P, 2, P], I32)
        hot = [sb(f"a_hot{u}", [P, HOT, P + NT], BF16) for u in range(2)]
        nought = sb("a_nought", [P, P], BF16)
        counts = sb("a_counts", [P, NT])
        counts_t = sb("a_counts_t", [NT, P])
        counts_ps = pb("a_counts_ps", [P, 512])
        counts_t_ps = pb("a_counts_t_ps", [P, 512])
        row_key = sb("a_row_key", [P, 1], I32)
        row_dst = sb("a_row_dst", [P, 1], I32)
        row_index = sb("a_row_index", [P, 1], I32)
        row_got = sb("a_row_got", [P, TABW])
        tail = sb("a_tail", [P, 4, NF])
        rows = sb("a_rows", [NF, 4, P])
        join = sb("a_join", [NF, 8, P])
        run_top = sb("a_run_top", [NF, P + 1])
        run_sum = sb("a_run_sum", [NF, P + 1])
        carry = sb("a_carry", [P, 3, NF])
        last_key = sb("a_last_key", [P, 1], I32)
        last_dst = sb("a_last_dst", [P, 1], I32)
        end_f = sb("a_end_f", [P, 2])
        place_f = sb("a_place_f", [P, 1])
        target_f = sb("a_target_f", [P, 1])
        place = sb("a_place", [P, 1], I32)
        target = sb("a_target", [P, 1], I32)
        ended = sb("a_ended", [P, STW])
        mix = sb("a_mix", [P, 6, NF])
        tr_ps = pb("a_tr", [P, 4, P])
        back_ps = pb("a_back", [P, 4, P])

        held = sem("a_held")
        apart_in, apart_used = sem("a_apart_in"), sem("a_apart_used")
        line_made, part_step, hot_ready, hot_used = sem("a_line_made"), sem("a_part_step"), sem("a_hot_ready"), sem("a_hot_used")
        counts_ready, counts_out, counts_turned = sem("a_counts_ready"), sem("a_counts_out"), sem("a_counts_turned")
        counts_back, counts_stored = sem("a_counts_back"), sem("a_counts_stored")
        keys_in = [sem(f"a_keys_in{u}") for u in range(2)]
        keys_used = sem("a_keys_used")
        row_in, row_ready, row_got_in, row_set = sem("a_row_in"), sem("a_row_ready"), pool_sem(nc, s, "a_row_got_in"), sem("a_row_set")
        index_ready, got_in, got_used = sem("a_index_ready"), [pool_sem(nc, s, f"a_got_in{u}") for u in range(2)], sem("a_got_used")
        prep_step, main_step = sem("a_prep_step"), sem("a_main_step")
        gaps_ready, weights_ready = sem("a_gaps_ready"), sem("a_weights_ready")
        sums_ready, sums_stored = sem("a_sums_ready"), [sem(f"a_sums_stored{u}") for u in range(2)]
        end_step, tails_ready, turned = sem("a_end_step"), sem("a_tails_ready"), sem("a_turned")
        gap_ready, gap_exp, carry_ready, carry_turned = sem("a_gap_ready"), sem("a_gap_exp"), sem("a_carry_ready"), sem("a_carry_turned")
        place_in, ended_in, mix_ready, mix_exp = pool_sem(nc, s, "a_place_in"), pool_sem(nc, s, "a_ended_in"), sem("a_mix_ready"), sem("a_mix_exp")
        last_in = sem("a_last_in")
        fixed, fixed_stored, edges_done = sem("a_fixed"), pool_sem(nc, s, "a_fixed_stored"), sem("a_edges_done")
        block = ctx.enter_context(nc.Block())
        sums_flat = sums_dram.rearrange("(p c) f -> p (c f)", p=P)

        @block.sync
        def _(sp):
            count = sp.value_load(s["chunks"][0:1, 0:1], min_val=1, max_val=CHMAX)
            sp.dma_start(row_key[:], rows_dram[:, 0:1], allow_slow_non_contiguous=True).then_inc(row_in, 16)
            for u in range(2):
                sp.dma_start(keys[u][:], rows_dram[:, u * HF:(u + 1) * HF]).then_inc(keys_in[u], 16)
                sp.sem_inc(sums_stored[u], 16)
            with sp.Fori(0, count) as i:
                for u in range(2):
                    sp.wait_ge(keys_used, 2 * i + u + 1)
                    sp.dma_start(keys[u][:], rows_dram[:, bass.ds((i + 1) * CH + u * HF, HF)]).then_inc(keys_in[u], 16)
                    sp.wait_ge(sums_ready, 2 * i + u + 1)
                    sp.dma_start(sums_flat[:, bass.ds((i * CH + u * HF) * STW, HF * STW)],
                                 sums[u][:].rearrange("p c f -> p (c f)")).then_inc(sums_stored[u], 16)
            sp.dma_start(last_key[:], rows_dram[:, bass.ds(count * CH - 1, 1)], allow_slow_non_contiguous=True).then_inc(last_in, 16)
            for u in range(2):
                hold(sp, sums_stored[u], 16 * count + 16, held)
                hold(sp, keys_in[u], 16 * count + 16, held)
            sp.sem_inc(edges_done, 1)
            sp.wait_ge(counts_back, 1)
            sp.dma_start(counts_dram.rearrange("(t p) -> t p", p=P), counts_t[:]).then_inc(counts_stored, 16)
            sp.wait_ge(counts_stored, 16)

        @block.gpsimd
        def _(pool):
            count = pool.value_load(s["chunks"][0:1, 0:1], min_val=1, max_val=CHMAX)
            nc.gpsimd.iota(line_i[:, 0, :], [[1, P]], base=0, channel_multiplier=0)
            nc.gpsimd.iota(line_i[:, 1, :], [[1, P]], base=P, channel_multiplier=0)
            nc.gpsimd.memset(nought[:], 0.0).then_inc(line_made, 1)
            pool.wait_ge(row_ready, 1)
            pool.indirect_dma_start(row_got[:], None, s["table"], bass.IndirectOffsetOnAxis(ap=row_index[:, 0:1], axis=0)).then_inc(row_got_in, 16)
            pool.sem_inc(got_used, 2)
            with pool.Fori(0, count) as i:
                for u in range(2):
                    hold(pool, index_ready, 2 * i + u + 1, held)
                    hold(pool, got_used, 2 * i + u + 1, held)
                    for j in range(HF):
                        pool.indirect_dma_start(got[u][:, j, :], None, s["table"],
                                                bass.IndirectOffsetOnAxis(ap=index[u][:, j:j + 1], axis=0)).then_inc(got_in[u], 16)
            pool.wait_ge(edges_done, 1)
            pool.indirect_dma_start(place[:], None, s["end_id"], bass.IndirectOffsetOnAxis(ap=row_index[:, 0:1], axis=0)).then_inc(place_in, 16)
            pool.wait_ge(place_in, 16)
            pool.indirect_dma_start(ended[:], None, sums_dram, bass.IndirectOffsetOnAxis(ap=place[:, 0:1], axis=0)).then_inc(ended_in, 16)
            pool.wait_ge(fixed, 1)
            pool.indirect_dma_start(sums_dram, bass.IndirectOffsetOnAxis(ap=target[:, 0:1], axis=0), ended[:], None,
                                    bounds_check=P * RMAX - 1, oob_is_err=False).then_inc(fixed_stored, 16)
            pool.wait_ge(fixed_stored, 16)

        @block.scalar
        def _(act):
            count = act.value_load(s["chunks"][0:1, 0:1], min_val=1, max_val=CHMAX)
            each = act.value_load(s["apart_each"][0:1, 0:1], min_val=1, max_val=CHMAX + 1)
            by_chunk = keys_dram.rearrange("(n j) -> n j", j=CH)
            act.sem_inc(apart_used, 1)
            with act.Fori(0, count) as i:
                for u in range(2):
                    act.wait_ge(gaps_ready, 2 * i + u + 1)
                    nc.scalar.activation(weight[:], weight[:], ACT.Exp).then_inc(weights_ready, 1)
                    if u == 0:
                        with act.Fori(0, each) as k:
                            hold(act, apart_used, i * each + k + 1, held)
                            first = act.value_load(s["apart_first"][0:1, 0:1], min_val=0, max_val=3 * E // CH - P)
                            act.dma_start(apart[:], by_chunk[bass.ds(first, P), :]).then_inc(apart_in, 16)
            act.wait_ge(gap_ready, 1)
            nc.scalar.activation(join[:, 5:7, :], join[:, 5:7, :], ACT.Exp).then_inc(gap_exp, 1)
            act.wait_ge(mix_ready, 1)
            nc.scalar.activation(mix[:, 1:3, :], mix[:, 1:3, :], ACT.Exp).then_inc(mix_exp, 1)

        @block.vector
        def _(dve):
            count = dve.value_load(s["chunks"][0:1, 0:1], min_val=1, max_val=CHMAX)
            steps = [0]

            def step(ins, sem):
                steps[0] += 1
                ins.then_inc(sem, 1)
                dve.wait_ge(sem, steps[0])

            dve.wait_ge(row_in, 16)
            step(nc.vector.tensor_scalar(row_dst[:], row_key[:], DST_SHIFT, DST_FIELD, ALU.logical_shift_right, ALU.bitwise_and), row_set)
            step(nc.vector.tensor_scalar(row_index[:], row_dst[:], N - 1, None, ALU.min), row_set)
            dve.sem_inc(row_ready, 1)
            nc.vector.memset(top[1][:, :, HF:HF + 1], NEG)
            step(nc.vector.memset(sums[1][:, HF - 1, :], 0.0), row_set)
            dve.wait_ge(row_got_in, 16)
            step(nc.vector.tensor_copy(a_dst[1][:, :, HF - 1], row_got[:, NF + H0:TABW]), row_set)

            PREP, MAIN = 4, 9
            each_count = dve.value_load(s["apart_each"][0:1, 0:1], min_val=1, max_val=CHMAX + 1)
            dve.wait_ge(line_made, 1)
            step(nc.vector.tensor_copy(line[:], line_i[:]), row_set)

            def count_apart(n):
                dve.wait_ge(apart_in, n * 16 + 16)
                nc.vector.tensor_scalar(part[:, 0, :], apart[:], DST_SHIFT, P - 1, ALU.logical_shift_right, ALU.bitwise_and)
                nc.vector.tensor_scalar(part[:, 1, :], apart[:], DST_SHIFT + LO, 2 * P - 1, ALU.logical_shift_right,
                                        ALU.bitwise_and)
                nc.vector.tensor_scalar(s["apart_first"][:], s["apart_first"][:], P, None, ALU.add).then_inc(part_step, 1)
                dve.wait_ge(part_step, 2 * n + 1)
                dve.sem_inc(apart_used, 1)
                nc.vector.tensor_copy(part_b[:], part[:]).then_inc(part_step, 1)
                dve.wait_ge(part_step, 2 * n + 2)
                for q in range(CH // HOT):
                    dve.wait_ge(hot_used, n * (CH // HOT) + (q + 1))
                    for v, (at, w) in enumerate(((0, P), (P, NT))):
                        ins = nc.vector.tensor_tensor(
                            hot[q % 2][:, :, at:at + w],
                            part_b[:, v, q * HOT:(q + 1) * HOT].rearrange("p (j o) -> p j o", o=1).to_broadcast([P, HOT, w]),
                            line[:, v:v + 1, 0:w].to_broadcast([P, HOT, w]), ALU.is_equal)
                    ins.then_inc(hot_ready, 1)

            def prep(u, n):
                at = PREP * n

                def done(ins, k):
                    ins.then_inc(prep_step, 1)
                    dve.wait_ge(prep_step, at + k)
                dve.wait_ge(keys_in[u], 8 * n + (16 - 8 * u))
                nc.vector.tensor_scalar(field[:], keys[u][:], FIELD, None, ALU.bitwise_and)
                done(nc.vector.tensor_scalar(dst[:], keys[u][:], DST_SHIFT, DST_FIELD, ALU.logical_shift_right, ALU.bitwise_and), 1)
                nc.vector.tensor_scalar(first[u][:], field[:], 0, None, ALU.is_equal)
                done(nc.vector.tensor_scalar(is_loop[:], field[:], 0, None, ALU.is_equal), 2)
                nc.vector.tensor_scalar(rest_[u][:], first[u][:], -1.0, 1.0, ALU.mult, ALU.add)
                nc.vector.tensor_scalar(wall[u][:], first[u][:], NEG, None, ALU.mult)
                nc.vector.tensor_scalar(field[:], field[:], 1, None, ALU.subtract)
                done(nc.vector.scalar_tensor_tensor(out=dst[:], in0=dst[:], scalar=1, in1=is_loop[:], op0=ALU.add, op1=ALU.mult), 3)
                dve.sem_inc(held, 1)
                done(nc.vector.tensor_tensor(dst[:], dst[:], field[:], ALU.add), 4)
                nc.vector.tensor_scalar(index[u][:], dst[:], N - 1, None, ALU.min).then_inc(index_ready, 1)
                dve.wait_ge(index_ready, n + 1)
                dve.sem_inc(keys_used, 1)

            def halves(u, i):
                n = 2 * i + u
                at = MAIN * n
                g, t, before = got[u], top[u], 1 - u
                each = lambda v: v[:].rearrange("p (o j) -> p o j", o=1).to_broadcast([P, H0, HF])

                def done(ins, k):
                    ins.then_inc(main_step, 1)
                    dve.wait_ge(main_step, at + k)

                dve.wait_ge(got_in[u], i * (16 * HF) + 16 * HF)
                nc.vector.tensor_copy(t[:, :, 0:1], top[before][:, :, HF:HF + 1])
                done(nc.vector.tensor_tensor(start[:], g[:, :, NF + H0:TABW].rearrange("p j k -> p k j"), each(first[u]), ALU.mult), 1)
                for k in range(H0):
                    ins = nc.vector.tensor_tensor_scan(a_dst[u][:, k, :], rest_[u][:], start[:, k, :],
                                                       a_dst[before][:, k, HF - 1:HF], ALU.mult, ALU.add)
                done(ins, 2)
                done(nc.vector.tensor_tensor(start[:], g[:, :, NF:NF + H0].rearrange("p j k -> p k j"), a_dst[u][:], ALU.add), 3)
                done(nc.vector.scalar_tensor_tensor(out=score[:], in0=start[:], scalar=0.2, in1=start[:], op0=ALU.mult, op1=ALU.max), 4)
                for k in range(H0):
                    ins = nc.vector.tensor_tensor_scan(t[:, k, 1:HF + 1], wall[u][:], score[:, k, :], t[:, k, 0:1], ALU.add, ALU.max)
                done(ins, 5)
                nc.vector.tensor_tensor(weight[:, 1], score[:], t[:, :, 1:HF + 1], ALU.subtract)
                done(nc.vector.tensor_tensor(weight[:, 0], t[:, :, 0:HF], t[:, :, 1:HF + 1], ALU.subtract), 6)
                done(nc.vector.tensor_tensor(weight[:, 0], weight[:, 0], each(wall[u]), ALU.add), 7)
                dve.sem_inc(gaps_ready, 1)
                dve.wait_ge(weights_ready, n + 1)
                for k in range(H0):
                    ins = nc.vector.tensor_tensor(value[:, k * HC:(k + 1) * HC, :],
                                                  g[:, :, k * HC:(k + 1) * HC].rearrange("p j c -> p c j"),
                                                  weight[:, 1, k:k + 1, :].to_broadcast([P, HC, HF]), ALU.mult)
                done(ins, 8)
                dve.sem_inc(got_used, 1)
                dve.wait_ge(sums_stored[u], 16 * i + 16)
                for f in range(NF):
                    nc.vector.tensor_tensor_scan(sums[u][:, :, f], weight[:, 0, f // HC, :], value[:, f, :],
                                                 sums[before][:, HF - 1, f:f + 1], ALU.mult, ALU.add)
                done(nc.vector.tensor_copy(sums[u][:, :, NF:STW], t[:, :, 1:HF + 1].rearrange("p k j -> p j k")), 9)
                dve.sem_inc(sums_ready, 1)

            prep(0, 0)
            with dve.Fori(0, count) as i:
                prep(1, 2 * i + 1)
                halves(0, i)
                with dve.Fori(0, each_count) as k:
                    count_apart(i * each_count + k)
                prep(0, 2 * i + 2)
                halves(1, i)

            dve.wait_ge(counts_ready, 1)
            step(nc.vector.tensor_copy(counts[:], counts_ps[:, 0:NT]), row_set)
            dve.sem_inc(counts_out, 1)
            dve.wait_ge(counts_turned, 1)
            step(nc.vector.tensor_copy(counts_t[:], counts_t_ps[0:NT, 0:P]), row_set)
            dve.sem_inc(counts_back, 1)

            steps[0] = 0
            step = lambda ins: (steps.__setitem__(0, steps[0] + 1), ins.then_inc(end_step, 1), dve.wait_ge(end_step, steps[0]))
            dve.wait_ge(last_in, 16)
            nc.vector.tensor_copy(tail[:, 0, :], sums[1][:, HF - 1, 0:NF])
            for k in range(H0):
                nc.vector.tensor_scalar(tail[:, 1, k * HC:(k + 1) * HC], s["ones"][:, 0:HC], top[1][:, k, HF:HF + 1], None, ALU.mult)
            nc.vector.tensor_copy(end_f[:, 1:2], row_dst[:])
            step(nc.vector.tensor_scalar(last_dst[:], last_key[:], DST_SHIFT, DST_FIELD, ALU.logical_shift_right, ALU.bitwise_and))
            step(nc.vector.tensor_copy(end_f[:, 0:1], last_dst[:]))
            nc.vector.tensor_scalar(tail[:, 2, :], s["ones"][:, 0:NF], end_f[:, 0:1], None, ALU.mult)
            step(nc.vector.tensor_scalar(tail[:, 3, :], s["ones"][:, 0:NF], end_f[:, 1:2], None, ALU.mult))
            dve.sem_inc(tails_ready, 1)
            dve.wait_ge(turned, 1)
            nc.vector.memset(run_top[:, 0:1], NEG)
            nc.vector.memset(run_sum[:, 0:1], 0.0)
            nc.vector.memset(join[:, 0, 0:1], 0.0)
            nc.vector.memset(join[:, 4, P - 1:P], 0.0)
            step(nc.vector.tensor_copy(rows[:], tr_ps[0:NF, :, :]))
            S, M, T, F = (rows[:, n, :] for n in range(4))
            CONT, WHOLE, THROUGH, WALL, ON, RATIO, SHARE, PART = (join[:, n, :] for n in range(8))
            nc.vector.tensor_tensor(CONT[:, 1:P], F[:, 1:P], T[:, 0:P - 1], ALU.is_equal)
            nc.vector.tensor_tensor(ON[:, 0:P - 1], F[:, 1:P], T[:, 0:P - 1], ALU.is_equal)
            step(nc.vector.tensor_tensor(WHOLE, F, T, ALU.is_equal))
            step(nc.vector.tensor_tensor(THROUGH, CONT, WHOLE, ALU.mult))
            step(nc.vector.tensor_scalar(WALL, THROUGH, -NEG, NEG, ALU.mult, ALU.add))
            step(nc.vector.tensor_tensor_scan(run_top[:, 1:P + 1], WALL, M, NEG, ALU.add, ALU.max))
            nc.vector.tensor_tensor(SHARE, M, run_top[:, 1:P + 1], ALU.subtract)
            step(nc.vector.tensor_tensor(RATIO, run_top[:, 0:P], run_top[:, 1:P + 1], ALU.subtract))
            step(nc.vector.tensor_tensor(RATIO, RATIO, WALL, ALU.add))
            dve.sem_inc(gap_ready, 1)
            dve.wait_ge(gap_exp, 1)
            step(nc.vector.tensor_tensor(PART, S, SHARE, ALU.mult))
            nc.vector.tensor_tensor_scan(run_sum[:, 1:P + 1], RATIO, PART, 0.0, ALU.mult, ALU.add)
            step(nc.vector.tensor_tensor(THROUGH, WHOLE, ON, ALU.mult))
            step(nc.vector.tensor_scalar(THROUGH, THROUGH, -1.0, 1.0, ALU.mult, ALU.add))
            step(nc.vector.tensor_tensor(THROUGH, THROUGH, CONT, ALU.mult))
            step(nc.vector.scalar_tensor_tensor(out=THROUGH, in0=F, scalar=float(N), in1=THROUGH, op0=ALU.is_lt, op1=ALU.mult))
            dve.sem_inc(carry_ready, 1)
            dve.wait_ge(carry_turned, 1)
            step(nc.vector.tensor_copy(carry[:], back_ps[:, 0:3, 0:NF]))
            dve.wait_ge(place_in, 16)
            dve.wait_ge(ended_in, 16)
            for k in range(H0):
                nc.vector.tensor_scalar(mix[:, 0, k * HC:(k + 1) * HC], s["ones"][:, 0:HC], ended[:, NF + k:NF + k + 1], None, ALU.mult)
            nc.vector.tensor_copy(place_f[:], place[:])
            step(nc.vector.tensor_scalar(target_f[:], carry[:, 2, 0:1], -float(BIG), float(BIG), ALU.mult, ALU.add))
            nc.vector.tensor_tensor(target[:], target_f[:], place_f[:], ALU.add)
            step(nc.vector.tensor_tensor(mix[:, 3, :], mix[:, 0, :], carry[:, 0, :], ALU.max))
            nc.vector.tensor_tensor(mix[:, 1, :], mix[:, 0, :], mix[:, 3, :], ALU.subtract)
            step(nc.vector.tensor_tensor(mix[:, 2, :], carry[:, 0, :], mix[:, 3, :], ALU.subtract))
            dve.sem_inc(mix_ready, 1)
            dve.wait_ge(mix_exp, 1)
            nc.vector.tensor_tensor(mix[:, 4, :], ended[:, 0:NF], mix[:, 1, :], ALU.mult)
            step(nc.vector.tensor_tensor(mix[:, 5, :], carry[:, 1, :], mix[:, 2, :], ALU.mult))
            nc.vector.tensor_tensor(ended[:, 0:NF], mix[:, 4, :], mix[:, 5, :], ALU.add)
            step(nc.vector.tensor_copy(ended[:, NF:STW], mix[:, 3, :].rearrange("p (k c) -> p k c", c=HC)[:, :, 0]))
            dve.sem_inc(fixed, 1)

        @block.tensor
        def _(pe):
            total = pe.value_load(s["apart_all"][0:1, 0:1], min_val=1, max_val=4 * CHMAX)
            pe.sem_inc(hot_used, 2)
            pe.wait_ge(line_made, 1)
            nc.tensor.matmul(counts_ps[:, 0:NT], nought[:], nought[:, 0:NT], start=True, stop=False)
            with pe.Fori(0, total) as n:
                for q in range(CH // HOT):
                    pe.wait_ge(hot_ready, n * (CH // HOT) + (q + 1))
                    for j in range(HOT):
                        ins = nc.tensor.matmul(counts_ps[:, 0:NT], hot[q % 2][:, j, 0:P], hot[q % 2][:, j, P:P + NT],
                                               start=False, stop=False)
                    ins.then_inc(hot_used, 1)
            nc.tensor.matmul(counts_ps[:, 0:NT], nought[:], nought[:, 0:NT], start=False, stop=True).then_inc(counts_ready, 1)
            pe.wait_ge(counts_out, 1)
            nc.tensor.transpose(counts_t_ps[0:NT, 0:P], counts[:], s["ident"][:]).then_inc(counts_turned, 1)
            pe.wait_ge(tails_ready, 1)
            for n in range(4):
                ins = nc.tensor.transpose(tr_ps[0:NF, n, :], tail[:, n, :], s["ident"][:])
            ins.then_inc(turned, 1)
            pe.wait_ge(carry_ready, 1)
            for n, v in enumerate((run_top[:, 0:P], run_sum[:, 0:P], join[:, 2, :])):
                ins = nc.tensor.transpose(back_ps[:, n, 0:NF], v, s["ident"][0:NF, 0:NF])
            ins.then_inc(carry_turned, 1)


def gate_steps(nc, dve, step, s, E_, score, better, count, gate, best, total):
    step(nc.vector.memset(count[:], 0.0))
    for j in range(E_):
        one = score[:, :, j:j + 1]
        if j:
            ins = nc.vector.tensor_tensor(better[:, :, 0:j], score[:, :, 0:j], one.to_broadcast([P, NT, j]), ALU.is_lt)
        if j < E_ - 1:
            ins = nc.vector.tensor_tensor(better[:, :, j + 1:E_], score[:, :, j + 1:E_],
                                          one.to_broadcast([P, NT, E_ - 1 - j]), ALU.is_le)
        step(ins)
        if j:
            ins = nc.vector.tensor_tensor(count[:, :, 0:j], count[:, :, 0:j], better[:, :, 0:j], ALU.add)
        if j < E_ - 1:
            ins = nc.vector.tensor_tensor(count[:, :, j + 1:E_], count[:, :, j + 1:E_], better[:, :, j + 1:E_], ALU.add)
        step(ins)
    step(nc.vector.tensor_reduce(best[:], score[:], AX.X, ALU.max))
    step(nc.vector.tensor_tensor(gate[:], score[:], best[:].rearrange("p (t o) -> p t o", o=1).to_broadcast([P, NT, E_]),
                                 ALU.subtract))


def gate_ends(nc, step, E_, count, gate, total):
    step(nc.vector.scalar_tensor_tensor(out=gate[:], in0=count[:], scalar=2.0, in1=gate[:], op0=ALU.is_lt, op1=ALU.mult))
    step(nc.vector.tensor_reduce(total[:], gate[:], AX.X, ALU.add))
    step(nc.vector.reciprocal(total[:], total[:]))
    step(nc.vector.tensor_tensor(gate[:], gate[:], total[:].rearrange("p (t o) -> p t o", o=1).to_broadcast([P, NT, E_]), ALU.mult))


def turn_gates_pe(nc, pe, s, gate, E_, gate_ps, gates_ready, bank_free, bank_ready):
    pe.sem_inc(bank_free, 2)
    pe.wait_ge(gates_ready, 1)
    for g in range(-(-NT // 4)):
        pe.wait_ge(bank_free, g + 1)
        for q in range(min(4, NT - 4 * g)):
            ins = nc.tensor.transpose(gate_ps[g % 2][0:E_, q * P:(q + 1) * P], gate[:, 4 * g + q, :], s["ident"][:])
        ins.then_inc(bank_ready, 1)


def turn_gates_act(nc, act, s, E_, gate_ps, bank_free, bank_ready):
    by_tile = s["gates"][0:E_, :].rearrange("e (p t) -> e t p", t=NT)
    for g in range(-(-NT // 4)):
        n = min(4, NT - 4 * g)
        act.wait_ge(bank_ready, g + 1)
        nc.scalar.copy(by_tile[:, 4 * g:4 * g + n, :],
                       gate_ps[g % 2][0:E_, 0:n * P].rearrange("e (t p) -> e t p", p=P)).then_inc(bank_free, 1)


def graph_gates(nc, shared, sums_dram, counts_dram, b_gat, ln_gamma, ln_beta):
    with ExitStack() as ctx:
        sb = lambda name, shape, dt=F32: ctx.enter_context(nc.sbuf_tensor(name, shape, dt))
        pb = lambda name, shape: ctx.enter_context(nc.psum_tensor(name, shape, F32))
        sem = lambda name: keep(shared, ctx.enter_context(nc.semaphore(name)))
        s = shared
        Q = H0 * C0
        ends = sb("g_ends", [P, NT], I32)
        got = sb("g_got", [P, NT, STW])
        rows = sb("g_rows", [P, 3, Q])
        table = sb("g_table", [P, NT, TABW])
        last = sb("g_last", [P, TABW])
        times = sb("g_times", [P, NT])
        tall = sb("g_tall", [P, NT])
        extra = sb("g_extra", [P, NT, H0])
        top = sb("g_top", [P, NT, H0])
        scale = sb("g_scale", [P, 2, NT, H0])
        more = sb("g_more", [P, NT, NF])
        agg = sb("g_agg", [P, NT, Q])
        sq = sb("g_sq", [P, NT, Q])
        den = sb("g_den", [P, NT, H0])
        mean = sb("g_mean", [P, NT])
        var = sb("g_var", [P, NT])
        score = sb("g_score", [P, NT, C0])
        better = sb("g_better", [P, NT, C0])
        count = sb("g_count", [P, NT, C0])
        gate = sb("g_gate", [P, NT, C0])
        gate_ps = [pb(f"g_ps{u}", [P, 512]) for u in range(2)]
        ends_in, got_in, rows_in = sem("g_ends_in"), pool_sem(nc, s, "g_got_in"), sem("g_rows_in")
        table_in, scale_ready, scaled = sem("g_table_in"), sem("g_scale_ready"), sem("g_scaled")
        step_done, var_ready, rooted = sem("g_step"), sem("g_var_ready"), sem("g_rooted")
        raised, exp_done, gates_ready = sem("g_raised"), sem("g_exp_done"), sem("g_gates_ready")
        bank_free, bank_ready = sem("g_bank_free"), sem("g_bank_ready")
        block = ctx.enter_context(nc.Block())

        @block.sync
        def _(sp):
            sp.dma_start(ends[:], s["end_id"].rearrange("(p t) o -> p (t o)", p=P)).then_inc(ends_in, 16)
            sp.dma_start(table[:].rearrange("p t f -> p (t f)"), s["table"].rearrange("(p t) f -> p (t f)", p=P)).then_inc(table_in, 16)
            sp.dma_start(last[:], s["table"][N - 1:N, :].to_broadcast([P, TABW])).then_inc(table_in, 16)
            sp.dma_start(times[:], counts_dram.rearrange("(p t) -> p t", p=P)).then_inc(table_in, 16)
            for n, v in enumerate((b_gat, ln_gamma, ln_beta)):
                sp.dma_start(rows[:, n, :], v.to_broadcast([P, Q])).then_inc(rows_in, 16)

        @block.gpsimd
        def _(pool):
            pool.wait_ge(ends_in, 16)
            for t in range(NT):
                pool.indirect_dma_start(got[:, t, :], None, sums_dram,
                                        bass.IndirectOffsetOnAxis(ap=ends[:, t:t + 1], axis=0)).then_inc(got_in, 16)

        @block.vector
        def _(dve):
            steps = [0]

            def step(ins):
                steps[0] += 1
                ins.then_inc(step_done, 1)
                dve.wait_ge(step_done, steps[0])

            per_tile = lambda v: v.rearrange("p (o q) -> p o q", o=1).to_broadcast([P, NT, Q])
            per_node = lambda v: v[:].rearrange("p (t o) -> p t o", o=1).to_broadcast([P, NT, Q])
            dve.wait_ge(table_in, 48)
            wide = lambda v, n: v.rearrange("p (t o) -> p t o", o=1).to_broadcast([P, NT, n])
            nc.vector.tensor_scalar(tall[:], times[:], 0.0, None, ALU.is_gt)
            step(nc.vector.tensor_tensor(top[:], table[:, :, NF + H0:TABW],
                                         last[:, NF:NF + H0].rearrange("p (o k) -> p o k", o=1).to_broadcast([P, NT, H0]), ALU.add))
            nc.vector.scalar_tensor_tensor(out=extra[:], in0=top[:], scalar=0.2, in1=top[:], op0=ALU.mult, op1=ALU.max)
            step(nc.vector.tensor_scalar(tall[:], tall[:], -NEG, NEG, ALU.mult, ALU.add))
            step(nc.vector.tensor_tensor(extra[:], extra[:], wide(tall[:], H0), ALU.add))
            dve.wait_ge(got_in, 16 * NT)
            dve.wait_ge(rows_in, 48)
            step(nc.vector.tensor_tensor(top[:], extra[:], got[:, :, NF:STW], ALU.max))
            nc.vector.tensor_tensor(scale[:, 0], got[:, :, NF:STW], top[:], ALU.subtract)
            step(nc.vector.tensor_tensor(scale[:, 1], extra[:], top[:], ALU.subtract))
            dve.sem_inc(scale_ready, 1)
            dve.wait_ge(scaled, 1)
            step(nc.vector.tensor_tensor(scale[:, 1], scale[:, 1], wide(times[:], H0), ALU.mult))
            for k in range(H0):
                f = slice(k * HC, (k + 1) * HC)
                nc.vector.tensor_tensor(more[:, :, f], last[:, f].rearrange("p (o c) -> p o c", o=1).to_broadcast([P, NT, HC]),
                                        scale[:, 1, :, k:k + 1].to_broadcast([P, NT, HC]), ALU.mult)
                ins = nc.vector.tensor_tensor(got[:, :, f], got[:, :, f], scale[:, 0, :, k:k + 1].to_broadcast([P, NT, HC]), ALU.mult)
            step(ins)
            step(nc.vector.tensor_tensor(got[:, :, 0:NF], got[:, :, 0:NF], more[:], ALU.add))
            heads = got[:, :, 0:NF].rearrange("p t (k c) -> p t k c", c=HC)
            step(nc.vector.tensor_scalar(den[:], heads[:, :, :, C0], 1e-16, None, ALU.add))
            step(nc.vector.reciprocal(den[:], den[:]))
            for k in range(H0):
                ins = nc.vector.tensor_tensor(agg[:, :, k * C0:(k + 1) * C0], heads[:, :, k, 0:C0],
                                              den[:, :, k:k + 1].to_broadcast([P, NT, C0]), ALU.mult)
            step(ins)
            step(nc.vector.tensor_tensor(agg[:], agg[:], per_tile(rows[:, 0, :]), ALU.add))
            step(nc.vector.tensor_reduce(mean[:], agg[:], AX.X, ALU.add))
            step(nc.vector.tensor_scalar(mean[:], mean[:], 1.0 / Q, None, ALU.mult))
            step(nc.vector.tensor_tensor(agg[:], agg[:], per_node(mean), ALU.subtract))
            step(nc.vector.tensor_tensor(sq[:], agg[:], agg[:], ALU.mult))
            step(nc.vector.tensor_reduce(var[:], sq[:], AX.X, ALU.add))
            step(nc.vector.tensor_scalar(var[:], var[:], 1.0 / Q, EPS, ALU.mult, ALU.add))
            dve.sem_inc(var_ready, 1)
            dve.wait_ge(rooted, 1)
            step(nc.vector.reciprocal(var[:], var[:]))
            step(nc.vector.tensor_tensor(agg[:], agg[:], per_node(var), ALU.mult))
            step(nc.vector.tensor_tensor(agg[:], agg[:], per_tile(rows[:, 1, :]), ALU.mult))
            step(nc.vector.tensor_tensor(agg[:], agg[:], per_tile(rows[:, 2, :]), ALU.add))
            step(nc.vector.tensor_reduce(score[:], agg[:].rearrange("p t (k c) -> p t c k", c=C0), AX.X, ALU.add))
            step(nc.vector.tensor_scalar(score[:], score[:], 1.0 / H0, None, ALU.mult))
            gate_steps(nc, dve, step, s, C0, score, better, count, gate, mean, var)
            dve.sem_inc(raised, 1)
            dve.wait_ge(exp_done, 1)
            gate_ends(nc, step, C0, count, gate, var)
            dve.sem_inc(gates_ready, 1)

        @block.scalar
        def _(act):
            act.wait_ge(scale_ready, 1)
            nc.scalar.activation(scale[:], scale[:], ACT.Exp).then_inc(scaled, 1)
            act.wait_ge(var_ready, 1)
            nc.scalar.activation(var[:], var[:], ACT.Sqrt).then_inc(rooted, 1)
            act.wait_ge(raised, 1)
            nc.scalar.activation(gate[:], gate[:], ACT.Exp).then_inc(exp_done, 1)
            turn_gates_act(nc, act, s, C0, gate_ps, bank_free, bank_ready)

        @block.tensor
        def _(pe):
            turn_gates_pe(nc, pe, s, gate, C0, gate_ps, gates_ready, bank_free, bank_ready)


def routed_gates(nc, shared, w_r, b_r):
    with ExitStack() as ctx:
        sb = lambda name, shape, dt=F32: ctx.enter_context(nc.sbuf_tensor(name, shape, dt))
        pb = lambda name, shape: ctx.enter_context(nc.psum_tensor(name, shape, F32))
        sem = lambda name: keep(shared, ctx.enter_context(nc.semaphore(name)))
        s = shared
        E_ = 8
        w = sb("r_w", [P, E_])
        bias = sb("r_b", [P, E_])
        score = sb("r_score", [P, NT, E_])
        better = sb("r_better", [P, NT, E_])
        count = sb("r_count", [P, NT, E_])
        gate = sb("r_gate", [P, NT, E_])
        best = sb("r_best", [P, NT])
        total = sb("r_total", [P, NT])
        score_ps = pb("r_score_ps", [P, 2, 512])
        gate_ps = [pb(f"r_ps{u}", [P, 512]) for u in range(2)]
        w_in, score_ready, step_done = sem("r_w_in"), sem("r_score_ready"), sem("r_step")
        raised, exp_done, gates_ready = sem("r_raised"), sem("r_exp_done"), sem("r_gates_ready")
        bank_free, bank_ready = sem("r_bank_free"), sem("r_bank_ready")
        block = ctx.enter_context(nc.Block())

        @block.sync
        def _(sp):
            sp.dma_start(w[:], w_r).then_inc(w_in, 16)
            sp.dma_start(bias[:], b_r.to_broadcast([P, E_])).then_inc(w_in, 16)

        @block.tensor
        def _(pe):
            pe.wait_ge(w_in, 32)
            by_tile = s["y"][:].rearrange("p (n t) -> p t n", t=NT)
            for t in range(NT):
                ins = nc.tensor.matmul(score_ps[:, t // 64, t % 64 * E_:t % 64 * E_ + E_], by_tile[:, t, :], w[:],
                                       start=True, stop=True)
            ins.then_inc(score_ready, 1)
            turn_gates_pe(nc, pe, s, gate, E_, gate_ps, gates_ready, bank_free, bank_ready)

        @block.scalar
        def _(act):
            act.wait_ge(raised, 1)
            nc.scalar.activation(gate[:], gate[:], ACT.Exp).then_inc(exp_done, 1)
            turn_gates_act(nc, act, s, E_, gate_ps, bank_free, bank_ready)

        @block.vector
        def _(dve):
            steps = [0]

            def step(ins):
                steps[0] += 1
                ins.then_inc(step_done, 1)
                dve.wait_ge(step_done, steps[0])

            dve.wait_ge(score_ready, 1)
            dve.wait_ge(w_in, 32)
            for g in range(2):
                n = min(64, NT - 64 * g)
                ins = nc.vector.tensor_tensor(score[:, 64 * g:64 * g + n, :],
                                              score_ps[:, g, 0:n * E_].rearrange("p (t e) -> p t e", e=E_),
                                              bias[:].rearrange("p (o e) -> p o e", o=1).to_broadcast([P, n, E_]), ALU.add)
            step(ins)
            gate_steps(nc, dve, step, s, E_, score, better, count, gate, best, total)
            dve.sem_inc(raised, 1)
            dve.wait_ge(exp_done, 1)
            gate_ends(nc, step, E_, count, gate, total)
            dve.sem_inc(gates_ready, 1)


def experts(nc, shared, name, E_, w1_d, b1_d, w2_d, b2_d, out):
    with ExitStack() as ctx:
        sb = lambda what, shape, dt=F32: ctx.enter_context(nc.sbuf_tensor(f"{name}_{what}", shape, dt))
        pb = lambda what, shape: ctx.enter_context(nc.psum_tensor(f"{name}_{what}", shape, F32))
        sem = lambda what: keep(shared, ctx.enter_context(nc.semaphore(f"{name}_{what}")))
        s = shared
        x, y, gates = s["x"], s["y"], s["gates"]
        w1 = sb("w1", [P, E_, HID])
        b1 = sb("b1", [P, E_, 2])
        w2 = sb("w2", [P, E_, 2, D])
        b2 = sb("b2", [E_, D])
        hid = [sb(f"hid{u}", [P, 2, UB]) for u in range(2)]
        up_ps = [pb(f"up{u}", [P, 2, 512]) for u in range(2)]
        gate_ps = [pb(f"gate{u}", [P, 512]) for u in range(2)]
        acc = [pb(f"acc{u}", [P, 512]) for u in range(2)]
        held = sem("held")
        w_in = sem("w_in")
        up_ready, up_free, gate_free = sem("up_ready"), sem("up_free"), sem("gate_free")
        hid_ready, hid_scaled, hid_free = sem("hid_ready"), sem("hid_scaled"), sem("hid_free")
        acc_ready, acc_free, stored = sem("acc_ready"), sem("acc_free"), sem("stored")
        block = ctx.enter_context(nc.Block())
        at = lambda t, b: t[:, bass.ds(b * UB, UB)]

        @block.sync
        def _(sp):
            sp.dma_start(w1[:].rearrange("p e h -> p (e h)"), w1_d).then_inc(w_in, 16)
            sp.dma_start(b1[:].rearrange("p e h -> p (e h)"), b1_d).then_inc(w_in, 16)
            sp.dma_start(w2[:].rearrange("p e h d -> p (e h d)"), w2_d).then_inc(w_in, 16)
            sp.dma_start(b2[:], b2_d).then_inc(w_in, 16)
            if out is not None:
                with sp.Fori(0, NUB) as b:
                    sp.wait_ge(acc_free, b + 3)
                    sp.dma_start(out[:, bass.ds(b * UB, UB)], at(x, b)).then_inc(stored, 16)
                sp.wait_ge(stored, 16 * NUB)

        @block.tensor
        def _(pe):
            pe.wait_ge(w_in, 64)
            pe.sem_inc(up_free, 2)
            pe.sem_inc(gate_free, 2)
            pe.sem_inc(acc_free, 2)

            def up(b, e, n):
                pe.wait_ge(up_free, n + 1)
                pe.wait_ge(gate_free, n + 1)
                for h in range(2):
                    nc.tensor.matmul(up_ps[e % 2][:, h, 0:UB], w1[:, e, h * P:(h + 1) * P], at(y, b), start=True, stop=True)
                nc.tensor.matmul(gate_ps[e % 2][:, 0:UB], s["ident"][0:E_, e:e + 1].to_broadcast([E_, P]),
                                 at(gates[0:E_, :], b), start=True, stop=True).then_inc(up_ready, 1)

            def down(u, b, e, n):
                pe.wait_ge(hid_scaled, n + 1)
                for h in range(2):
                    ins = nc.tensor.matmul(acc[u][:, 0:UB], w2[:, e, h, :], hid[e % 2][:, h, :],
                                           start=(e == 0 and h == 0), stop=False)
                ins.then_inc(hid_free, 1)

            with pe.Fori(0, NUB // 2) as i:
                for u in range(2):
                    b = 2 * i + u
                    up(b, 0, b * E_)
                    pe.wait_ge(acc_free, b + 1)
                    for e in range(E_):
                        if e < E_ - 1:
                            up(b, e + 1, b * E_ + (e + 1))
                        down(u, b, e, b * E_ + e)
                    nc.tensor.matmul(acc[u][:, 0:UB], b2[:], at(gates[0:E_, :], b), start=False, stop=True).then_inc(acc_ready, 1)

        @block.scalar
        def _(act):
            act.wait_ge(w_in, 64)
            act.sem_inc(hid_free, 2)
            with act.Fori(0, NUB) as b:
                for e in range(E_):
                    n = b * E_ + e
                    act.wait_ge(up_ready, n + 1)
                    act.wait_ge(hid_free, n + 1)
                    for h in range(2):
                        ins = nc.scalar.activation(hid[e % 2][:, h, :], up_ps[e % 2][:, h, 0:UB], ACT.Gelu, bias=b1[:, e, h:h + 1])
                    ins.then_inc(hid_ready, 1)
                    act.wait_ge(hid_ready, n + 1)
                    act.sem_inc(up_free, 1)

        @block.vector
        def _(dve):
            with dve.Fori(0, NUB // 2) as i:
                for u in range(2):
                    b = 2 * i + u
                    for e in range(E_):
                        n = b * E_ + e
                        dve.wait_ge(hid_ready, n + 1)
                        for h in range(2):
                            ins = nc.vector.tensor_tensor(hid[e % 2][:, h, :], hid[e % 2][:, h, :], gate_ps[e % 2][:, 0:UB], ALU.mult)
                        ins.then_inc(hid_scaled, 1)
                        dve.wait_ge(hid_scaled, n + 1)
                        dve.sem_inc(gate_free, 1)
                    dve.wait_ge(acc_ready, b + 1)
                    nc.vector.tensor_tensor(at(x, b), at(x, b), acc[u][:, 0:UB], ALU.add).then_inc(acc_free, 1)


def second_pass(nc, shared, adj_t, w_msg, b_msg):
    with ExitStack() as ctx:
        sb = lambda name, shape, dt=F32: ctx.enter_context(nc.sbuf_tensor(name, shape, dt))
        pb = lambda name, shape: ctx.enter_context(nc.psum_tensor(name, shape, F32))
        sem = lambda name: keep(shared, ctx.enter_context(nc.semaphore(name)))
        s = shared
        x, y = s["x"], s["y"]
        w = sb("m_w", [P, D])
        b_row = sb("m_b", [1, D])
        msg = sb("m_msg", [P, NT, D])
        adj = sb("m_adj", [P, MBUF, MT * UB])
        inv = [y[:, u * MT * UB:(u + 1) * MT * UB] for u in range(NINV)]
        msg_ps = [pb(f"m_msg_ps{u}", [P, 512]) for u in range(2)]
        acc = pb("m_acc", [P, 512])
        w_in = sem("m_w_in")
        msg_free, msg_ready = sem("m_msg_free"), sem("m_msg_ready")
        adj_in = [sem(f"m_adj_in{n}") for n in range(MBUF)]
        adj_used, acc_free, acc_ready = sem("m_adj_used"), sem("m_acc_free"), sem("m_acc_ready")
        logged, inverted, raised, weighted = sem("m_logged"), sem("m_inverted"), sem("m_raised"), sem("m_weighted")
        squared = sem("m_squared")
        block = ctx.enter_context(nc.Block())
        width = lambda c: min(MT, NT - c * MT) * UB

        @block.sync
        def _(sp):
            sp.dma_start(w[:], w_msg).then_inc(w_in, 16)
            sp.dma_start(b_row[:], b_msg).then_inc(w_in, 16)

            def load(ub, c):
                n = width(c)
                sp.dma_start(adj[:, c % MBUF, 0:n], adj_t[ub, :, c * MT * UB:c * MT * UB + n] if isinstance(ub, int) else
                             adj_t[bass.ds(ub, 1), :, c * MT * UB:c * MT * UB + n].rearrange("o p n -> (o p) n")
                             ).then_inc(adj_in[c % MBUF], 16)
            for c in range(MCH):
                if c >= MBUF:
                    sp.wait_ge(adj_used, c - MBUF + 1)
                load(0, c)
            with sp.Fori(1, NUB) as ub:
                for c in range(MCH):
                    sp.wait_ge(adj_used, MCH * ub + (c - MBUF + 1))
                    load(ub, c)

        @block.tensor
        def _(pe):
            pe.wait_ge(w_in, 32)
            pe.sem_inc(msg_free, 2)
            pe.sem_inc(acc_free, 1)
            for t in range(NT):
                g, q = divmod(t, 4)
                if q == 0:
                    pe.wait_ge(msg_free, g + 1)
                nc.tensor.matmul(msg_ps[g % 2][:, q * D:(q + 1) * D], y[:, t * P:(t + 1) * P], w[:], start=True, stop=False)
                ins = nc.tensor.matmul(msg_ps[g % 2][:, q * D:(q + 1) * D], s["ones"][0:1, :], b_row[:], start=False, stop=True)
                if q == 3 or t == NT - 1:
                    ins.then_inc(msg_ready, 1)
            pe.wait_ge(msg_free, -(-NT // 4) + 2)
            with pe.Fori(0, NUB) as ub:
                pe.wait_ge(acc_free, ub + 1)
                for c in range(MCH):
                    pe.wait_ge(weighted, MCH * ub + (c + 1 + NINV))
                    for k in range(min(MT, NT - c * MT)):
                        ins = nc.tensor.matmul(acc[:, 0:UB], msg[:, c * MT + k, :], adj[:, c % MBUF, k * UB:(k + 1) * UB],
                                               start=(c == 0 and k == 0), stop=(c * MT + k == NT - 1))
                    ins.then_inc(adj_used, 1)
                pe.wait_ge(adj_used, MCH * ub + MCH)
                pe.sem_inc(acc_ready, 1)

        @block.scalar
        def _(act):
            for g in range(-(-NT // 4)):
                n = min(4, NT - 4 * g)
                act.wait_ge(msg_ready, g + 1)
                nc.scalar.copy(msg[:, 4 * g:4 * g + n, :].rearrange("p t d -> p (t d)"), msg_ps[g % 2][:, 0:n * D]).then_inc(msg_free, 1)
            act.wait_ge(msg_free, -(-NT // 4) + 2)

            def log(ub, c):
                n, v = width(c), inv[c % NINV]
                act.wait_ge(adj_in[c % MBUF], (16 * MCH // MBUF) * ub + 16 * (c // MBUF + 1))
                act.wait_ge(weighted, MCH * ub + (c + 1))
                nc.scalar.activation(v[:, 0:n], adj[:, c % MBUF, 0:n], ACT.Ln, bias=s["tiny"][:, 0:1]).then_inc(logged, 1)

            def invert(ub, c):
                n, v = width(c), inv[c % NINV]
                act.wait_ge(logged, MCH * ub + (c + 1))
                nc.scalar.activation(v[:, 0:n], v[:, 0:n], ACT.Exp, scale=-1.0).then_inc(inverted, 1)

            def raise_(ub, c):
                n, v = width(c), inv[c % NINV]
                act.wait_ge(squared, MCH * ub + (c + 1))
                nc.scalar.activation(v[:, 0:n], v[:, 0:n], ACT.Exp, bias=s["minus2"][:, 0:1], scale=-2.0).then_inc(raised, 1)

            def chunks(ub, last):
                for c in range(MCH):
                    then = (ub, c + AHEAD) if c < MCH - AHEAD else None if last else (ub + 1, c + AHEAD - MCH)
                    if then:
                        log(*then)
                    raise_(ub, c)
                    if then:
                        invert(*then)

            nc.scalar.preload_act_table_set("natural_log_exp_and_others")
            for c in range(AHEAD):
                log(0, c)
                invert(0, c)
            with act.Fori(0, NUB - 1) as ub:
                nc.scalar.preload_act_table_set("natural_log_exp_and_others")
                chunks(ub, False)
            chunks(NUB - 1, True)

        @block.vector
        def _(dve):
            def square(ub, c):
                n, v = width(c), inv[c % NINV]
                dve.wait_ge(inverted, MCH * ub + (c + 1))
                nc.vector.scalar_tensor_tensor(out=v[:, 0:n], in0=v[:, 0:n], scalar=-2.0, in1=v[:, 0:n],
                                               op0=ALU.add, op1=ALU.mult).then_inc(squared, 1)

            def weigh(ub, c):
                n, v = width(c), inv[c % NINV]
                dve.wait_ge(raised, MCH * ub + (c + 1))
                r = adj[:, c % MBUF, 0:n]
                nc.vector.scalar_tensor_tensor(out=r, in0=r, scalar=1.0, in1=v[:, 0:n], op0=ALU.is_lt, op1=ALU.mult).then_inc(weighted, 1)

            def chunks(ub, last):
                for c in range(MCH):
                    if c < MCH - 1:
                        square(ub, c + 1)
                    elif not last:
                        square(ub + 1, 0)
                    weigh(ub, c)
                dve.wait_ge(acc_ready, ub + 1)
                nc.vector.tensor_tensor(x[:, bass.ds(ub * UB, UB)], x[:, bass.ds(ub * UB, UB)], acc[:, 0:UB], ALU.add).then_inc(acc_free, 1)

            dve.sem_inc(weighted, NINV)
            square(0, 0)
            with dve.Fori(0, NUB - 1) as ub:
                chunks(ub, False)
            chunks(NUB - 1, True)


def layer_kernel(nc, a, out, stop=99):
    with ExitStack() as ctx:
        dram = lambda name, shape, dt=F32: nc.dram_tensor(name, shape, dt).ap()
        y0_dram = dram("d_y0", [P, N])
        r_dram = dram("d_r", [P, N])
        keys_dram = dram("d_keys", [3 * E], I32)
        counts_dram = dram("d_counts", [NPAD])
        rows_dram = dram("d_rows", [P, RMAX + CH], I32)
        sums_dram = dram("d_sums", [P * RMAX, STW])
        sb = lambda name, shape, dt=F32: ctx.enter_context(nc.sbuf_tensor(name, shape, dt))
        shared = {
            "used_sems": [], "stack": ctx,
            "mean_w": sb("mean_w", [P, P]), "ones": sb("ones", [P, P]), "ident": sb("ident", [P, P]),
            "sign": sb("sign", [P, LOGP]), "eps": sb("eps", [P, 1]), "zero": sb("zero", [P, 1]),
            "tiny": sb("tiny", [P, 1]), "minus2": sb("minus2", [P, 1]),
            "chunks": sb("chunks", [P, 1], I32), "row_first": sb("row_first", [P, 1], I32),
            "apart_first": sb("apart_first", [P, 1], I32), "apart_each": sb("apart_each", [P, 1], I32),
            "apart_all": sb("apart_all", [P, 1], I32),
            "end_id": dram("d_end_id", [NPAD, 1], I32),
        }
        with ExitStack() as early:
            shared["keys"] = early.enter_context(nc.sbuf_tensor("keys", [P, 4, ROW], I32))
            shared["h"] = early.enter_context(nc.sbuf_tensor("h_items", [P, NT, D], F32))
            prepare(nc, shared, a["x_t"], a["item_t"], a["edges"], a["w_item_t"], a["b_item"], y0_dram)
            if stop >= 1:
                first_pass(nc, shared, a["adj_t"], a["w_user_t"], a["b_user"], y0_dram, r_dram, keys_dram, rows_dram, sums_dram)
        if stop < 2:
            return
        shared["x_in"] = a["x_t"]
        shared["x"] = sb("x", [P, N])
        shared["y"] = sb("y", [P, NPAD])
        shared["table"] = dram("d_table", [NPAD, TABW])
        layernorm(nc, shared, "ln1", add=r_dram)
        node_table(nc, shared, a["w_gat"], a["att_src"], a["att_dst"])
        attend(nc, shared, keys_dram, rows_dram, sums_dram, counts_dram)
        clear_semaphores(nc, shared)
        if stop < 3:
            return
        with ExitStack() as late:
            shared["gates"] = late.enter_context(nc.sbuf_tensor("gates0", [8, NPAD], F32))
            graph_gates(nc, shared, sums_dram, counts_dram, a["b_gat"], a["ln_gamma"], a["ln_beta"])
            experts(nc, shared, "e0", 4, a["w1_0"], a["b1_0"], a["w2_0"], a["b2_0"], None)
        layernorm(nc, shared, "ln2")
        if stop < 4:
            return
        second_pass(nc, shared, a["adj_t"], a["w_msg"], a["b_msg"])
        layernorm(nc, shared, "ln3", gamma=a["gamma"], beta=a["beta"])
        with ExitStack() as late:
            shared["gates"] = late.enter_context(nc.sbuf_tensor("gates1", [8, NPAD], F32))
            routed_gates(nc, shared, a["w_r"], a["b_r"])
            experts(nc, shared, "e1", 8, a["w1_1"], a["b1_1"], a["w2_1"], a["b2_1"], out)


def lay_out(x, adj, L0_gnn_item_feat, L0_gnn_W_item, L0_gnn_b_item, L0_gnn_W_user, L0_gnn_b_user,
            L0_ffn_W_gat, L0_ffn_att_src, L0_ffn_att_dst, L0_ffn_b_gat, L0_ffn_ln_gamma, L0_ffn_ln_beta,
            L0_ffn_W1, L0_ffn_b1, L0_ffn_W2, L0_ffn_b2, L0_ffn_edge_index, L1_gnn_W, L1_gnn_B,
            L1_ffn_gamma, L1_ffn_beta, L1_ffn_Wr, L1_ffn_br, L1_ffn_W1, L1_ffn_b1, L1_ffn_W2, L1_ffn_b2):
    import numpy as np
    c = np.ascontiguousarray
    padded = np.zeros((NUB, UB, NT * P), adj.dtype)
    padded[:, :, :N] = np.asarray(adj).reshape(NUB, UB, N)
    adj_t = c(padded.reshape(NUB, UB, NT, P).transpose(0, 3, 2, 1)).reshape(NUB, P, NT * UB)
    item_t = np.zeros((D, NPAD), np.asarray(x).dtype)
    item_t[:, :N] = np.asarray(L0_gnn_item_feat).T
    col = lambda v: c(np.asarray(v).reshape(-1, 1))
    row = lambda v: c(np.asarray(v).reshape(1, -1))
    w1 = lambda w: c(np.asarray(w).transpose(1, 0, 2)).reshape(D, -1)
    w2 = lambda w: c(np.asarray(w).reshape(w.shape[0], 2, P, D).transpose(2, 0, 1, 3)).reshape(P, -1)
    b1 = lambda b: c(np.asarray(b).reshape(-1, P).T)
    return {
        "x_t": c(np.asarray(x).T), "adj_t": adj_t, "item_t": item_t,
        "w_item_t": c(np.asarray(L0_gnn_W_item).T), "b_item": row(L0_gnn_b_item),
        "w_user_t": c(np.asarray(L0_gnn_W_user).T), "b_user": col(L0_gnn_b_user),
        "edges": c(np.asarray(L0_ffn_edge_index)),
        "w_gat": c(np.asarray(L0_ffn_W_gat)), "att_src": row(L0_ffn_att_src), "att_dst": row(L0_ffn_att_dst),
        "b_gat": row(L0_ffn_b_gat), "ln_gamma": row(L0_ffn_ln_gamma), "ln_beta": row(L0_ffn_ln_beta),
        "w1_0": w1(L0_ffn_W1), "b1_0": b1(L0_ffn_b1), "w2_0": w2(L0_ffn_W2), "b2_0": c(np.asarray(L0_ffn_b2)),
        "w_msg": c(np.asarray(L1_gnn_W)), "b_msg": row(L1_gnn_B),
        "gamma": col(L1_ffn_gamma), "beta": col(L1_ffn_beta), "w_r": c(np.asarray(L1_ffn_Wr)), "b_r": row(L1_ffn_br),
        "w1_1": w1(L1_ffn_W1), "b1_1": b1(L1_ffn_b1), "w2_1": w2(L1_ffn_W2), "b2_1": c(np.asarray(L1_ffn_b2)),
    }


def kernel(**inputs):
    import numpy as np
    import concourse.bacc as bacc
    from concourse.bass_utils import run_bass_kernel_spmd

    arrays = lay_out(**inputs)
    nc = bacc.Bacc("TRN2", target_bir_lowering=False, num_devices=1)
    aps = {k: nc.dram_tensor(k, v.shape, mybir.dt.from_np(v.dtype), kind="ExternalInput").ap() for k, v in arrays.items()}
    out = nc.dram_tensor("out_t", (D, N), F32, kind="ExternalOutput").ap()
    layer_kernel(nc, aps, out)
    result = run_bass_kernel_spmd(nc, [arrays], core_ids=[0])
    return np.ascontiguousarray(result.results[0]["out_t"].T)
```

```python
import concourse.bass as bass
from concourse import mybir
from contextlib import ExitStack

F32 = mybir.dt.float32
I32 = mybir.dt.int32
BF16 = mybir.dt.bfloat16
ALU = mybir.AluOpType
ACT = mybir.ActivationFunctionType
AX = mybir.AxisListType

P = 128
N = 10000
D = 128
EPS = 1e-5

UB = 500
NUB = N // UB
PARTS = 5
NT = -(-N // P)
NPAD = NT * P
CT = 8
NCH = -(-NT // CT)
BEFORE = 3
CUT = 5
NBUF = 5

MT = 5
MCH = -(-NT // MT)
MBUF = 8
NINV = 4
AHEAD = 2

E = 524288
ROW = E // P
LOGP, LOGR = 7, 12
DST_SHIFT = 14
FIELD = (1 << DST_SHIFT) - 1
APART = 1 << DST_SHIFT
DST_FIELD = 2 * APART - 1
KEY_BASE = 0x20000000
LO = 7
CH = 128
HF = CH // 2
CHMAX = (E + N) // (P * CH) + 1
RMAX = CHMAX * CH
BIG = 1 << 20
NEG = -1e30

H0, C0 = 4, 4
HC = C0 + 1
NF = H0 * HC
TABW = NF + 2 * H0
STW = NF + H0
HID = 256
E1 = 8
GE = E1 // 2
UT = 4
BT = UB // UT
GATE_PIECE_STEPS = (4 + 2 * 4, 2 * 4, 4)
HOT = 16
BLANK = RMAX * STW // 48


def keep(shared, sem):
    shared["used_sems"].append(sem)
    return sem


def pool_sem(nc, shared, name):
    return shared["stack"].enter_context(nc.semaphore(name))


def clear_semaphores(nc, shared):
    with nc.Block() as block:
        @block.gpsimd
        def _(pool):
            for sem in shared["used_sems"]:
                pool.sem_clear(sem)
    shared["used_sems"] = []


def hold(eng, sem, value, passed):
    eng.wait_ge(sem, value)
    eng.sem_inc(passed, 1)


def stage_views(buf, b, k, width):
    if k is None:
        v = buf.rearrange("p (a two d) -> p a two d", two=2, d=1 << b)
        yield v[:, :, 0, :], v[:, :, 1, :], True
    elif k > b:
        v = buf.rearrange("p (a dir c two d) -> p a dir c two d", dir=2, c=1 << (k - 1 - b), two=2, d=1 << b)
        for way in range(2):
            yield v[:, :, way, :, 0, :], v[:, :, way, :, 1, :], way == 0
    else:
        v = buf.rearrange("p (a two c dir d) -> p a two c dir d", two=2, c=1 << (b - 1 - k), dir=2, d=1 << k)
        for way in range(2):
            yield v[:, :, 0, :, way, :], v[:, :, 1, :, way, :], way == 0


def prepare(nc, shared, x_t, item_t, edges, w_item_t, b_item, y0_dram):
    with ExitStack() as ctx:
        sb = lambda name, shape, dt=F32: ctx.enter_context(nc.sbuf_tensor(name, shape, dt))
        pb = lambda name, shape: ctx.enter_context(nc.psum_tensor(name, shape, F32))
        sem = lambda name: keep(shared, ctx.enter_context(nc.semaphore(name)))
        s = shared
        xc = sb("p_xc", [P, N])
        sq = sb("p_sq", [P, N])
        item = sb("p_item", [P, 2, CT * P])
        w_item = sb("p_w_item", [P, D])
        b_row = sb("p_b_item", [1, D])
        count = sb("p_count", [P, 16])
        total_i = sb("p_total_i", [P, 1], I32)
        part_i = sb("p_part_i", [P, 1], I32)
        totals = sb("p_totals", [P, 4])
        bits = sb("p_bits", [P, LOGP], I32)
        zero_ids = sb("p_zero_ids", [1, NPAD - N], I32)
        mean_ps = [pb(f"p_mean{u}", [P, 512]) for u in range(2)]
        var_ps = [pb(f"p_var{u}", [P, 512]) for u in range(2)]
        h_ps = [pb(f"p_h{u}", [P, 512]) for u in range(2)]
        tot_ps = pb("p_tot", [P, 512])

        weights_in = sem("p_weights_in")
        x_in = sem("p_x_in")
        item_in = [sem(f"p_item_in{u}") for u in range(2)]
        item_used = sem("p_item_used")
        src_in = sem("p_src_in")
        dst_in = sem("p_dst_in")
        consts = sem("p_consts")
        ident_zero = sem("p_ident_zero")
        loops_made = sem("p_loops_made")
        mean_free, mean_ready = sem("p_mean_free"), sem("p_mean_ready")
        centred, squared = sem("p_centred"), sem("p_squared")
        var_free, var_ready = sem("p_var_free"), sem("p_var_ready")
        rstd_ready = sem("p_rstd_ready")
        normed, y_stored = sem("p_normed"), sem("p_y_stored")
        h_free, h_ready = sem("p_h_free"), sem("p_h_ready")
        key_step = sem("p_key_step")
        counted, total_ready = sem("p_counted"), sem("p_total_ready")
        held = sem("p_held")
        zeroed, ids_stored = sem("p_zeroed"), sem("p_ids_stored")
        block = ctx.enter_context(nc.Block())

        @block.sync
        def _(sp):
            sp.dma_start(w_item[:], w_item_t).then_inc(weights_in, 16)
            sp.dma_start(b_row[:], b_item).then_inc(weights_in, 16)
            sp.dma_start(xc[:], x_t).then_inc(x_in, 16)
            sp.dma_start(s["keys"][:, 1, :], edges[0].rearrange("(p j) -> p j", p=P)).then_inc(src_in, 16)
            sp.dma_start(s["keys"][:, 0, :], edges[1].rearrange("(p j) -> p j", p=P)).then_inc(dst_in, 16)
            for c in range(NCH):
                if c >= 2:
                    sp.wait_ge(item_used, c - 1)
                w = min(CT * P, NPAD - c * CT * P)
                sp.dma_start(item[:, c % 2, 0:w], item_t[:, c * CT * P:c * CT * P + w]).then_inc(item_in[c % 2], 16)
            with sp.Fori(0, NUB // 4) as i:
                sp.wait_ge(normed, 4 * i + 4)
                sp.dma_start(y0_dram[:, bass.ds(i * (4 * UB), 4 * UB)],
                             xc[:, bass.ds(i * (4 * UB), 4 * UB)]).then_inc(y_stored, 16)
            sp.wait_ge(zeroed, 1)
            sp.dma_start(s["end_id"][N:NPAD, :].rearrange("n o -> o n"), zero_ids[:]).then_inc(ids_stored, 16)
            sp.wait_ge(ids_stored, 16)
            sp.wait_ge(y_stored, 16 * (NUB // 4))

        @block.gpsimd
        def _(pool):
            nc.gpsimd.iota(s["keys"][:, 3, :], [[-1, ROW]], base=P * ROW - 1, channel_multiplier=-ROW).then_inc(loops_made, 1)
            nc.gpsimd.memset(s["mean_w"][:], 1.0 / D)
            nc.gpsimd.memset(s["ones"][:], 1.0)
            nc.gpsimd.memset(s["eps"][:], EPS)
            nc.gpsimd.memset(s["tiny"][:], 1e-18)
            nc.gpsimd.memset(s["minus2"][:], -2.0)
            nc.gpsimd.memset(zero_ids[:], 0).then_inc(zeroed, 1)
            nc.gpsimd.iota(part_i[:], [[0, 1]], base=0, channel_multiplier=1)
            nc.gpsimd.memset(s["ident"][:], 0.0).then_inc(ident_zero, 1)
            pool.wait_ge(ident_zero, 1)
            nc.gpsimd.affine_select(out=s["ident"][:], in_=s["ident"][:], compare_op=ALU.not_equal, fill=1.0,
                                    base=0, pattern=[[-1, P]], channel_multiplier=1).then_inc(consts, 1)

        @block.tensor
        def _(pe):
            pe.wait_ge(consts, 1)
            pe.wait_ge(x_in, 16)
            pe.sem_inc(mean_free, 2)
            pe.sem_inc(var_free, 2)
            pe.sem_inc(h_free, 2)
            with pe.Fori(0, NUB // 2) as i:
                for u in range(2):
                    pe.wait_ge(mean_free, 2 * i + u + 1)
                    nc.tensor.matmul(mean_ps[u][:, 0:UB], s["mean_w"][:], xc[:, bass.ds((2 * i + u) * UB, UB)],
                                     start=True, stop=True).then_inc(mean_ready, 1)
            with pe.Fori(0, NUB // 2) as i:
                for u in range(2):
                    pe.wait_ge(var_free, 2 * i + u + 1)
                    pe.wait_ge(squared, 2 * i + u + 1)
                    nc.tensor.matmul(var_ps[u][:, 0:UB], s["mean_w"][:], sq[:, bass.ds((2 * i + u) * UB, UB)],
                                     start=True, stop=True).then_inc(var_ready, 1)
            pe.wait_ge(counted, 1)
            nc.tensor.matmul(tot_ps[:, 0:2], s["ones"][:], count[:, 8:10], start=True, stop=True).then_inc(total_ready, 1)
            pe.wait_ge(weights_in, 32)
            for t in range(NT):
                c, k = divmod(t, CT)
                if k == 0:
                    pe.wait_ge(item_in[c % 2], 16 * (c // 2 + 1))
                g, q = divmod(t, 4)
                if q == 0:
                    pe.wait_ge(h_free, g + 1)
                nc.tensor.matmul(h_ps[g % 2][:, q * D:(q + 1) * D], item[:, c % 2, k * P:(k + 1) * P], w_item[:],
                                 start=True, stop=False)
                last = nc.tensor.matmul(h_ps[g % 2][:, q * D:(q + 1) * D], s["ones"][0:1, :], b_row[:],
                                        start=False, stop=True)
                if k == CT - 1 or t == NT - 1:
                    last.then_inc(item_used, 1)
                elif q == 3:
                    last.then_inc(h_ready, 1)
                if (q == 3 or t == NT - 1) and (k == CT - 1 or t == NT - 1):
                    pe.wait_ge(item_used, c + 1)
                    pe.sem_inc(h_ready, 1)

        @block.scalar
        def _(act):
            with act.Fori(0, NUB) as b:
                hold(act, centred, b + 1, held)
                nc.scalar.activation(sq[:, bass.ds(b * UB, UB)], xc[:, bass.ds(b * UB, UB)], ACT.Square).then_inc(squared, 1)
            with act.Fori(0, NUB // 2) as i:
                nc.scalar.preload_act_table_set("natural_log_exp_and_others")
                for u in range(2):
                    hold(act, var_ready, 2 * i + u + 1, held)
                    nc.scalar.activation(sq[:, bass.ds((2 * i + u) * UB, UB)], var_ps[u][:, 0:UB], ACT.Ln,
                                         bias=s["eps"][:, 0:1]).then_inc(var_free, 1)
                    hold(act, var_free, 2 * i + u + 3, held)
                    nc.scalar.activation(sq[:, bass.ds((2 * i + u) * UB, UB)], sq[:, bass.ds((2 * i + u) * UB, UB)],
                                         ACT.Exp, scale=-0.5).then_inc(rstd_ready, 1)
            for g in range(-(-NT // 4)):
                act.wait_ge(h_ready, g + 1)
                w = min(4, NT - 4 * g)
                nc.scalar.copy(s["h"][:, 4 * g:4 * g + w, :].rearrange("p t d -> p (t d)"),
                               h_ps[g % 2][:, 0:w * D]).then_inc(h_free, 1)

        @block.vector
        def _(dve):
            with dve.Fori(0, NUB // 2) as i:
                for u in range(2):
                    dve.wait_ge(mean_ready, 2 * i + u + 1)
                    nc.vector.tensor_tensor(xc[:, bass.ds((2 * i + u) * UB, UB)], xc[:, bass.ds((2 * i + u) * UB, UB)],
                                            mean_ps[u][:, 0:UB], ALU.subtract).then_inc(centred, 1)
                    dve.wait_ge(centred, 2 * i + u + 1)
                    dve.sem_inc(mean_free, 1)

            steps = [0]

            def step(ins):
                steps[0] += 1
                ins.then_inc(key_step, 1)
                dve.wait_ge(key_step, steps[0])

            dst, src, apart, loops = (s["keys"][:, n, :] for n in range(4))
            flags = apart.bitcast(F32)
            dve.wait_ge(dst_in, 16)
            step(nc.vector.tensor_scalar(flags, dst, float(N), None, ALU.is_lt))
            step(nc.vector.tensor_reduce(count[:, 8:9], flags, AX.X, ALU.add))
            dve.wait_ge(src_in, 16)
            step(nc.vector.scalar_tensor_tensor(out=flags, in0=src, scalar=float(N - 1), in1=flags, op0=ALU.is_lt, op1=ALU.mult))
            step(nc.vector.tensor_reduce(count[:, 9:10], flags, AX.X, ALU.add))
            dve.sem_inc(counted, 1)
            step(nc.vector.tensor_scalar(apart, flags, -float(APART), float(APART), ALU.mult, ALU.add))
            step(nc.vector.tensor_scalar(dst, dst, FIELD, None, ALU.min))
            step(nc.vector.tensor_scalar(src, src, N - 1, 1, ALU.min, ALU.add))
            step(nc.vector.tensor_tensor(dst, dst, apart, ALU.bitwise_or))
            step(nc.vector.tensor_scalar(dst, dst, DST_SHIFT, KEY_BASE, ALU.logical_shift_left, ALU.bitwise_or))
            step(nc.vector.tensor_tensor(dst, dst, src, ALU.bitwise_or))
            dve.wait_ge(loops_made, 1)
            step(nc.vector.tensor_scalar(apart, loops, float(N), float(DST_FIELD), ALU.is_ge, ALU.mult))
            step(nc.vector.scalar_tensor_tensor(out=loops, in0=loops, scalar=float(DST_FIELD), in1=apart, op0=ALU.min, op1=ALU.max))
            step(nc.vector.tensor_scalar(loops, loops, DST_SHIFT, KEY_BASE, ALU.logical_shift_left, ALU.bitwise_or))
            with dve.Fori(0, NUB) as b:
                dve.wait_ge(rstd_ready, b + 1)
                nc.vector.tensor_tensor(xc[:, bass.ds(b * UB, UB)], xc[:, bass.ds(b * UB, UB)],
                                        sq[:, bass.ds(b * UB, UB)], ALU.mult).then_inc(normed, 1)
            dve.wait_ge(total_ready, 1)
            step(nc.vector.tensor_copy(totals[:, 0:2], tot_ps[:, 0:2]))
            step(nc.vector.tensor_scalar(total_i[:], totals[:, 1:2], float(N), None, ALU.add))
            step(nc.vector.tensor_scalar(s["apart_first"][:], total_i[:], 7, None, ALU.logical_shift_right))
            step(nc.vector.tensor_scalar(total_i[:], total_i[:], 14, None, ALU.logical_shift_right))
            step(nc.vector.tensor_scalar(s["chunks"][:], total_i[:], 1, None, ALU.add))
            step(nc.vector.tensor_tensor(totals[:, 0:1], totals[:, 0:1], totals[:, 1:2], ALU.subtract))
            step(nc.vector.tensor_scalar(total_i[:], totals[:, 0:1], float(P), None, ALU.add))
            step(nc.vector.tensor_scalar(total_i[:], total_i[:], 14, None, ALU.logical_shift_right))
            step(nc.vector.tensor_scalar(totals[:, 0:1], total_i[:], 1.0, None, ALU.add))
            step(nc.vector.tensor_copy(totals[:, 1:2], s["chunks"][:]))
            step(nc.vector.reciprocal(totals[:, 2:3], totals[:, 1:2]))
            step(nc.vector.tensor_tensor(total_i[:], totals[:, 0:1], totals[:, 2:3], ALU.mult))
            step(nc.vector.tensor_scalar(s["apart_each"][:], total_i[:], 1, None, ALU.add))
            step(nc.vector.tensor_tensor(s["apart_all"][:], s["apart_each"][:], s["chunks"][:], ALU.mult))
            dve.wait_ge(consts, 1)
            step(nc.vector.tensor_tensor(s["row_first"][:], part_i[:], s["chunks"][:], ALU.mult))
            for r in range(LOGP):
                step(nc.vector.tensor_scalar(bits[:, r:r + 1], part_i[:], r, 1, ALU.logical_shift_right, ALU.bitwise_and))
            step(nc.vector.tensor_scalar(s["sign"][:], bits[:], -2.0, 1.0, ALU.mult, ALU.add))


def first_pass(nc, shared, adj_t, w_user_t, b_user, y0_dram, r_dram, keys_dram, rows_dram, sums_dram):
    with ExitStack() as ctx:
        sb = lambda name, shape, dt=F32: ctx.enter_context(nc.sbuf_tensor(name, shape, dt))
        pb = lambda name, shape: ctx.enter_context(nc.psum_tensor(name, shape, F32))
        sem = lambda name: keep(shared, ctx.enter_context(nc.semaphore(name)))
        s = shared
        adj = sb("f_adj", [P, NBUF, CT * UB])
        y = sb("f_y", [P, UB])
        r = sb("f_r", [P, UB])
        w_user = sb("f_w_user", [P, D])
        b_u = sb("f_b_user", [P, 1])
        cur = sb("f_cur", [P, CH], I32)
        nxt = sb("f_nxt", [P, CH], I32)
        dst = sb("f_dst", [P, CH + 1], I32)
        same = sb("f_same", [P, CH], I32)
        target = sb("f_target", [P, CH], I32)
        place = sb("f_place", [P, CH], I32)
        row_cur = sb("f_row_cur", [P, 1], I32)
        row_nxt = sb("f_row_nxt", [P, 1], I32)
        blank = sb("f_blank", [P, BLANK])
        acc = pb("f_acc", [P, 512])
        tp = [pb(f"f_tp{n}", [P, 512]) for n in range(4)]

        adj_in = [sem(f"f_adj_in{n}") for n in range(NBUF)]
        adj_used = sem("f_adj_used")
        small_in = sem("f_small_in")
        y_in = sem("f_y_in")
        acc_free, acc_ready = sem("f_acc_free"), sem("f_acc_ready")
        r_stored = sem("f_r_stored")
        blank_made, blanks_stored = sem("f_blank_made"), pool_sem(nc, s, "f_blanks_stored")
        sorted_step = sem("f_sorted_step")
        unflipped = sem("f_unflipped")
        turned, turn_free = sem("f_turned"), sem("f_turn_free")
        place_made = sem("f_place_made")
        keys_stored = pool_sem(nc, s, "f_keys_stored")
        row_ready = sem("f_row_ready")
        chunk_in = pool_sem(nc, s, "f_chunk_in")
        ends_ready = sem("f_ends_ready")
        index_step = sem("f_index_step")
        rows_stored = pool_sem(nc, s, "f_rows_stored")
        ends_stored = pool_sem(nc, s, "f_ends_stored")
        held = sem("f_held")
        tail_made = sem("f_tail_made")
        block = ctx.enter_context(nc.Block())

        K = [s["keys"][:, n, :].bitcast(F32) for n in range(4)]
        KI = [s["keys"][:, n, :] for n in range(4)]

        done_rows, done_cols = {}, {}
        n = 0
        for k in range(1, LOGR):
            n += k
        n += 1 + LOGR
        done_rows[12] = n
        for k in range(13, 20):
            n += k - LOGP
            done_cols[k] = n
            n += LOGP
            done_rows[k] = n
        n += 1
        merge_first = n
        n += 12
        done_cols[20] = n
        n += LOGP
        done_rows[20] = n

        @block.sync
        def _(sp):
            def load(ub, c):
                w = min(CT, NT - c * CT) * UB
                sp.dma_start(adj[:, c % NBUF, 0:w], adj_t[ub, :, c * CT * UB:c * CT * UB + w]
                             if isinstance(ub, int) else
                             adj_t[bass.ds(ub, 1), :, c * CT * UB:c * CT * UB + w].rearrange("o p n -> (o p) n")
                             ).then_inc(adj_in[c % NBUF], 16)
            for c in range(NCH):
                if c >= NBUF:
                    sp.wait_ge(adj_used, c - NBUF + 1)
                load(0, c)
            with sp.Fori(1, NUB) as ub:
                for c in range(NCH):
                    sp.wait_ge(adj_used, NCH * ub + (c - NBUF + 1))
                    load(ub, c)

        @block.tensor
        def _(pe):
            pe.sem_inc(acc_free, 1)
            pe.sem_inc(turn_free, 4)

            def products(ub, first, last):
                for c in range(first, last):
                    pe.wait_ge(adj_in[c % NBUF], 32 * ub + 16 * (c // NBUF + 1))
                    if c == 0:
                        pe.wait_ge(acc_free, ub + 1)
                    w = min(CT, NT - c * CT)
                    for k in range(w):
                        ins = nc.tensor.matmul(acc[:, 0:UB], s["h"][:, c * CT + k, :], adj[:, c % NBUF, k * UB:(k + 1) * UB],
                                               start=(c == 0 and k == 0), stop=False)
                    ins.then_inc(adj_used, 1)
                if last == NCH:
                    pe.wait_ge(y_in, 16 * ub + 16)
                    nc.tensor.matmul(acc[:, 0:UB], w_user[:], y[:], start=False, stop=True).then_inc(acc_ready, 1)

            def turn(src, group):
                for q in range(8):
                    pe.wait_ge(turn_free, group + (q + 1))
                    for m in range(4):
                        b = 4 * q + m
                        ins = nc.tensor.transpose(tp[q % 4][:, m * P:(m + 1) * P], src[:, b * P:(b + 1) * P], s["ident"][:])
                    ins.then_inc(turned, 1)

            pe.wait_ge(small_in, 32)
            with pe.Fori(0, BEFORE) as ub:
                products(ub, 0, NCH)
            for pair in range(3):
                for v in range(2):
                    k = 13 + 2 * pair + v
                    ub = BEFORE + 2 * pair + v
                    pe.wait_ge(unflipped, k - 12)
                    turn(K[0], 16 * (k - 13))
                    products(ub, 0, CUT)
                    pe.wait_ge(sorted_step, done_cols[k])
                    turn(K[1], 16 * (k - 13) + 8)
                    products(ub, CUT, NCH)
            pe.wait_ge(unflipped, 7)
            turn(K[0], 96)
            products(BEFORE + 6, 0, CUT + 1)
            pe.wait_ge(sorted_step, done_cols[19])
            turn(K[1], 104)
            products(BEFORE + 6, CUT + 1, NCH)
            pe.wait_ge(sorted_step, merge_first)
            turn(K[1], 112)
            turn(K[2], 120)
            products(BEFORE + 7, 0, NCH)
            products(BEFORE + 8, 0, 4)
            pe.wait_ge(sorted_step, done_cols[20])
            turn(K[0], 128)
            turn(K[3], 136)
            products(BEFORE + 8, 4, NCH)
            with pe.Fori(BEFORE + 9, NUB) as ub:
                products(ub, 0, NCH)

        @block.scalar
        def _(act):
            act.dma_start(w_user[:], w_user_t).then_inc(small_in, 16)
            act.dma_start(b_u[:], b_user).then_inc(small_in, 16)
            act.dma_start(y[:], y0_dram[:, 0:UB]).then_inc(y_in, 16)
            act.wait_ge(small_in, 32)
            act.sem_inc(r_stored, 16)

            def finish(ub, more):
                act.wait_ge(acc_ready, ub + 1)
                act.wait_ge(r_stored, 16 * ub + 16)
                if more:
                    act.dma_start(y[:], y0_dram[:, bass.ds((ub + 1) * UB, UB)]).then_inc(y_in, 16)
                nc.scalar.activation(r[:], acc[:, 0:UB], ACT.Relu, bias=b_u[:, 0:1]).then_inc(acc_free, 1)
                act.wait_ge(acc_free, ub + 2)
                act.dma_start(r_dram[:, bass.ds(ub * UB, UB)], r[:]).then_inc(r_stored, 16)

            def unturn(dst, group, sign=None):
                for q in range(8):
                    act.wait_ge(turned, group + (q + 1))
                    if sign is None:
                        nc.scalar.copy(dst[:, q * 512:(q + 1) * 512], tp[q % 4][:]).then_inc(turn_free, 1)
                    else:
                        nc.scalar.mul(dst[:, q * 512:(q + 1) * 512], tp[q % 4][:], sign).then_inc(turn_free, 1)

            with act.Fori(0, BEFORE) as ub:
                finish(ub, True)
            for k in range(13, 20):
                act.wait_ge(sorted_step, done_rows[k - 1])
                nc.scalar.mul(K[0], K[0], s["sign"][:, k - 13:k - 12]).then_inc(unflipped, 1)
                unturn(K[1] if (k - LOGP) % 2 == 0 else K[2], 16 * (k - 13))
                unturn(K[2], 16 * (k - 13) + 8, s["sign"][:, k - 12:k - 11] if k < 19 else None)
                finish(k - 13 + BEFORE, True)
            unturn(K[0], 112)
            unturn(K[3], 120)
            finish(BEFORE + 7, True)
            unturn(K[1], 128)
            unturn(K[2], 136)
            finish(BEFORE + 8, True)
            with act.Fori(BEFORE + 9, NUB - 1) as ub:
                finish(ub, True)
            finish(NUB - 1, False)
            act.wait_ge(r_stored, 16 * NUB + 16)

        @block.vector
        def _(dve):
            steps = [0]

            def exchange(pairs):
                for lo_in, hi_in, lo_out, hi_out, up in pairs:
                    nc.vector.tensor_tensor(lo_out, lo_in, hi_in, ALU.min if up else ALU.max)
                    ins = nc.vector.tensor_tensor(hi_out, lo_in, hi_in, ALU.max if up else ALU.min)
                steps[0] += 1
                ins.then_inc(sorted_step, 1)
                dve.wait_ge(sorted_step, steps[0])

            def stage(bufs_in, bufs_out, b, k):
                pairs = []
                for i, o in zip(bufs_in, bufs_out):
                    for (li, hi, up), (lo, ho, _) in zip(stage_views(i, b, k, LOGR), stage_views(o, b, k, LOGR)):
                        pairs.append((li, hi, lo, ho, up))
                exchange(pairs)

            at = 0
            for k in range(1, LOGR):
                for b in reversed(range(k)):
                    stage([K[at]], [K[1 - at]], b, k)
                    at = 1 - at
            assert at == 0
            nc.vector.tensor_scalar(K[0], K[0], s["sign"][:, 0:1], None, ALU.mult).then_inc(sorted_step, 1)
            steps[0] += 1
            dve.wait_ge(sorted_step, steps[0])
            for b in reversed(range(LOGR)):
                stage([K[at]], [K[1 - at]], b, None)
                at = 1 - at
            assert at == 0 and steps[0] == done_rows[12]
            for k in range(13, 20):
                dve.wait_ge(turn_free, 4 + 16 * (k - 13) + 8)
                at = 1 if (k - LOGP) % 2 == 0 else 2
                for b in reversed(range(LOGP, k)):
                    place_bit = b - LOGR if b >= LOGR else b
                    stage([K[at]], [K[3 - at]], place_bit, k - LOGR if k < 19 else None)
                    at = 3 - at
                assert at == 1 and steps[0] == done_cols[k]
                dve.wait_ge(turn_free, 4 + 16 * (k - 13) + 16)
                at = 2
                for b in reversed(range(LOGP)):
                    stage([K[at]], [K[2 - at]], b, None)
                    at = 2 - at
                assert at == 0 and steps[0] == done_rows[k]
            exchange([(K[0], K[3], K[1], K[2], True)])
            dve.wait_ge(turn_free, 4 + 128)
            a, o = [K[0], K[3]], [K[1], K[2]]
            for b in reversed(range(LOGP, 19)):
                stage(a, o, b - LOGR if b >= LOGR else b, None)
                a, o = o, a
            dve.wait_ge(turn_free, 4 + 144)
            a, o = [K[1], K[2]], [K[0], K[3]]
            for b in reversed(range(LOGP)):
                stage(a, o, b, None)
                a, o = o, a
            assert steps[0] == done_rows[20]

            nc.vector.memset(KI[1], KEY_BASE | DST_FIELD << DST_SHIFT).then_inc(tail_made, 1)

            count = dve.value_load(s["chunks"][0:1, 0:1], min_val=1, max_val=CHMAX)
            nc.vector.tensor_copy(row_cur[:], s["row_first"][:])
            nc.vector.tensor_scalar(row_nxt[:], s["row_first"][:], 1, None, ALU.add).then_inc(row_ready, 1)
            dve.wait_ge(place_made, 1)
            with dve.Fori(0, count) as i:
                dve.wait_ge(chunk_in, 32 * i + 32)
                nc.vector.tensor_scalar(row_cur[:], row_cur[:], 1, None, ALU.add)
                nc.vector.tensor_scalar(row_nxt[:], row_nxt[:], 1, None, ALU.add)
                nc.vector.tensor_scalar(dst[:, 0:CH], cur[:], DST_SHIFT, DST_FIELD, ALU.logical_shift_right, ALU.bitwise_and)
                nc.vector.tensor_scalar(dst[:, CH:CH + 1], nxt[:, 0:1], DST_SHIFT, DST_FIELD, ALU.logical_shift_right,
                                        ALU.bitwise_and).then_inc(index_step, 1)
                dve.wait_ge(index_step, 3 * i + 1)
                nc.vector.tensor_tensor(same[:], dst[:, 0:CH], dst[:, 1:CH + 1], ALU.is_equal).then_inc(index_step, 1)
                dve.wait_ge(index_step, 3 * i + 2)
                nc.vector.scalar_tensor_tensor(out=target[:], in0=same[:], scalar=float(BIG), in1=dst[:, 0:CH],
                                               op0=ALU.mult, op1=ALU.add)
                nc.vector.tensor_scalar(place[:], place[:], CH, None, ALU.add).then_inc(index_step, 1)
                dve.wait_ge(index_step, 3 * i + 3)
                dve.sem_inc(ends_ready, 1)
                dve.wait_ge(ends_stored, i * (16 * CH) + 16 * CH)
                dve.sem_inc(row_ready, 1)

        @block.gpsimd
        def _(pool):
            nc.gpsimd.iota(place[:], [[1, CH]], base=-CH, channel_multiplier=RMAX).then_inc(place_made, 1)
            nc.gpsimd.memset(blank[:], 0.0).then_inc(blank_made, 1)
            pool.wait_ge(blank_made, 1)
            sums_flat = sums_dram.rearrange("(p c) f -> p (c f)", p=P)
            with pool.Fori(0, RMAX * STW // BLANK) as i:
                pool.dma_start(sums_flat[:, bass.ds(i * BLANK, BLANK)], blank[:]).then_inc(blanks_stored, 16)
            pool.wait_ge(blanks_stored, RMAX * STW // BLANK * 16)
            pool.wait_ge(sorted_step, done_rows[20])
            for half, n in ((0, 0), (1, 3)):
                pool.dma_start(keys_dram[half * E:(half + 1) * E].rearrange("(p j) -> p j", p=P), KI[n]).then_inc(keys_stored, 16)
            pool.wait_ge(tail_made, 1)
            pool.dma_start(keys_dram[2 * E:3 * E].rearrange("(p j) -> p j", p=P), KI[1]).then_inc(keys_stored, 16)
            pool.wait_ge(keys_stored, 48)
            count = pool.value_load(s["chunks"][0:1, 0:1], min_val=1, max_val=CHMAX)
            by_chunk = keys_dram.rearrange("(n j) -> n j", j=CH)
            with pool.Fori(0, count) as i:
                hold(pool, row_ready, i + 1, held)
                pool.indirect_dma_start(cur[:], None, by_chunk, bass.IndirectOffsetOnAxis(ap=row_cur[:, 0:1], axis=0)).then_inc(chunk_in, 16)
                pool.indirect_dma_start(nxt[:], None, by_chunk, bass.IndirectOffsetOnAxis(ap=row_nxt[:, 0:1], axis=0)).then_inc(chunk_in, 16)
                pool.wait_ge(chunk_in, 32 * i + 32)
                pool.dma_start(rows_dram[:, bass.ds(i * CH, CH)], cur[:]).then_inc(rows_stored, 16)
                hold(pool, ends_ready, i + 1, held)
                for j in range(CH):
                    pool.indirect_dma_start(s["end_id"], bass.IndirectOffsetOnAxis(ap=target[:, j:j + 1], axis=0),
                                            place[:, j:j + 1], None, bounds_check=N - 1, oob_is_err=False).then_inc(ends_stored, 16)
                hold(pool, rows_stored, 16 * i + 16, held)
            pool.dma_start(rows_dram[:, bass.ds(count * CH, CH)], cur[:]).then_inc(rows_stored, 16)
            hold(pool, rows_stored, 16 * count + 16, held)
            hold(pool, ends_stored, count * (16 * CH), held)


def layernorm(nc, shared, name, add=None):
    with ExitStack() as ctx:
        sb = lambda what, shape, dt=F32: ctx.enter_context(nc.sbuf_tensor(f"{name}_{what}", shape, dt))
        pb = lambda what, shape: ctx.enter_context(nc.psum_tensor(f"{name}_{what}", shape, F32))
        sem = lambda what: keep(shared, ctx.enter_context(nc.semaphore(f"{name}_{what}")))
        s = shared
        x, y = s["x"], s["y"]
        sq = sb("sq", [P, N])
        mean_ps = [pb(f"mean{u}", [P, 512]) for u in range(2)]
        var_ps = [pb(f"var{u}", [P, 512]) for u in range(2)]
        held, added = sem("held"), sem("added")
        add_in = [sem(f"add_in{part}") for part in range(PARTS)] if add is not None else None
        centred, squared, normed = sem("centred"), sem("squared"), sem("normed")
        mean_free, mean_ready, var_free, var_ready = sem("mean_free"), sem("mean_ready"), sem("var_free"), sem("var_ready")
        rstd_ready = sem("rstd_ready")
        block = ctx.enter_context(nc.Block())
        at = lambda t, b: t[:, bass.ds(b * UB, UB)]

        @block.sync
        def _(sp):
            if add is not None:
                for part in range(PARTS):
                    cols = slice(part * (N // PARTS), (part + 1) * (N // PARTS))
                    sp.dma_start(x[:, cols], s["x_in"][:, cols]).then_inc(add_in[part], 16)
                    sp.dma_start(y[:, cols], add[:, cols]).then_inc(add_in[part], 16)
                for part in range(PARTS):
                    sp.wait_ge(add_in[part], 32)

        @block.tensor
        def _(pe):
            pe.sem_inc(mean_free, 2)
            pe.sem_inc(var_free, 2)
            with pe.Fori(0, NUB // 2) as i:
                for u in range(2):
                    b = 2 * i + u
                    pe.wait_ge(mean_free, b + 1)
                    if add is not None:
                        pe.wait_ge(added, b + 1)
                    nc.tensor.matmul(mean_ps[u][:, 0:UB], s["mean_w"][:], at(x, b), start=True, stop=True).then_inc(mean_ready, 1)
            with pe.Fori(0, NUB // 2) as i:
                for u in range(2):
                    b = 2 * i + u
                    pe.wait_ge(var_free, b + 1)
                    pe.wait_ge(squared, b + 1)
                    nc.tensor.matmul(var_ps[u][:, 0:UB], s["mean_w"][:], at(sq, b), start=True, stop=True).then_inc(var_ready, 1)

        @block.scalar
        def _(act):
            with act.Fori(0, NUB) as b:
                hold(act, centred, b + 1, held)
                nc.scalar.activation(at(sq, b), at(y, b), ACT.Square).then_inc(squared, 1)
            with act.Fori(0, NUB // 2) as i:
                nc.scalar.preload_act_table_set("natural_log_exp_and_others")
                for u in range(2):
                    b = 2 * i + u
                    hold(act, var_ready, b + 1, held)
                    nc.scalar.activation(at(sq, b), var_ps[u][:, 0:UB], ACT.Ln, bias=s["eps"][:, 0:1]).then_inc(var_free, 1)
                    hold(act, var_free, b + 3, held)
                    nc.scalar.activation(at(sq, b), at(sq, b), ACT.Exp, scale=-0.5).then_inc(rstd_ready, 1)

        @block.vector
        def _(dve):
            if add is not None:
                nc.vector.memset(y[:, N:NPAD], 0.0)

            def centre(i):
                if add is not None:
                    for u in range(2):
                        b = 2 * i + u
                        nc.vector.tensor_tensor(at(x, b), at(x, b), at(y, b), ALU.add).then_inc(added, 1)
                for u in range(2):
                    b = 2 * i + u
                    dve.wait_ge(mean_ready, b + 1)
                    nc.vector.tensor_tensor(at(y, b), at(x, b), mean_ps[u][:, 0:UB], ALU.subtract).then_inc(centred, 1)
                    dve.wait_ge(centred, b + 1)
                    dve.sem_inc(mean_free, 1)

            for part in range(PARTS):
                if add is not None:
                    dve.wait_ge(add_in[part], 32)
                with dve.Fori(part * (NUB // 2 // PARTS), (part + 1) * (NUB // 2 // PARTS)) as i:
                    centre(i)
            with dve.Fori(0, NUB) as b:
                dve.wait_ge(rstd_ready, b + 1)
                nc.vector.tensor_tensor(at(y, b), at(y, b), at(sq, b), ALU.mult).then_inc(normed, 1)


def node_table(nc, shared, w_gat, att_src, att_dst):
    with ExitStack() as ctx:
        sb = lambda name, shape, dt=F32: ctx.enter_context(nc.sbuf_tensor(name, shape, dt))
        pb = lambda name, shape: ctx.enter_context(nc.psum_tensor(name, shape, F32))
        sem = lambda name: keep(shared, ctx.enter_context(nc.semaphore(name)))
        s = shared
        w = sb("n_w", [P, H0 * C0])
        att = sb("n_att", [P, 2, H0 * C0])
        table = sb("n_table", [P, NT, TABW])
        prod = sb("n_prod", [P, NT, H0 * C0])
        h_ps = pb("n_h", [P, 3, 512])
        small_in, h_ready, padded = sem("n_small_in"), sem("n_h_ready"), sem("n_padded")
        step_done, table_ready, table_stored = sem("n_step"), sem("n_table_ready"), sem("n_table_stored")
        block = ctx.enter_context(nc.Block())

        @block.sync
        def _(sp):
            sp.dma_start(w[:], w_gat).then_inc(small_in, 16)
            for n, v in enumerate((att_src, att_dst)):
                sp.dma_start(att[:, n, :], v.to_broadcast([P, H0 * C0])).then_inc(small_in, 16)
            sp.wait_ge(table_ready, 1)
            sp.dma_start(s["table"].rearrange("(p t) f -> p (t f)", p=P), table[:].rearrange("p t f -> p (t f)")).then_inc(table_stored, 16)
            sp.wait_ge(table_stored, 16)

        @block.gpsimd
        def _(pool):
            for k in range(H0):
                ins = nc.gpsimd.memset(table[:, :, k * HC + C0:k * HC + HC], 1.0)
            ins.then_inc(padded, 1)

        @block.tensor
        def _(pe):
            pe.wait_ge(small_in, 48)
            by_tile = s["y"][:].rearrange("p (n t) -> p t n", t=NT)
            for t in range(NT):
                at = t % 32 * 16
                ins = nc.tensor.matmul(h_ps[:, t // 32, at:at + 16], by_tile[:, t, :], w[:], start=True, stop=True)
            ins.then_inc(h_ready, 1)

        @block.vector
        def _(dve):
            steps = [0]

            def step(ins):
                steps[0] += 1
                ins.then_inc(step_done, 1)
                dve.wait_ge(step_done, steps[0])

            dve.wait_ge(h_ready, 1)
            dve.wait_ge(padded, 1)
            dve.wait_ge(small_in, 48)
            for g in range(3):
                n = min(32, NT - 32 * g)
                ins = nc.vector.tensor_copy(
                    table[:, 32 * g:32 * g + n, 0:NF].rearrange("p t (k c) -> p t k c", c=HC)[:, :, :, 0:C0],
                    h_ps[:, g, 0:16 * n].rearrange("p (t k c) -> p t k c", k=H0, c=C0))
            step(ins)
            heads = table[:, :, 0:NF].rearrange("p t (k c) -> p t k c", c=HC)[:, :, :, 0:C0]
            for n in range(2):
                for k in range(H0):
                    ins = nc.vector.tensor_tensor(
                        prod[:, :, k * C0:(k + 1) * C0], heads[:, :, k, :],
                        att[:, n:n + 1, k * C0:(k + 1) * C0].to_broadcast([P, NT, C0]), ALU.mult)
                step(ins)
                step(nc.vector.tensor_reduce(table[:, :, NF + n * H0:NF + n * H0 + H0],
                                             prod[:].rearrange("p t (k c) -> p t k c", c=C0), AX.X, ALU.add))
            dve.sem_inc(table_ready, 1)


def attend(nc, shared, keys_dram, rows_dram, sums_dram, counts_dram):
    with ExitStack() as ctx:
        sb = lambda name, shape, dt=F32: ctx.enter_context(nc.sbuf_tensor(name, shape, dt))
        pb = lambda name, shape: ctx.enter_context(nc.psum_tensor(name, shape, F32))
        sem = lambda name: keep(shared, ctx.enter_context(nc.semaphore(name)))
        s = shared
        keys = [sb(f"a_keys{u}", [P, HF], I32) for u in range(2)]
        field = sb("a_field", [P, HF], I32)
        dst = sb("a_dst", [P, HF], I32)
        is_loop = sb("a_is_loop", [P, HF], I32)
        index = [sb(f"a_index{u}", [P, HF], I32) for u in range(2)]
        first = [sb(f"a_first{u}", [P, HF]) for u in range(2)]
        rest_ = [sb(f"a_rest{u}", [P, HF]) for u in range(2)]
        wall = [sb(f"a_wall{u}", [P, HF]) for u in range(2)]
        got = [sb(f"a_got{u}", [P, HF, TABW]) for u in range(2)]
        start = sb("a_start", [P, H0, HF])
        a_dst = [sb(f"a_a_dst{u}", [P, H0, HF]) for u in range(2)]
        score = sb("a_score", [P, H0, HF])
        top = [sb(f"a_top{u}", [P, H0, HF + 1]) for u in range(2)]
        weight = sb("a_weight", [P, 2, H0, HF])
        value = sb("a_value", [P, NF, HF])
        sums = [sb(f"a_sums{u}", [P, HF, STW]) for u in range(2)]
        apart = sb("a_apart", [P, CH], I32)
        part = sb("a_part", [P, 2, CH], I32)
        part_b = sb("a_part_b", [P, 2, CH], BF16)
        line = sb("a_line", [P, 2, P], BF16)
        line_i = sb("a_line_i", [P, 2, P], I32)
        hot = [sb(f"a_hot{u}", [P, HOT, P + NT], BF16) for u in range(2)]
        nought = sb("a_nought", [P, P], BF16)
        counts = sb("a_counts", [P, NT])
        counts_t = sb("a_counts_t", [NT, P])
        counts_ps = pb("a_counts_ps", [P, 512])
        counts_t_ps = pb("a_counts_t_ps", [P, 512])
        row_key = sb("a_row_key", [P, 1], I32)
        row_dst = sb("a_row_dst", [P, 1], I32)
        row_index = sb("a_row_index", [P, 1], I32)
        row_got = sb("a_row_got", [P, TABW])
        tail = sb("a_tail", [P, 4, NF])
        rows = sb("a_rows", [NF, 4, P])
        join = sb("a_join", [NF, 8, P])
        run_top = sb("a_run_top", [NF, P + 1])
        run_sum = sb("a_run_sum", [NF, P + 1])
        carry = sb("a_carry", [P, 3, NF])
        last_key = sb("a_last_key", [P, 1], I32)
        last_dst = sb("a_last_dst", [P, 1], I32)
        end_f = sb("a_end_f", [P, 2])
        place_f = sb("a_place_f", [P, 1])
        target_f = sb("a_target_f", [P, 1])
        place = sb("a_place", [P, 1], I32)
        target = sb("a_target", [P, 1], I32)
        ended = sb("a_ended", [P, STW])
        mix = sb("a_mix", [P, 6, NF])
        tr_ps = pb("a_tr", [P, 4, P])
        back_ps = pb("a_back", [P, 4, P])

        held = sem("a_held")
        apart_in, apart_used = sem("a_apart_in"), sem("a_apart_used")
        line_made, part_step, hot_ready, hot_used = sem("a_line_made"), sem("a_part_step"), sem("a_hot_ready"), sem("a_hot_used")
        counts_ready, counts_out, counts_turned = sem("a_counts_ready"), sem("a_counts_out"), sem("a_counts_turned")
        counts_back, counts_stored = sem("a_counts_back"), sem("a_counts_stored")
        keys_in = [sem(f"a_keys_in{u}") for u in range(2)]
        keys_used = sem("a_keys_used")
        row_in, row_ready, row_got_in, row_set = sem("a_row_in"), sem("a_row_ready"), pool_sem(nc, s, "a_row_got_in"), sem("a_row_set")
        index_ready, got_in, got_used = sem("a_index_ready"), [pool_sem(nc, s, f"a_got_in{u}") for u in range(2)], sem("a_got_used")
        prep_step, main_step = sem("a_prep_step"), sem("a_main_step")
        gaps_ready, weights_ready = sem("a_gaps_ready"), sem("a_weights_ready")
        sums_ready, sums_stored = sem("a_sums_ready"), [sem(f"a_sums_stored{u}") for u in range(2)]
        end_step, tails_ready, turned = sem("a_end_step"), sem("a_tails_ready"), sem("a_turned")
        gap_ready, gap_exp, carry_ready, carry_turned = sem("a_gap_ready"), sem("a_gap_exp"), sem("a_carry_ready"), sem("a_carry_turned")
        place_in, ended_in, mix_ready, mix_exp = pool_sem(nc, s, "a_place_in"), pool_sem(nc, s, "a_ended_in"), sem("a_mix_ready"), sem("a_mix_exp")
        last_in = sem("a_last_in")
        fixed, fixed_stored, edges_done = sem("a_fixed"), pool_sem(nc, s, "a_fixed_stored"), sem("a_edges_done")
        block = ctx.enter_context(nc.Block())
        sums_flat = sums_dram.rearrange("(p c) f -> p (c f)", p=P)

        @block.sync
        def _(sp):
            count = sp.value_load(s["chunks"][0:1, 0:1], min_val=1, max_val=CHMAX)
            sp.dma_start(row_key[:], rows_dram[:, 0:1], allow_slow_non_contiguous=True).then_inc(row_in, 16)
            for u in range(2):
                sp.dma_start(keys[u][:], rows_dram[:, u * HF:(u + 1) * HF]).then_inc(keys_in[u], 16)
                sp.sem_inc(sums_stored[u], 16)
            with sp.Fori(0, count) as i:
                for u in range(2):
                    sp.wait_ge(keys_used, 2 * i + u + 1)
                    sp.dma_start(keys[u][:], rows_dram[:, bass.ds((i + 1) * CH + u * HF, HF)]).then_inc(keys_in[u], 16)
                    sp.wait_ge(sums_ready, 2 * i + u + 1)
                    sp.dma_start(sums_flat[:, bass.ds((i * CH + u * HF) * STW, HF * STW)],
                                 sums[u][:].rearrange("p c f -> p (c f)")).then_inc(sums_stored[u], 16)
            sp.dma_start(last_key[:], rows_dram[:, bass.ds(count * CH - 1, 1)], allow_slow_non_contiguous=True).then_inc(last_in, 16)
            for u in range(2):
                hold(sp, sums_stored[u], 16 * count + 16, held)
                hold(sp, keys_in[u], 16 * count + 16, held)
            sp.sem_inc(edges_done, 1)
            sp.wait_ge(counts_back, 1)
            sp.dma_start(counts_dram.rearrange("(t p) -> t p", p=P), counts_t[:]).then_inc(counts_stored, 16)
            sp.wait_ge(counts_stored, 16)

        @block.gpsimd
        def _(pool):
            count = pool.value_load(s["chunks"][0:1, 0:1], min_val=1, max_val=CHMAX)
            nc.gpsimd.iota(line_i[:, 0, :], [[1, P]], base=0, channel_multiplier=0)
            nc.gpsimd.iota(line_i[:, 1, :], [[1, P]], base=P, channel_multiplier=0)
            nc.gpsimd.memset(nought[:], 0.0).then_inc(line_made, 1)
            pool.wait_ge(row_ready, 1)
            pool.indirect_dma_start(row_got[:], None, s["table"], bass.IndirectOffsetOnAxis(ap=row_index[:, 0:1], axis=0)).then_inc(row_got_in, 16)
            pool.sem_inc(got_used, 2)
            with pool.Fori(0, count) as i:
                for u in range(2):
                    hold(pool, index_ready, 2 * i + u + 1, held)
                    hold(pool, got_used, 2 * i + u + 1, held)
                    for j in range(HF):
                        pool.indirect_dma_start(got[u][:, j, :], None, s["table"],
                                                bass.IndirectOffsetOnAxis(ap=index[u][:, j:j + 1], axis=0)).then_inc(got_in[u], 16)
            pool.wait_ge(edges_done, 1)
            pool.indirect_dma_start(place[:], None, s["end_id"], bass.IndirectOffsetOnAxis(ap=row_index[:, 0:1], axis=0)).then_inc(place_in, 16)
            pool.wait_ge(place_in, 16)
            pool.indirect_dma_start(ended[:], None, sums_dram, bass.IndirectOffsetOnAxis(ap=place[:, 0:1], axis=0)).then_inc(ended_in, 16)
            pool.wait_ge(fixed, 1)
            pool.indirect_dma_start(sums_dram, bass.IndirectOffsetOnAxis(ap=target[:, 0:1], axis=0), ended[:], None,
                                    bounds_check=P * RMAX - 1, oob_is_err=False).then_inc(fixed_stored, 16)
            pool.wait_ge(fixed_stored, 16)

        @block.scalar
        def _(act):
            count = act.value_load(s["chunks"][0:1, 0:1], min_val=1, max_val=CHMAX)
            each = act.value_load(s["apart_each"][0:1, 0:1], min_val=1, max_val=CHMAX + 1)
            by_chunk = keys_dram.rearrange("(n j) -> n j", j=CH)
            act.sem_inc(apart_used, 1)
            with act.Fori(0, count) as i:
                for u in range(2):
                    act.wait_ge(gaps_ready, 2 * i + u + 1)
                    nc.scalar.activation(weight[:], weight[:], ACT.Exp).then_inc(weights_ready, 1)
                    if u == 0:
                        with act.Fori(0, each) as k:
                            hold(act, apart_used, i * each + k + 1, held)
                            first = act.value_load(s["apart_first"][0:1, 0:1], min_val=0, max_val=3 * E // CH - P)
                            act.dma_start(apart[:], by_chunk[bass.ds(first, P), :]).then_inc(apart_in, 16)
            act.wait_ge(gap_ready, 1)
            nc.scalar.activation(join[:, 5:7, :], join[:, 5:7, :], ACT.Exp).then_inc(gap_exp, 1)
            act.wait_ge(mix_ready, 1)
            nc.scalar.activation(mix[:, 1:3, :], mix[:, 1:3, :], ACT.Exp).then_inc(mix_exp, 1)

        @block.vector
        def _(dve):
            count = dve.value_load(s["chunks"][0:1, 0:1], min_val=1, max_val=CHMAX)
            steps = [0]

            def step(ins, sem):
                steps[0] += 1
                ins.then_inc(sem, 1)
                dve.wait_ge(sem, steps[0])

            dve.wait_ge(row_in, 16)
            step(nc.vector.tensor_scalar(row_dst[:], row_key[:], DST_SHIFT, DST_FIELD, ALU.logical_shift_right, ALU.bitwise_and), row_set)
            step(nc.vector.tensor_scalar(row_index[:], row_dst[:], N - 1, None, ALU.min), row_set)
            dve.sem_inc(row_ready, 1)
            nc.vector.memset(top[1][:, :, HF:HF + 1], NEG)
            step(nc.vector.memset(sums[1][:, HF - 1, :], 0.0), row_set)
            dve.wait_ge(row_got_in, 16)
            step(nc.vector.tensor_copy(a_dst[1][:, :, HF - 1], row_got[:, NF + H0:TABW]), row_set)

            PREP, MAIN = 4, 9
            each_count = dve.value_load(s["apart_each"][0:1, 0:1], min_val=1, max_val=CHMAX + 1)
            dve.wait_ge(line_made, 1)
            step(nc.vector.tensor_copy(line[:], line_i[:]), row_set)

            def count_apart(n):
                dve.wait_ge(apart_in, n * 16 + 16)
                nc.vector.tensor_scalar(part[:, 0, :], apart[:], DST_SHIFT, P - 1, ALU.logical_shift_right, ALU.bitwise_and)
                nc.vector.tensor_scalar(part[:, 1, :], apart[:], DST_SHIFT + LO, 2 * P - 1, ALU.logical_shift_right,
                                        ALU.bitwise_and)
                nc.vector.tensor_scalar(s["apart_first"][:], s["apart_first"][:], P, None, ALU.add).then_inc(part_step, 1)
                dve.wait_ge(part_step, 2 * n + 1)
                dve.sem_inc(apart_used, 1)
                nc.vector.tensor_copy(part_b[:], part[:]).then_inc(part_step, 1)
                dve.wait_ge(part_step, 2 * n + 2)
                for q in range(CH // HOT):
                    dve.wait_ge(hot_used, n * (CH // HOT) + (q + 1))
                    for v, (at, w) in enumerate(((0, P), (P, NT))):
                        ins = nc.vector.tensor_tensor(
                            hot[q % 2][:, :, at:at + w],
                            part_b[:, v, q * HOT:(q + 1) * HOT].rearrange("p (j o) -> p j o", o=1).to_broadcast([P, HOT, w]),
                            line[:, v:v + 1, 0:w].to_broadcast([P, HOT, w]), ALU.is_equal)
                    ins.then_inc(hot_ready, 1)

            def prep(u, n):
                at = PREP * n

                def done(ins, k):
                    ins.then_inc(prep_step, 1)
                    dve.wait_ge(prep_step, at + k)
                dve.wait_ge(keys_in[u], 8 * n + (16 - 8 * u))
                nc.vector.tensor_scalar(field[:], keys[u][:], FIELD, None, ALU.bitwise_and)
                done(nc.vector.tensor_scalar(dst[:], keys[u][:], DST_SHIFT, DST_FIELD, ALU.logical_shift_right, ALU.bitwise_and), 1)
                nc.vector.tensor_scalar(first[u][:], field[:], 0, None, ALU.is_equal)
                done(nc.vector.tensor_scalar(is_loop[:], field[:], 0, None, ALU.is_equal), 2)
                nc.vector.tensor_scalar(rest_[u][:], first[u][:], -1.0, 1.0, ALU.mult, ALU.add)
                nc.vector.tensor_scalar(wall[u][:], first[u][:], NEG, None, ALU.mult)
                nc.vector.tensor_scalar(field[:], field[:], 1, None, ALU.subtract)
                done(nc.vector.scalar_tensor_tensor(out=dst[:], in0=dst[:], scalar=1, in1=is_loop[:], op0=ALU.add, op1=ALU.mult), 3)
                dve.sem_inc(held, 1)
                done(nc.vector.tensor_tensor(dst[:], dst[:], field[:], ALU.add), 4)
                nc.vector.tensor_scalar(index[u][:], dst[:], N - 1, None, ALU.min).then_inc(index_ready, 1)
                dve.wait_ge(index_ready, n + 1)
                dve.sem_inc(keys_used, 1)

            def halves(u, i):
                n = 2 * i + u
                at = MAIN * n
                g, t, before = got[u], top[u], 1 - u
                each = lambda v: v[:].rearrange("p (o j) -> p o j", o=1).to_broadcast([P, H0, HF])

                def done(ins, k):
                    ins.then_inc(main_step, 1)
                    dve.wait_ge(main_step, at + k)

                dve.wait_ge(got_in[u], i * (16 * HF) + 16 * HF)
                nc.vector.tensor_copy(t[:, :, 0:1], top[before][:, :, HF:HF + 1])
                done(nc.vector.tensor_tensor(start[:], g[:, :, NF + H0:TABW].rearrange("p j k -> p k j"), each(first[u]), ALU.mult), 1)
                for k in range(H0):
                    ins = nc.vector.tensor_tensor_scan(a_dst[u][:, k, :], rest_[u][:], start[:, k, :],
                                                       a_dst[before][:, k, HF - 1:HF], ALU.mult, ALU.add)
                done(ins, 2)
                done(nc.vector.tensor_tensor(start[:], g[:, :, NF:NF + H0].rearrange("p j k -> p k j"), a_dst[u][:], ALU.add), 3)
                done(nc.vector.scalar_tensor_tensor(out=score[:], in0=start[:], scalar=0.2, in1=start[:], op0=ALU.mult, op1=ALU.max), 4)
                for k in range(H0):
                    ins = nc.vector.tensor_tensor_scan(t[:, k, 1:HF + 1], wall[u][:], score[:, k, :], t[:, k, 0:1], ALU.add, ALU.max)
                done(ins, 5)
                nc.vector.tensor_tensor(weight[:, 1], score[:], t[:, :, 1:HF + 1], ALU.subtract)
                done(nc.vector.tensor_tensor(weight[:, 0], t[:, :, 0:HF], t[:, :, 1:HF + 1], ALU.subtract), 6)
                done(nc.vector.tensor_tensor(weight[:, 0], weight[:, 0], each(wall[u]), ALU.add), 7)
                dve.sem_inc(gaps_ready, 1)
                dve.wait_ge(weights_ready, n + 1)
                for k in range(H0):
                    ins = nc.vector.tensor_tensor(value[:, k * HC:(k + 1) * HC, :],
                                                  g[:, :, k * HC:(k + 1) * HC].rearrange("p j c -> p c j"),
                                                  weight[:, 1, k:k + 1, :].to_broadcast([P, HC, HF]), ALU.mult)
                done(ins, 8)
                dve.sem_inc(got_used, 1)
                dve.wait_ge(sums_stored[u], 16 * i + 16)
                for f in range(NF):
                    nc.vector.tensor_tensor_scan(sums[u][:, :, f], weight[:, 0, f // HC, :], value[:, f, :],
                                                 sums[before][:, HF - 1, f:f + 1], ALU.mult, ALU.add)
                done(nc.vector.tensor_copy(sums[u][:, :, NF:STW], t[:, :, 1:HF + 1].rearrange("p k j -> p j k")), 9)
                dve.sem_inc(sums_ready, 1)

            prep(0, 0)
            with dve.Fori(0, count) as i:
                prep(1, 2 * i + 1)
                halves(0, i)
                prep(0, 2 * i + 2)
                with dve.Fori(0, each_count) as k:
                    count_apart(i * each_count + k)
                halves(1, i)

            dve.wait_ge(counts_ready, 1)
            step(nc.vector.tensor_copy(counts[:], counts_ps[:, 0:NT]), row_set)
            dve.sem_inc(counts_out, 1)
            dve.wait_ge(counts_turned, 1)
            step(nc.vector.tensor_copy(counts_t[:], counts_t_ps[0:NT, 0:P]), row_set)
            dve.sem_inc(counts_back, 1)

            steps[0] = 0
            step = lambda ins: (steps.__setitem__(0, steps[0] + 1), ins.then_inc(end_step, 1), dve.wait_ge(end_step, steps[0]))
            dve.wait_ge(last_in, 16)
            nc.vector.tensor_copy(tail[:, 0, :], sums[1][:, HF - 1, 0:NF])
            for k in range(H0):
                nc.vector.tensor_scalar(tail[:, 1, k * HC:(k + 1) * HC], s["ones"][:, 0:HC], top[1][:, k, HF:HF + 1], None, ALU.mult)
            nc.vector.tensor_copy(end_f[:, 1:2], row_dst[:])
            step(nc.vector.tensor_scalar(last_dst[:], last_key[:], DST_SHIFT, DST_FIELD, ALU.logical_shift_right, ALU.bitwise_and))
            step(nc.vector.tensor_copy(end_f[:, 0:1], last_dst[:]))
            nc.vector.tensor_scalar(tail[:, 2, :], s["ones"][:, 0:NF], end_f[:, 0:1], None, ALU.mult)
            step(nc.vector.tensor_scalar(tail[:, 3, :], s["ones"][:, 0:NF], end_f[:, 1:2], None, ALU.mult))
            dve.sem_inc(tails_ready, 1)
            dve.wait_ge(turned, 1)
            nc.vector.memset(run_top[:, 0:1], NEG)
            nc.vector.memset(run_sum[:, 0:1], 0.0)
            nc.vector.memset(join[:, 0, 0:1], 0.0)
            nc.vector.memset(join[:, 4, P - 1:P], 0.0)
            step(nc.vector.tensor_copy(rows[:], tr_ps[0:NF, :, :]))
            S, M, T, F = (rows[:, n, :] for n in range(4))
            CONT, WHOLE, THROUGH, WALL, ON, RATIO, SHARE, PART = (join[:, n, :] for n in range(8))
            nc.vector.tensor_tensor(CONT[:, 1:P], F[:, 1:P], T[:, 0:P - 1], ALU.is_equal)
            nc.vector.tensor_tensor(ON[:, 0:P - 1], F[:, 1:P], T[:, 0:P - 1], ALU.is_equal)
            step(nc.vector.tensor_tensor(WHOLE, F, T, ALU.is_equal))
            step(nc.vector.tensor_tensor(THROUGH, CONT, WHOLE, ALU.mult))
            step(nc.vector.tensor_scalar(WALL, THROUGH, -NEG, NEG, ALU.mult, ALU.add))
            step(nc.vector.tensor_tensor_scan(run_top[:, 1:P + 1], WALL, M, NEG, ALU.add, ALU.max))
            nc.vector.tensor_tensor(SHARE, M, run_top[:, 1:P + 1], ALU.subtract)
            step(nc.vector.tensor_tensor(RATIO, run_top[:, 0:P], run_top[:, 1:P + 1], ALU.subtract))
            step(nc.vector.tensor_tensor(RATIO, RATIO, WALL, ALU.add))
            dve.sem_inc(gap_ready, 1)
            dve.wait_ge(gap_exp, 1)
            step(nc.vector.tensor_tensor(PART, S, SHARE, ALU.mult))
            nc.vector.tensor_tensor_scan(run_sum[:, 1:P + 1], RATIO, PART, 0.0, ALU.mult, ALU.add)
            step(nc.vector.tensor_tensor(THROUGH, WHOLE, ON, ALU.mult))
            step(nc.vector.tensor_scalar(THROUGH, THROUGH, -1.0, 1.0, ALU.mult, ALU.add))
            step(nc.vector.tensor_tensor(THROUGH, THROUGH, CONT, ALU.mult))
            step(nc.vector.scalar_tensor_tensor(out=THROUGH, in0=F, scalar=float(N), in1=THROUGH, op0=ALU.is_lt, op1=ALU.mult))
            dve.sem_inc(carry_ready, 1)
            dve.wait_ge(carry_turned, 1)
            step(nc.vector.tensor_copy(carry[:], back_ps[:, 0:3, 0:NF]))
            dve.wait_ge(place_in, 16)
            dve.wait_ge(ended_in, 16)
            for k in range(H0):
                nc.vector.tensor_scalar(mix[:, 0, k * HC:(k + 1) * HC], s["ones"][:, 0:HC], ended[:, NF + k:NF + k + 1], None, ALU.mult)
            nc.vector.tensor_copy(place_f[:], place[:])
            step(nc.vector.tensor_scalar(target_f[:], carry[:, 2, 0:1], -float(BIG), float(BIG), ALU.mult, ALU.add))
            nc.vector.tensor_tensor(target[:], target_f[:], place_f[:], ALU.add)
            step(nc.vector.tensor_tensor(mix[:, 3, :], mix[:, 0, :], carry[:, 0, :], ALU.max))
            nc.vector.tensor_tensor(mix[:, 1, :], mix[:, 0, :], mix[:, 3, :], ALU.subtract)
            step(nc.vector.tensor_tensor(mix[:, 2, :], carry[:, 0, :], mix[:, 3, :], ALU.subtract))
            dve.sem_inc(mix_ready, 1)
            dve.wait_ge(mix_exp, 1)
            nc.vector.tensor_tensor(mix[:, 4, :], ended[:, 0:NF], mix[:, 1, :], ALU.mult)
            step(nc.vector.tensor_tensor(mix[:, 5, :], carry[:, 1, :], mix[:, 2, :], ALU.mult))
            nc.vector.tensor_tensor(ended[:, 0:NF], mix[:, 4, :], mix[:, 5, :], ALU.add)
            step(nc.vector.tensor_copy(ended[:, NF:STW], mix[:, 3, :].rearrange("p (k c) -> p k c", c=HC)[:, :, 0]))
            dve.sem_inc(fixed, 1)

        @block.tensor
        def _(pe):
            total = pe.value_load(s["apart_all"][0:1, 0:1], min_val=1, max_val=4 * CHMAX)
            pe.sem_inc(hot_used, 2)
            pe.wait_ge(line_made, 1)
            nc.tensor.matmul(counts_ps[:, 0:NT], nought[:], nought[:, 0:NT], start=True, stop=False)
            with pe.Fori(0, total) as n:
                for q in range(CH // HOT):
                    pe.wait_ge(hot_ready, n * (CH // HOT) + (q + 1))
                    for j in range(HOT):
                        ins = nc.tensor.matmul(counts_ps[:, 0:NT], hot[q % 2][:, j, 0:P], hot[q % 2][:, j, P:P + NT],
                                               start=False, stop=False)
                    ins.then_inc(hot_used, 1)
            nc.tensor.matmul(counts_ps[:, 0:NT], nought[:], nought[:, 0:NT], start=False, stop=True).then_inc(counts_ready, 1)
            pe.wait_ge(counts_out, 1)
            nc.tensor.transpose(counts_t_ps[0:NT, 0:P], counts[:], s["ident"][:]).then_inc(counts_turned, 1)
            pe.wait_ge(tails_ready, 1)
            for n in range(4):
                ins = nc.tensor.transpose(tr_ps[0:NF, n, :], tail[:, n, :], s["ident"][:])
            ins.then_inc(turned, 1)
            pe.wait_ge(carry_ready, 1)
            for n, v in enumerate((run_top[:, 0:P], run_sum[:, 0:P], join[:, 2, :])):
                ins = nc.tensor.transpose(back_ps[:, n, 0:NF], v, s["ident"][0:NF, 0:NF])
            ins.then_inc(carry_turned, 1)


def gate_ranks(nc, step, parts, tiles, E_, score, better, count, first, last):
    for j in range(first, last):
        one = score[:, :, j:j + 1]
        if j:
            ins = nc.vector.tensor_tensor(better[:, :, 0:j], score[:, :, 0:j], one.to_broadcast([parts, tiles, j]), ALU.is_lt)
        if j < E_ - 1:
            ins = nc.vector.tensor_tensor(better[:, :, j + 1:E_], score[:, :, j + 1:E_],
                                          one.to_broadcast([parts, tiles, E_ - 1 - j]), ALU.is_le)
        step(ins)
        if j:
            ins = nc.vector.tensor_tensor(count[:, :, 0:j], count[:, :, 0:j], better[:, :, 0:j], ALU.add)
        if j < E_ - 1:
            ins = nc.vector.tensor_tensor(count[:, :, j + 1:E_], count[:, :, j + 1:E_], better[:, :, j + 1:E_], ALU.add)
        step(ins)


def gate_steps(nc, step, parts, tiles, E_, score, better, count, gate, best):
    step(nc.vector.memset(count[:], 0.0))
    gate_ranks(nc, step, parts, tiles, E_, score, better, count, 0, E_)
    gate_tops(nc, step, parts, tiles, E_, score, gate, best)


def gate_tops(nc, step, parts, tiles, E_, score, gate, best):
    step(nc.vector.tensor_reduce(best[:], score[:], AX.X, ALU.max))
    step(nc.vector.tensor_tensor(gate[:], score[:], best[:].rearrange("p (t o) -> p t o", o=1).to_broadcast([parts, tiles, E_]),
                                 ALU.subtract))


def gate_ends(nc, step, parts, tiles, E_, count, gate, total):
    step(nc.vector.scalar_tensor_tensor(out=gate[:], in0=count[:], scalar=2.0, in1=gate[:], op0=ALU.is_lt, op1=ALU.mult))
    step(nc.vector.tensor_reduce(total[:], gate[:], AX.X, ALU.add))
    step(nc.vector.reciprocal(total[:], total[:]))
    step(nc.vector.tensor_tensor(gate[:], gate[:], total[:].rearrange("p (t o) -> p t o", o=1).to_broadcast([parts, tiles, E_]), ALU.mult))


def turn_gates_pe(nc, pe, s, gate, E_, gate_ps, gates_ready, bank_free, bank_ready):
    pe.sem_inc(bank_free, 2)
    pe.wait_ge(gates_ready, 1)
    for g in range(-(-NT // 4)):
        pe.wait_ge(bank_free, g + 1)
        for q in range(min(4, NT - 4 * g)):
            ins = nc.tensor.transpose(gate_ps[g % 2][0:E_, q * P:(q + 1) * P], gate[:, 4 * g + q, :], s["ident"][:])
        ins.then_inc(bank_ready, 1)


def turn_gates_act(nc, act, s, E_, gate_ps, bank_free, bank_ready):
    by_tile = s["gates"][0:E_, :].rearrange("e (p t) -> e t p", t=NT)
    for g in range(-(-NT // 4)):
        n = min(4, NT - 4 * g)
        act.wait_ge(bank_ready, g + 1)
        nc.scalar.copy(by_tile[:, 4 * g:4 * g + n, :],
                       gate_ps[g % 2][0:E_, 0:n * P].rearrange("e (t p) -> e t p", p=P)).then_inc(bank_free, 1)


def graph_gates(nc, shared, sums_dram, counts_dram, b_gat, ln_gamma, ln_beta):
    with ExitStack() as ctx:
        sb = lambda name, shape, dt=F32: ctx.enter_context(nc.sbuf_tensor(name, shape, dt))
        pb = lambda name, shape: ctx.enter_context(nc.psum_tensor(name, shape, F32))
        sem = lambda name: keep(shared, ctx.enter_context(nc.semaphore(name)))
        s = shared
        Q = H0 * C0
        ends = sb("g_ends", [P, NT], I32)
        got = sb("g_got", [P, NT, STW])
        rows = sb("g_rows", [P, 3, Q])
        table = sb("g_table", [P, NT, TABW])
        last = sb("g_last", [P, TABW])
        times = sb("g_times", [P, NT])
        tall = sb("g_tall", [P, NT])
        extra = sb("g_extra", [P, NT, H0])
        top = sb("g_top", [P, NT, H0])
        scale = sb("g_scale", [P, 2, NT, H0])
        more = sb("g_more", [P, NT, NF])
        agg = sb("g_agg", [P, NT, Q])
        sq = sb("g_sq", [P, NT, Q])
        den = sb("g_den", [P, NT, H0])
        mean = sb("g_mean", [P, NT])
        var = sb("g_var", [P, NT])
        score = sb("g_score", [P, NT, C0])
        better = sb("g_better", [P, NT, C0])
        count = sb("g_count", [P, NT, C0])
        gate = sb("g_gate", [P, NT, C0])
        gate_ps = [pb(f"g_ps{u}", [P, 512]) for u in range(2)]
        ends_in, got_in, rows_in = sem("g_ends_in"), pool_sem(nc, s, "g_got_in"), sem("g_rows_in")
        table_in, scale_ready, scaled = sem("g_table_in"), sem("g_scale_ready"), sem("g_scaled")
        step_done, var_ready, rooted = sem("g_step"), sem("g_var_ready"), sem("g_rooted")
        raised, exp_done, gates_ready = sem("g_raised"), sem("g_exp_done"), sem("g_gates_ready")
        bank_free, bank_ready = sem("g_bank_free"), sem("g_bank_ready")
        block = ctx.enter_context(nc.Block())

        @block.sync
        def _(sp):
            sp.dma_start(ends[:], s["end_id"].rearrange("(p t) o -> p (t o)", p=P)).then_inc(ends_in, 16)
            sp.dma_start(table[:].rearrange("p t f -> p (t f)"), s["table"].rearrange("(p t) f -> p (t f)", p=P)).then_inc(table_in, 16)
            sp.dma_start(last[:], s["table"][N - 1:N, :].to_broadcast([P, TABW])).then_inc(table_in, 16)
            sp.dma_start(times[:], counts_dram.rearrange("(p t) -> p t", p=P)).then_inc(table_in, 16)
            for n, v in enumerate((b_gat, ln_gamma, ln_beta)):
                sp.dma_start(rows[:, n, :], v.to_broadcast([P, Q])).then_inc(rows_in, 16)

        @block.gpsimd
        def _(pool):
            pool.wait_ge(ends_in, 16)
            for t in range(NT):
                pool.indirect_dma_start(got[:, t, :], None, sums_dram,
                                        bass.IndirectOffsetOnAxis(ap=ends[:, t:t + 1], axis=0)).then_inc(got_in, 16)

        @block.vector
        def _(dve):
            steps = [0]

            def step(ins):
                steps[0] += 1
                ins.then_inc(step_done, 1)
                dve.wait_ge(step_done, steps[0])

            per_tile = lambda v: v.rearrange("p (o q) -> p o q", o=1).to_broadcast([P, NT, Q])
            per_node = lambda v: v[:].rearrange("p (t o) -> p t o", o=1).to_broadcast([P, NT, Q])
            dve.wait_ge(table_in, 48)
            wide = lambda v, n: v.rearrange("p (t o) -> p t o", o=1).to_broadcast([P, NT, n])
            nc.vector.tensor_scalar(tall[:], times[:], 0.0, None, ALU.is_gt)
            step(nc.vector.tensor_tensor(top[:], table[:, :, NF + H0:TABW],
                                         last[:, NF:NF + H0].rearrange("p (o k) -> p o k", o=1).to_broadcast([P, NT, H0]), ALU.add))
            nc.vector.scalar_tensor_tensor(out=extra[:], in0=top[:], scalar=0.2, in1=top[:], op0=ALU.mult, op1=ALU.max)
            step(nc.vector.tensor_scalar(tall[:], tall[:], -NEG, NEG, ALU.mult, ALU.add))
            step(nc.vector.tensor_tensor(extra[:], extra[:], wide(tall[:], H0), ALU.add))
            dve.wait_ge(got_in, 16 * NT)
            dve.wait_ge(rows_in, 48)
            step(nc.vector.tensor_tensor(top[:], extra[:], got[:, :, NF:STW], ALU.max))
            nc.vector.tensor_tensor(scale[:, 0], got[:, :, NF:STW], top[:], ALU.subtract)
            step(nc.vector.tensor_tensor(scale[:, 1], extra[:], top[:], ALU.subtract))
            dve.sem_inc(scale_ready, 1)
            dve.wait_ge(scaled, 1)
            step(nc.vector.tensor_tensor(scale[:, 1], scale[:, 1], wide(times[:], H0), ALU.mult))
            for k in range(H0):
                f = slice(k * HC, (k + 1) * HC)
                nc.vector.tensor_tensor(more[:, :, f], last[:, f].rearrange("p (o c) -> p o c", o=1).to_broadcast([P, NT, HC]),
                                        scale[:, 1, :, k:k + 1].to_broadcast([P, NT, HC]), ALU.mult)
                ins = nc.vector.tensor_tensor(got[:, :, f], got[:, :, f], scale[:, 0, :, k:k + 1].to_broadcast([P, NT, HC]), ALU.mult)
            step(ins)
            step(nc.vector.tensor_tensor(got[:, :, 0:NF], got[:, :, 0:NF], more[:], ALU.add))
            heads = got[:, :, 0:NF].rearrange("p t (k c) -> p t k c", c=HC)
            step(nc.vector.tensor_scalar(den[:], heads[:, :, :, C0], 1e-16, None, ALU.add))
            step(nc.vector.reciprocal(den[:], den[:]))
            for k in range(H0):
                ins = nc.vector.tensor_tensor(agg[:, :, k * C0:(k + 1) * C0], heads[:, :, k, 0:C0],
                                              den[:, :, k:k + 1].to_broadcast([P, NT, C0]), ALU.mult)
            step(ins)
            step(nc.vector.tensor_tensor(agg[:], agg[:], per_tile(rows[:, 0, :]), ALU.add))
            step(nc.vector.tensor_reduce(mean[:], agg[:], AX.X, ALU.add))
            step(nc.vector.tensor_scalar(mean[:], mean[:], 1.0 / Q, None, ALU.mult))
            step(nc.vector.tensor_tensor(agg[:], agg[:], per_node(mean), ALU.subtract))
            step(nc.vector.tensor_tensor(sq[:], agg[:], agg[:], ALU.mult))
            step(nc.vector.tensor_reduce(var[:], sq[:], AX.X, ALU.add))
            step(nc.vector.tensor_scalar(var[:], var[:], 1.0 / Q, EPS, ALU.mult, ALU.add))
            dve.sem_inc(var_ready, 1)
            dve.wait_ge(rooted, 1)
            step(nc.vector.reciprocal(var[:], var[:]))
            step(nc.vector.tensor_tensor(agg[:], agg[:], per_node(var), ALU.mult))
            step(nc.vector.tensor_tensor(agg[:], agg[:], per_tile(rows[:, 1, :]), ALU.mult))
            step(nc.vector.tensor_tensor(agg[:], agg[:], per_tile(rows[:, 2, :]), ALU.add))
            step(nc.vector.tensor_reduce(score[:], agg[:].rearrange("p t (k c) -> p t c k", c=C0), AX.X, ALU.add))
            step(nc.vector.tensor_scalar(score[:], score[:], 1.0 / H0, None, ALU.mult))
            gate_steps(nc, step, P, NT, C0, score, better, count, gate, mean)
            dve.sem_inc(raised, 1)
            dve.wait_ge(exp_done, 1)
            gate_ends(nc, step, P, NT, C0, count, gate, var)
            dve.sem_inc(gates_ready, 1)

        @block.scalar
        def _(act):
            act.wait_ge(scale_ready, 1)
            nc.scalar.activation(scale[:], scale[:], ACT.Exp).then_inc(scaled, 1)
            act.wait_ge(var_ready, 1)
            nc.scalar.activation(var[:], var[:], ACT.Sqrt).then_inc(rooted, 1)
            act.wait_ge(raised, 1)
            nc.scalar.activation(gate[:], gate[:], ACT.Exp).then_inc(exp_done, 1)
            turn_gates_act(nc, act, s, C0, gate_ps, bank_free, bank_ready)

        @block.tensor
        def _(pe):
            turn_gates_pe(nc, pe, s, gate, C0, gate_ps, gates_ready, bank_free, bank_ready)


def experts(nc, shared, name, E_, w1_d, b1_d, w2_d, b2_d, gates_dram, out):
    with ExitStack() as ctx:
        sb = lambda what, shape, dt=F32: ctx.enter_context(nc.sbuf_tensor(f"{name}_{what}", shape, dt))
        pb = lambda what, shape: ctx.enter_context(nc.psum_tensor(f"{name}_{what}", shape, F32))
        sem = lambda what: keep(shared, ctx.enter_context(nc.semaphore(f"{name}_{what}")))
        s = shared
        x, y, gates = s["x"], s["y"], s["gates"]
        w1 = sb("w1", [P, E_, HID])
        b1 = sb("b1", [P, E_, 2])
        w2 = sb("w2", [P, E_, 2, D])
        b2 = sb("b2", [E_, D])
        hid = [sb(f"hid{u}", [P, 2, UB]) for u in range(2)]
        up_ps = [pb(f"up{u}", [P, 2, 512]) for u in range(2)]
        spread = [sb(f"spread{u}", [P, E_, UB]) for u in range(2)]
        acc = [pb(f"acc{u}", [P, 512]) for u in range(2)]
        held = sem("held")
        w_in = sem("w_in")
        up_ready, up_free = sem("up_ready"), sem("up_free")
        gates_stored, spread_in, spread_free = sem("gates_stored"), [sem(f"spread_in{u}") for u in range(2)], sem("spread_free")
        hid_ready, hid_scaled, hid_free = sem("hid_ready"), sem("hid_scaled"), sem("hid_free")
        acc_ready, acc_free, stored = sem("acc_ready"), sem("acc_free"), pool_sem(nc, s, f"{name}_stored")
        block = ctx.enter_context(nc.Block())
        at = lambda t, b: t[:, bass.ds(b * UB, UB)]

        @block.sync
        def _(sp):
            sp.dma_start(w1[:].rearrange("p e h -> p (e h)"), w1_d).then_inc(w_in, 16)
            sp.dma_start(b1[:].rearrange("p e h -> p (e h)"), b1_d).then_inc(w_in, 16)
            sp.dma_start(w2[:].rearrange("p e h d -> p (e h d)"), w2_d).then_inc(w_in, 16)
            sp.dma_start(b2[:], b2_d).then_inc(w_in, 16)
            sp.dma_start(gates_dram, gates[0:E_, :]).then_inc(gates_stored, 16)
            sp.wait_ge(gates_stored, 16)
            with sp.Fori(0, NUB // 2) as i:
                for u in range(2):
                    b = 2 * i + u
                    sp.wait_ge(spread_free, b + 1)
                    for e in range(E_):
                        sp.dma_start(spread[u][:, e, :], gates_dram[e:e + 1, bass.ds(b * UB, UB)].to_broadcast([P, UB])
                                     ).then_inc(spread_in[u], 16)

        @block.gpsimd
        def _(pool):
            with pool.Fori(0, NUB) as b:
                hold(pool, acc_free, b + 3, held)
                pool.dma_start(out[:, bass.ds(b * UB, UB)], at(x, b)).then_inc(stored, 16)
            pool.wait_ge(stored, 16 * NUB)

        @block.tensor
        def _(pe):
            pe.wait_ge(w_in, 64)
            pe.sem_inc(up_free, 2)
            pe.sem_inc(acc_free, 2)

            def up(b, e, n):
                pe.wait_ge(up_free, n + 1)
                for h in range(2):
                    ins = nc.tensor.matmul(up_ps[e % 2][:, h, 0:UB], w1[:, e, h * P:(h + 1) * P], at(y, b), start=True, stop=True)
                ins.then_inc(up_ready, 1)

            def down(u, b, e, n):
                pe.wait_ge(hid_scaled, n + 1)
                for h in range(2):
                    ins = nc.tensor.matmul(acc[u][:, 0:UB], w2[:, e, h, :], hid[e % 2][:, h, :],
                                           start=(e == 0 and h == 0), stop=False)
                ins.then_inc(hid_free, 1)

            def pair(i, last):
                for u in range(2):
                    b = 2 * i + u
                    pe.wait_ge(acc_free, b + 1)
                    for e in range(E_):
                        if e < E_ - 1:
                            up(b, e + 1, b * E_ + (e + 1))
                        elif not (last and u == 1):
                            up(b + 1, 0, b * E_ + E_)
                        down(u, b, e, b * E_ + e)
                    nc.tensor.matmul(acc[u][:, 0:UB], b2[:], at(gates[0:E_, :], b), start=False, stop=True).then_inc(acc_ready, 1)

            up(0, 0, 0)
            with pe.Fori(0, NUB // 2 - 1) as i:
                pair(i, False)
            pair(NUB // 2 - 1, True)

        @block.scalar
        def _(act):
            act.wait_ge(w_in, 64)
            act.sem_inc(hid_free, 2)
            with act.Fori(0, NUB // 2) as i:
                for m in range(2 * E_):
                    e = m % E_
                    n = i * (2 * E_) + m
                    act.wait_ge(up_ready, n + 1)
                    act.wait_ge(hid_free, n + 1)
                    for h in range(2):
                        ins = nc.scalar.activation(hid[e % 2][:, h, :], up_ps[e % 2][:, h, 0:UB], ACT.Gelu, bias=b1[:, e, h:h + 1])
                    ins.then_inc(hid_ready, 1)
                    act.wait_ge(hid_ready, n + 1)
                    act.sem_inc(up_free, 1)

        @block.vector
        def _(dve):
            dve.sem_inc(spread_free, 2)
            with dve.Fori(0, NUB // 2) as i:
                for u in range(2):
                    b = 2 * i + u
                    dve.wait_ge(spread_in[u], i * (16 * E_) + 16 * E_)
                    for e in range(E_):
                        n = b * E_ + e
                        dve.wait_ge(hid_ready, n + 1)
                        nc.vector.tensor_tensor(hid[e % 2][:], hid[e % 2][:], spread[u][:, e:e + 1, :].to_broadcast([P, 2, UB]),
                                                ALU.mult).then_inc(hid_scaled, 1)
                    dve.wait_ge(hid_scaled, b * E_ + E_)
                    dve.sem_inc(spread_free, 1)
                    dve.wait_ge(acc_ready, b + 1)
                    nc.vector.tensor_tensor(at(x, b), at(x, b), acc[u][:, 0:UB], ALU.add).then_inc(acc_free, 1)


def second_half(nc, shared, adj_t, w_msg, b_msg, gamma, beta, w_r, b_r, w1_d, b1_d, w2_d, b2_d, x_dram, out):
    with ExitStack() as ctx:
        sb = lambda name, shape, dt=F32: ctx.enter_context(nc.sbuf_tensor(name, shape, dt))
        pb = lambda name, shape: ctx.enter_context(nc.psum_tensor(name, shape, F32))
        sem = lambda name: keep(shared, ctx.enter_context(nc.semaphore(name)))
        s = shared
        y = s["y"]
        w = sb("m_w", [P, D])
        b_wide = sb("m_b", [P, D])
        msg = sb("m_msg", [P, NT, D])
        adj = sb("m_adj", [P, MBUF, MT * UB])
        inv = [y[:, u * MT * UB:(u + 1) * MT * UB] for u in range(NINV)]
        x_in = sb("m_x_in", [P, UB])
        x = sb("m_x", [P, UB])
        x_out = sb("m_x_out", [P, UB])
        z = sb("m_z", [P, UB])
        sq = sb("m_sq", [P, UB])
        gain = sb("m_gain", [P, 2])
        w1 = sb("m_w1", [P, E1, HID])
        b1 = sb("m_b1", [P, E1, 2])
        w2 = sb("m_w2", [P, E1, 2, D])
        b2 = sb("m_b2", [E1, D])
        hid = sb("m_hid", [P, GE, 2, UB])
        w_route = sb("m_w_route", [P, E1])
        b_route = sb("m_b_route", [BT, E1])
        score = sb("m_score", [BT, UT, E1])
        better = sb("m_better", [BT, UT, E1])
        count = sb("m_count", [BT, UT, E1])
        gate = sb("m_gate", [BT, UT, E1])
        best = sb("m_best", [BT, UT])
        total = sb("m_total", [BT, UT])
        gates = sb("m_gates", [E1, UB])
        acc = pb("m_acc", [P, 512])
        out_acc = pb("m_out_acc", [P, 512])
        stats = pb("m_stats", [P, 512])
        route = pb("m_route", [P, 512])
        up_ps = [pb(f"m_up{u}", [P, 512]) for u in range(2)]
        gate_ps = [pb(f"m_gate{u}", [P, 512]) for u in range(2)]
        msg_ps = gate_ps
        up_ps.append(stats)
        w_in, late_in = sem("m_w_in"), sem("m_late_in")
        msg_free, msg_ready = sem("m_msg_free"), sem("m_msg_ready")
        adj_in = [sem(f"m_adj_in{n}") for n in range(MBUF)]
        adj_used, acc_ready = sem("m_adj_used"), sem("m_acc_ready")
        logged, inverted, raised, weighted = sem("m_logged"), sem("m_inverted"), sem("m_raised"), sem("m_weighted")
        squared = sem("m_squared")
        x_made = sem("m_x_made")
        mean_ready, centred, dev_squared = sem("m_mean_ready"), sem("m_centred"), sem("m_dev_squared")
        var_ready, var_logged, rstd_ready = sem("m_var_ready"), sem("m_var_logged"), sem("m_rstd_ready")
        scaled, normed, routed, gate_step = sem("m_scaled"), sem("m_normed"), sem("m_routed"), sem("m_gate_step")
        gate_raised, gate_exp, gates_ready = sem("m_gate_raised"), sem("m_gate_exp"), sem("m_gates_ready")
        turned, lined = sem("m_turned"), sem("m_lined")
        up_ready, activated = sem("m_up_ready"), sem("m_activated")
        hid_free, gate_ready, hid_gated = sem("m_hid_free"), sem("m_gate_ready"), sem("m_hid_gated")
        out_ready, out_made = sem("m_out_ready"), sem("m_out_made")
        x_loaded, out_stored = pool_sem(nc, s, "m_x_loaded"), pool_sem(nc, s, "m_out_stored")
        out_left = sem("m_out_left")
        held = sem("m_held")
        block = ctx.enter_context(nc.Block())
        width = lambda c: min(MT, NT - c * MT) * UB

        @block.sync
        def _(sp):
            sp.dma_start(w[:], w_msg).then_inc(w_in, 16)
            sp.dma_start(b_wide[:], b_msg.to_broadcast([P, D])).then_inc(w_in, 16)

            def load(ub, c):
                n = width(c)
                sp.dma_start(adj[:, c % MBUF, 0:n], adj_t[ub, :, c * MT * UB:c * MT * UB + n] if isinstance(ub, int) else
                             adj_t[bass.ds(ub, 1), :, c * MT * UB:c * MT * UB + n].rearrange("o p n -> (o p) n")
                             ).then_inc(adj_in[c % MBUF], 16)
            for c in range(MCH):
                if c == MBUF:
                    for to, of in ((gain[:, 0:1], gamma), (gain[:, 1:2], beta), (w_route[:], w_r),
                                   (b_route[:], b_r.to_broadcast([BT, E1])), (w1[:].rearrange("p e h -> p (e h)"), w1_d),
                                   (b1[:].rearrange("p e h -> p (e h)"), b1_d),
                                   (w2[:].rearrange("p e h d -> p (e h d)"), w2_d), (b2[:], b2_d)):
                        sp.dma_start(to, of).then_inc(late_in, 16)
                if c >= MBUF:
                    sp.wait_ge(adj_used, c - MBUF + 1)
                load(0, c)
            with sp.Fori(1, NUB) as ub:
                for c in range(MCH):
                    sp.wait_ge(adj_used, MCH * ub + (c - MBUF + 1))
                    load(ub, c)

        @block.gpsimd
        def _(pool):
            pool.dma_start(x_in[:], x_dram[:, 0:UB]).then_inc(x_loaded, 16)
            with pool.Fori(0, NUB - 1) as b:
                hold(pool, x_made, b + 2, held)
                pool.dma_start(x_in[:], x_dram[:, bass.ds((b + 1) * UB, UB)]).then_inc(x_loaded, 16)
                hold(pool, out_made, b + 2, held)
                pool.dma_start(out[:, bass.ds(b * UB, UB)], x_out[:]).then_inc(out_stored, 16)
                hold(pool, out_stored, 16 * b + 16, out_left)
            pool.wait_ge(out_made, NUB + 1)
            pool.dma_start(out[:, (NUB - 1) * UB:N], x_out[:]).then_inc(out_stored, 16)
            pool.wait_ge(out_stored, 16 * NUB)

        @block.tensor
        def _(pe):
            def ups(b, g):
                for j in range(2 * GE):
                    pe.wait_ge(activated, 2 * E1 * b + (2 * GE * g + j + 1))
                    nc.tensor.matmul(up_ps[j % 3][:, 0:UB], w1[:, GE * g + j // 2, j % 2 * P:(j % 2 + 1) * P], z[:],
                                     start=True, stop=True).then_inc(up_ready, 1)

            def spread(b, e):
                pe.wait_ge(hid_gated, E1 * b + (e + 1))
                nc.tensor.matmul(gate_ps[e % 2][:, 0:UB], s["ident"][0:E1, e:e + 1].to_broadcast([E1, P]), gates[:],
                                 start=True, stop=True).then_inc(gate_ready, 1)

            def downs(b, pair, then):
                for e in (2 * pair, 2 * pair + 1):
                    pe.wait_ge(hid_gated, E1 * b + (e + 3))
                    for h in range(2):
                        ins = nc.tensor.matmul(out_acc[:, 0:UB], w2[:, e, h, :], hid[:, e % GE, h, :],
                                               start=(e == 0 and h == 0), stop=False)
                    ins.then_inc(hid_free, 1)
                if then:
                    spread(b, 2 * pair + 2)
                    spread(b, 2 * pair + 3)

            def piece(b, c):
                if c == 0:
                    pe.wait_ge(x_made, b + 2)
                    nc.tensor.matmul(stats[:, 0:UB], s["mean_w"][:], x[:], start=True, stop=True).then_inc(mean_ready, 1)
                elif c == 2:
                    pe.wait_ge(dev_squared, b + 1)
                    nc.tensor.matmul(stats[:, 0:UB], s["mean_w"][:], sq[:], start=True, stop=True).then_inc(var_ready, 1)
                elif c == 4:
                    pe.wait_ge(normed, b + 1)
                    for t in range(UT):
                        ins = nc.tensor.matmul(route[0:BT, t * E1:(t + 1) * E1], z[:, t * BT:(t + 1) * BT], w_route[:],
                                               start=True, stop=True)
                    ins.then_inc(routed, 1)
                elif c == 5:
                    ups(b, 0)
                elif c == 7:
                    pe.wait_ge(gates_ready, b + 1)
                    for t in range(UT):
                        ins = nc.tensor.transpose(route[0:E1, t * BT:(t + 1) * BT], gate[:, t, :], s["ident"][0:BT, 0:BT])
                    ins.then_inc(turned, 1)
                elif c == 8:
                    pe.wait_ge(lined, b + 1)
                    spread(b, 0)
                    spread(b, 1)
                elif c == 9:
                    pe.wait_ge(out_made, b + 1)
                    downs(b, 0, True)
                elif c == 10:
                    downs(b, 1, True)
                elif c == 12:
                    ups(b, 1)
                elif c == 13:
                    downs(b, 2, True)
                elif c == 14:
                    downs(b, 3, False)
                    nc.tensor.matmul(out_acc[:, 0:UB], b2[:], gates[:], start=False, stop=True).then_inc(out_ready, 1)

            def products(ub, b):
                pe.wait_ge(x_made, ub + 1)
                for c in range(MCH):
                    pe.wait_ge(weighted, MCH * ub + (c + 1 + NINV))
                    for k in range(min(MT, NT - c * MT)):
                        ins = nc.tensor.matmul(acc[:, 0:UB], msg[:, c * MT + k, :], adj[:, c % MBUF, k * UB:(k + 1) * UB],
                                               start=(c == 0 and k == 0), stop=(c * MT + k == NT - 1))
                    ins.then_inc(adj_used, 1)
                    if b is not None and c < MCH - 1:
                        piece(b, c)
                pe.wait_ge(adj_used, MCH * ub + MCH)
                pe.sem_inc(acc_ready, 1)

            pe.wait_ge(w_in, 32)
            pe.sem_inc(msg_free, 2)
            pe.sem_inc(x_made, 1)
            for t in range(NT):
                g, q = divmod(t, 4)
                if q == 0:
                    pe.wait_ge(msg_free, g + 1)
                ins = nc.tensor.matmul(msg_ps[g % 2][:, q * D:(q + 1) * D], y[:, t * P:(t + 1) * P], w[:], start=True, stop=True)
                if q == 3 or t == NT - 1:
                    ins.then_inc(msg_ready, 1)
            pe.wait_ge(msg_free, -(-NT // 4) + 2)
            products(0, None)
            pe.wait_ge(late_in, 128)
            with pe.Fori(0, NUB - 1) as b:
                products(b + 1, b)
            for c in range(MCH):
                piece(NUB - 1, c)

        @block.scalar
        def _(act):
            def gelus(b, g):
                nc.scalar.preload_act_table_set("gelu_and_others")
                for j in range(2 * GE):
                    e = GE * g + j // 2
                    if j % 2 == 0:
                        act.wait_ge(hid_free, E1 * b + (e + 1))
                    act.wait_ge(up_ready, 2 * E1 * b + (2 * GE * g + j + 1))
                    nc.scalar.activation(hid[:, e % GE, j % 2, :], up_ps[j % 3][:, 0:UB], ACT.Gelu,
                                         bias=b1[:, e, j % 2:j % 2 + 1]).then_inc(activated, 1)
                nc.scalar.preload_act_table_set("natural_log_exp_and_others")

            def piece(b, c):
                if c == 2:
                    act.wait_ge(centred, b + 1)
                    nc.scalar.activation(sq[:], z[:], ACT.Square).then_inc(dev_squared, 1)
                elif c == 4:
                    act.wait_ge(var_ready, b + 1)
                    nc.scalar.activation(sq[:], stats[:, 0:UB], ACT.Ln, bias=s["eps"][:, 0:1]).then_inc(var_logged, 1)
                    act.wait_ge(var_logged, b + 1)
                    nc.scalar.activation(sq[:], sq[:], ACT.Exp, scale=-0.5).then_inc(rstd_ready, 1)
                elif c == 6:
                    gelus(b, 0)
                elif c == 7:
                    act.wait_ge(gate_raised, b + 1)
                    nc.scalar.activation(gate[:], gate[:], ACT.Exp).then_inc(gate_exp, 1)
                elif c == 13:
                    gelus(b, 1)

            def log(ub, c):
                n, v = width(c), inv[c % NINV]
                act.wait_ge(adj_in[c % MBUF], (16 * MCH // MBUF) * ub + 16 * (c // MBUF + 1))
                act.wait_ge(weighted, MCH * ub + (c + 1))
                nc.scalar.activation(v[:, 0:n], adj[:, c % MBUF, 0:n], ACT.Ln, bias=s["tiny"][:, 0:1]).then_inc(logged, 1)

            def invert(ub, c):
                n, v = width(c), inv[c % NINV]
                act.wait_ge(logged, MCH * ub + (c + 1))
                nc.scalar.activation(v[:, 0:n], v[:, 0:n], ACT.Exp, scale=-1.0).then_inc(inverted, 1)

            def raise_(ub, c):
                n, v = width(c), inv[c % NINV]
                act.wait_ge(squared, MCH * ub + (c + 1))
                nc.scalar.activation(v[:, 0:n], v[:, 0:n], ACT.Exp, bias=s["minus2"][:, 0:1], scale=-2.0).then_inc(raised, 1)

            def chunks(ub, b, last):
                for c in range(MCH):
                    then = (ub, c + AHEAD) if c < MCH - AHEAD else None if last else (ub + 1, c + AHEAD - MCH)
                    if then:
                        log(*then)
                    raise_(ub, c)
                    if then:
                        invert(*then)
                    if b is not None:
                        piece(b, c)

            act.wait_ge(msg_free, -(-NT // 4) + 2)
            act.sem_inc(activated, 3)
            act.sem_inc(hid_free, GE)
            nc.scalar.preload_act_table_set("natural_log_exp_and_others")
            for c in range(AHEAD):
                log(0, c)
                invert(0, c)
            chunks(0, None, False)
            act.wait_ge(late_in, 128)
            with act.Fori(0, NUB - 2) as b:
                nc.scalar.preload_act_table_set("natural_log_exp_and_others")
                chunks(b + 1, b, False)
            chunks(NUB - 1, NUB - 2, True)
            for c in range(MCH):
                piece(NUB - 1, c)

        @block.vector
        def _(dve):
            def gated(b, pair):
                for e in (2 * pair, 2 * pair + 1):
                    dve.wait_ge(activated, 2 * E1 * b + (2 * e + 5))
                    dve.wait_ge(gate_ready, E1 * b + (e + 1))
                    nc.vector.tensor_tensor(hid[:, e % GE], hid[:, e % GE],
                                            gate_ps[e % 2][:, 0:UB].rearrange("p (o n) -> p o n", o=1).to_broadcast([P, 2, UB]),
                                            ALU.mult).then_inc(hid_gated, 1)

            def piece(b, c):
                taken = [sum(GATE_PIECE_STEPS[0:max(0, min(c - 5, 2))])]

                def step(ins):
                    taken[0] += 1
                    ins.then_inc(gate_step, 1)
                    dve.wait_ge(gate_step, sum(GATE_PIECE_STEPS) * b + taken[0])

                if c == 1:
                    dve.wait_ge(mean_ready, b + 1)
                    nc.vector.tensor_tensor(z[:], x[:], stats[:, 0:UB], ALU.subtract).then_inc(centred, 1)
                elif c == 4:
                    dve.wait_ge(rstd_ready, b + 1)
                    nc.vector.scalar_tensor_tensor(out=z[:], in0=z[:], scalar=gain[:, 0:1], in1=sq[:],
                                                   op0=ALU.mult, op1=ALU.mult).then_inc(scaled, 1)
                    dve.wait_ge(scaled, b + 1)
                    nc.vector.tensor_scalar(z[:], z[:], gain[:, 1:2], None, ALU.add).then_inc(normed, 1)
                elif c == 5:
                    dve.wait_ge(routed, b + 1)
                    step(nc.vector.tensor_tensor(score[:], route[0:BT, 0:UT * E1].rearrange("p (t e) -> p t e", e=E1),
                                                 b_route[:].rearrange("p (o e) -> p o e", o=1).to_broadcast([BT, UT, E1]), ALU.add))
                    step(nc.vector.memset(count[:], 0.0))
                    gate_tops(nc, step, BT, UT, E1, score, gate, best)
                    dve.sem_inc(gate_raised, 1)
                    gate_ranks(nc, step, BT, UT, E1, score, better, count, 0, 4)
                elif c == 6:
                    gate_ranks(nc, step, BT, UT, E1, score, better, count, 4, E1)
                elif c == 7:
                    dve.wait_ge(gate_exp, b + 1)
                    gate_ends(nc, step, BT, UT, E1, count, gate, total)
                    dve.sem_inc(gates_ready, 1)
                elif c == 8:
                    dve.wait_ge(turned, b + 1)
                    nc.vector.tensor_copy(gates[:], route[0:E1, 0:UB]).then_inc(lined, 1)
                elif c == 9:
                    gated(b, 0)
                elif c == 10:
                    gated(b, 1)
                elif c == 13:
                    gated(b, 2)
                elif c == 14:
                    gated(b, 3)
                elif c == 15:
                    dve.wait_ge(out_ready, b + 1)
                    dve.wait_ge(out_left, b + 1)
                    nc.vector.tensor_tensor(x_out[:], x[:], out_acc[:, 0:UB], ALU.add).then_inc(out_made, 1)

            def square(ub, c):
                n, v = width(c), inv[c % NINV]
                dve.wait_ge(inverted, MCH * ub + (c + 1))
                nc.vector.scalar_tensor_tensor(out=v[:, 0:n], in0=v[:, 0:n], scalar=-2.0, in1=v[:, 0:n],
                                               op0=ALU.add, op1=ALU.mult).then_inc(squared, 1)

            def weigh(ub, c):
                n, v = width(c), inv[c % NINV]
                dve.wait_ge(raised, MCH * ub + (c + 1))
                r = adj[:, c % MBUF, 0:n]
                nc.vector.scalar_tensor_tensor(out=r, in0=r, scalar=1.0, in1=v[:, 0:n], op0=ALU.is_lt, op1=ALU.mult).then_inc(weighted, 1)

            def chunks(ub, b, last):
                for c in range(MCH):
                    if c < MCH - 1:
                        square(ub, c + 1)
                    elif not last:
                        square(ub + 1, 0)
                    weigh(ub, c)
                    if b is not None:
                        piece(b, c)
                dve.wait_ge(acc_ready, ub + 1)
                dve.wait_ge(x_loaded, 16 * ub + 16)
                if b is not None:
                    dve.wait_ge(out_made, b + 2)
                nc.vector.tensor_tensor(x[:], x_in[:], acc[:, 0:UB], ALU.add).then_inc(x_made, 1)

            dve.wait_ge(w_in, 32)
            for g in range(-(-NT // 4)):
                n = min(4, NT - 4 * g)
                dve.wait_ge(msg_ready, g + 1)
                nc.vector.tensor_tensor(msg[:, 4 * g:4 * g + n, :], msg_ps[g % 2][:, 0:n * D].rearrange("p (t d) -> p t d", d=D),
                                        b_wide[:].rearrange("p (o d) -> p o d", o=1).to_broadcast([P, n, D]),
                                        ALU.add).then_inc(msg_free, 1)
            dve.sem_inc(weighted, NINV)
            dve.sem_inc(out_made, 1)
            dve.sem_inc(out_left, 1)
            dve.sem_inc(hid_gated, 2)
            square(0, 0)
            chunks(0, None, False)
            dve.wait_ge(late_in, 128)
            with dve.Fori(0, NUB - 2) as b:
                chunks(b + 1, b, False)
            chunks(NUB - 1, NUB - 2, True)
            for c in range(MCH):
                piece(NUB - 1, c)


def layer_kernel(nc, a, out):
    with ExitStack() as ctx:
        dram = lambda name, shape, dt=F32: nc.dram_tensor(name, shape, dt).ap()
        y0_dram = dram("d_y0", [P, N])
        r_dram = dram("d_r", [P, N])
        keys_dram = dram("d_keys", [3 * E], I32)
        counts_dram = dram("d_counts", [NPAD])
        rows_dram = dram("d_rows", [P, RMAX + CH], I32)
        sums_dram = dram("d_sums", [P * RMAX, STW])
        sb = lambda name, shape, dt=F32: ctx.enter_context(nc.sbuf_tensor(name, shape, dt))
        shared = {
            "used_sems": [], "stack": ctx,
            "mean_w": sb("mean_w", [P, P]), "ones": sb("ones", [P, P]), "ident": sb("ident", [P, P]),
            "sign": sb("sign", [P, LOGP]), "eps": sb("eps", [P, 1]),
            "tiny": sb("tiny", [P, 1]), "minus2": sb("minus2", [P, 1]),
            "chunks": sb("chunks", [P, 1], I32), "row_first": sb("row_first", [P, 1], I32),
            "apart_first": sb("apart_first", [P, 1], I32), "apart_each": sb("apart_each", [P, 1], I32),
            "apart_all": sb("apart_all", [P, 1], I32),
            "end_id": dram("d_end_id", [NPAD, 1], I32),
        }
        with ExitStack() as early:
            shared["keys"] = early.enter_context(nc.sbuf_tensor("keys", [P, 4, ROW], I32))
            shared["h"] = early.enter_context(nc.sbuf_tensor("h_items", [P, NT, D], F32))
            prepare(nc, shared, a["x_t"], a["item_t"], a["edges"], a["w_item_t"], a["b_item"], y0_dram)
            first_pass(nc, shared, a["adj_t"], a["w_user_t"], a["b_user"], y0_dram, r_dram, keys_dram, rows_dram, sums_dram)
        shared["x_in"] = a["x_t"]
        shared["y"] = sb("y", [P, NPAD])
        x_dram = dram("d_x", [P, N])
        with_x = ExitStack()
        shared["x"] = with_x.enter_context(nc.sbuf_tensor("x", [P, N], F32))
        shared["table"] = dram("d_table", [NPAD, TABW])
        layernorm(nc, shared, "ln1", add=r_dram)
        node_table(nc, shared, a["w_gat"], a["att_src"], a["att_dst"])
        attend(nc, shared, keys_dram, rows_dram, sums_dram, counts_dram)
        clear_semaphores(nc, shared)
        with ExitStack() as late:
            shared["gates"] = late.enter_context(nc.sbuf_tensor("gates0", [8, NPAD], F32))
            graph_gates(nc, shared, sums_dram, counts_dram, a["b_gat"], a["ln_gamma"], a["ln_beta"])
            experts(nc, shared, "e0", 4, a["w1_0"], a["b1_0"], a["w2_0"], a["b2_0"], dram("d_gates", [C0, NPAD]), x_dram)
        layernorm(nc, shared, "ln2")
        with_x.close()
        second_half(nc, shared, a["adj_t"], a["w_msg"], a["b_msg"], a["gamma"], a["beta"], a["w_r"], a["b_r"],
                    a["w1_1"], a["b1_1"], a["w2_1"], a["b2_1"], x_dram, out)


def lay_out(x, adj, L0_gnn_item_feat, L0_gnn_W_item, L0_gnn_b_item, L0_gnn_W_user, L0_gnn_b_user,
            L0_ffn_W_gat, L0_ffn_att_src, L0_ffn_att_dst, L0_ffn_b_gat, L0_ffn_ln_gamma, L0_ffn_ln_beta,
            L0_ffn_W1, L0_ffn_b1, L0_ffn_W2, L0_ffn_b2, L0_ffn_edge_index, L1_gnn_W, L1_gnn_B,
            L1_ffn_gamma, L1_ffn_beta, L1_ffn_Wr, L1_ffn_br, L1_ffn_W1, L1_ffn_b1, L1_ffn_W2, L1_ffn_b2):
    import numpy as np
    c = np.ascontiguousarray
    padded = np.zeros((NUB, UB, NT * P), adj.dtype)
    padded[:, :, :N] = np.asarray(adj).reshape(NUB, UB, N)
    adj_t = c(padded.reshape(NUB, UB, NT, P).transpose(0, 3, 2, 1)).reshape(NUB, P, NT * UB)
    item_t = np.zeros((D, NPAD), np.asarray(x).dtype)
    item_t[:, :N] = np.asarray(L0_gnn_item_feat).T
    col = lambda v: c(np.asarray(v).reshape(-1, 1))
    row = lambda v: c(np.asarray(v).reshape(1, -1))
    w1 = lambda w: c(np.asarray(w).transpose(1, 0, 2)).reshape(D, -1)
    w2 = lambda w: c(np.asarray(w).reshape(w.shape[0], 2, P, D).transpose(2, 0, 1, 3)).reshape(P, -1)
    b1 = lambda b: c(np.asarray(b).reshape(-1, P).T)
    return {
        "x_t": c(np.asarray(x).T), "adj_t": adj_t, "item_t": item_t,
        "w_item_t": c(np.asarray(L0_gnn_W_item).T), "b_item": row(L0_gnn_b_item),
        "w_user_t": c(np.asarray(L0_gnn_W_user).T), "b_user": col(L0_gnn_b_user),
        "edges": c(np.asarray(L0_ffn_edge_index)),
        "w_gat": c(np.asarray(L0_ffn_W_gat)), "att_src": row(L0_ffn_att_src), "att_dst": row(L0_ffn_att_dst),
        "b_gat": row(L0_ffn_b_gat), "ln_gamma": row(L0_ffn_ln_gamma), "ln_beta": row(L0_ffn_ln_beta),
        "w1_0": w1(L0_ffn_W1), "b1_0": b1(L0_ffn_b1), "w2_0": w2(L0_ffn_W2), "b2_0": c(np.asarray(L0_ffn_b2)),
        "w_msg": c(np.asarray(L1_gnn_W)), "b_msg": row(L1_gnn_B),
        "gamma": col(L1_ffn_gamma), "beta": col(L1_ffn_beta), "w_r": c(np.asarray(L1_ffn_Wr)), "b_r": row(L1_ffn_br),
        "w1_1": w1(L1_ffn_W1), "b1_1": b1(L1_ffn_b1), "w2_1": w2(L1_ffn_W2), "b2_1": c(np.asarray(L1_ffn_b2)),
    }


def kernel(**inputs):
    import numpy as np
    import concourse.bacc as bacc
    from concourse.bass_utils import run_bass_kernel_spmd

    arrays = lay_out(**inputs)
    nc = bacc.Bacc("TRN2", target_bir_lowering=False, num_devices=1)
    aps = {k: nc.dram_tensor(k, v.shape, mybir.dt.from_np(v.dtype), kind="ExternalInput").ap() for k, v in arrays.items()}
    out = nc.dram_tensor("out_t", (D, N), F32, kind="ExternalOutput").ap()
    layer_kernel(nc, aps, out)
    result = run_bass_kernel_spmd(nc, [arrays], core_ids=[0])
    return np.ascontiguousarray(result.results[0]["out_t"].T)
```
